# Optimizing a Trainium2 kernel written in Bass

```python
import numpy as np
import jax
import jax.numpy as jnp

def _softmax(x, axis=-1):
    return jax.nn.softmax(x, axis=axis)

def _gelu(x):
    return jax.nn.gelu(x, approximate=True)

def _silu(x):
    return jax.nn.silu(x)

def _sigmoid(x):
    return jax.nn.sigmoid(x)

def _layernorm(x, axis=-1, eps=1e-05):
    m = jnp.mean(x, axis=axis, keepdims=True)
    v = jnp.var(x, axis=axis, keepdims=True)
    return (x - m) / jnp.sqrt(v + eps)

def _scatter_add(tgt, idx, src, axis=0):
    return tgt.at[idx].add(src)

def _segment_sum(src, seg, n):
    return jax.ops.segment_sum(src, seg, n)
kernel_name = 'mk_gnn_preln_d4_gnn_r64_a3c9f1'

def setup_inputs(seed: int=0):
    np.random.seed(seed)
    _w = jnp.asarray

    def _rec_inputs():
        import jax
        import jax.numpy as jnp
        _gk = jax.random.key(seed)
        x = -0.0009044 + 1 * jax.random.normal(jax.random.fold_in(_gk, 1), (100000, 16), jnp.float32)
        src = jax.random.randint(jax.random.fold_in(_gk, 2), (50000,), 0, 100000, jnp.int32)
        dst = jnp.minimum((100000 * jax.random.uniform(jax.random.fold_in(_gk, 3), (50000,)) ** 2.0).astype(jnp.int32), 99999)
        _o = jnp.argsort(dst, stable=True)
        src = src[_o]
        dst = dst[_o]
        edge_attr_2 = 0.000411684 + 0.577418 * jax.random.normal(jax.random.fold_in(_gk, 12), (50000, 2), jnp.float32)
        edge_type_8 = jax.random.randint(jax.random.fold_in(_gk, 14), (50000,), 0, 8, jnp.int32)
        edge_weight = -0.000107899 + 1.00008 * jax.random.normal(jax.random.fold_in(_gk, 15), (50000,), jnp.float32)
        return (x, src, dst, edge_attr_2, edge_type_8, edge_weight)
    x, src, dst, edge_attr_2, edge_type_8, edge_weight = _rec_inputs()

    def _L0_gnn_setup():
        import jax, jax.numpy as jnp
        import numpy as np
        N_NODES = 100000
        N_EDGES = 25000
        F_IN = 16
        F_OUT = 16
        N_BASIS = 4

        def linear_basis(u, n):
            centers = jnp.linspace(-1.0, 1.0, n, dtype=u.dtype)
            dx = 2.0 / (n - 1)
            return jnp.maximum(0.0, 1.0 - jnp.abs(u[:, None] - centers[None, :]) / dx)
        key = jax.random.key(seed)
        k1, k2, k3, k4, k5 = jax.random.split(key, 5)
        x = jax.random.normal(k1, (N_NODES, F_IN), dtype=jnp.float32)
        edge_index = jax.random.randint(k2, (2, N_EDGES), 0, N_NODES, dtype=jnp.int64)
        edge_attr = jax.random.uniform(k3, (N_EDGES, 2), dtype=jnp.float32, minval=-1.0, maxval=1.0)
        weight = jax.random.uniform(k4, (N_BASIS, N_BASIS, F_IN, F_OUT), dtype=jnp.float32, minval=-0.05, maxval=0.05)
        return {'x': x, 'edge_index': edge_index, 'edge_attr': edge_attr, 'weight': weight}
    _L0_gnn_all = _L0_gnn_setup()
    _L0_gnn_in = {k: v for k, v in _L0_gnn_all.items() if k in ('weight',)}
    del _L0_gnn_all

    def _L1_gnn_setup():
        import jax, jax.numpy as jnp
        import numpy as np
        N_NODES = 50000
        N_EDGES = 12500
        F_IN = 16
        F_OUT = 16
        HID = 256

        def _glorot(key, shape):
            fan_in, fan_out = (shape[0], shape[1])
            lim = np.sqrt(6.0 / (fan_in + fan_out)).astype(np.float32)
            return jax.random.uniform(key, shape, jnp.float32, -lim, lim)
        key = jax.random.key(seed)
        ks = jax.random.split(key, 12)
        x = jax.random.normal(ks[0], (N_NODES, F_IN), jnp.float32)
        edge_index = jax.random.randint(ks[1], (2, N_EDGES), 0, N_NODES, jnp.int64 if jax.config.jax_enable_x64 else jnp.int32)
        return {'x': x, 'edge_index': edge_index, 'pre_w1': _glorot(ks[2], (F_IN, HID)), 'pre_b1': jnp.zeros((HID,), jnp.float32), 'pre_w2': _glorot(ks[3], (HID, HID)), 'pre_b2': jnp.zeros((HID,), jnp.float32), 'conv_w': _glorot(ks[4], (HID, HID)), 'conv_b': jnp.zeros((HID,), jnp.float32), 'post_w1': _glorot(ks[5], (2 * HID, HID)), 'post_b1': jnp.zeros((HID,), jnp.float32), 'post_w2': _glorot(ks[6], (HID, F_OUT)), 'post_b2': jnp.zeros((F_OUT,), jnp.float32)}
    _L1_gnn_all = _L1_gnn_setup()
    _L1_gnn_in = {k: v for k, v in _L1_gnn_all.items() if k in ('pre_w1', 'pre_b1', 'pre_w2', 'pre_b2', 'conv_w', 'conv_b', 'post_w1', 'post_b1', 'post_w2', 'post_b2')}
    del _L1_gnn_all

    def _L2_gnn_setup():
        import jax, jax.numpy as jnp
        import numpy as np
        N_NODES = 100000
        N_EDGES = 50000
        NUM_REL = 8

        def _rgcn_layer(x, src, dst, edge_type, W, root, bias):
            out = x @ root + bias
            x_src = x[src]
            for r in range(W.shape[0]):
                mask = (edge_type == r).astype(x.dtype)
                s = jax.ops.segment_sum(x_src * mask[:, None], dst, num_segments=x.shape[0])
                cnt = jax.ops.segment_sum(mask, dst, num_segments=x.shape[0])
                agg = s / jnp.clip(cnt, 1.0)[:, None]
                out = out + agg @ W[r]
            return out
        key = jax.random.key(seed)
        ks = jax.random.split(key, 9)
        x = jax.random.normal(ks[0], (N_NODES, 16), dtype=jnp.float32)
        edge_index = jax.random.randint(ks[1], (2, N_EDGES), 0, N_NODES, dtype=jnp.int32)
        edge_type = jax.random.randint(ks[2], (N_EDGES,), 0, NUM_REL, dtype=jnp.int32)
        s1 = 1.0 / np.sqrt(16.0)
        s2 = 1.0 / np.sqrt(32.0)
        W1 = jax.random.normal(ks[3], (NUM_REL, 16, 32), dtype=jnp.float32) * s1
        root1 = jax.random.normal(ks[4], (16, 32), dtype=jnp.float32) * s1
        b1 = jnp.zeros((32,), dtype=jnp.float32)
        W2 = jax.random.normal(ks[5], (NUM_REL, 32, 16), dtype=jnp.float32) * s2
        root2 = jax.random.normal(ks[6], (32, 16), dtype=jnp.float32) * s2
        b2 = jnp.zeros((16,), dtype=jnp.float32)
        return {'x': x, 'edge_index': edge_index, 'edge_type': edge_type, 'W1': W1, 'root1': root1, 'b1': b1, 'W2': W2, 'root2': root2, 'b2': b2}
    _L2_gnn_all = _L2_gnn_setup()
    _L2_gnn_in = {k: v for k, v in _L2_gnn_all.items() if k in ('W1', 'root1', 'b1', 'W2', 'root2', 'b2')}
    del _L2_gnn_all

    def _L3_gnn_setup():
        import jax, jax.numpy as jnp
        import numpy as np
        N_NODES = 100000
        N_EDGES = 50000
        BATCH = 16
        LAYER_NUMBER = 4
        key = jax.random.key(seed)
        k1, k2, k3, k4 = jax.random.split(key, 4)
        x = jax.random.normal(k1, (N_NODES, BATCH), dtype=jnp.float32)
        weights = jax.random.normal(k2, (N_EDGES,), dtype=jnp.float32)
        row = jax.random.randint(k3, (N_EDGES,), 0, N_NODES, dtype=jnp.int64)
        col = jax.random.randint(k4, (N_EDGES,), 0, N_NODES, dtype=jnp.int64)
        return {'x': x, 'weights': weights, 'row': row, 'col': col}
    _L3_gnn_all = _L3_gnn_setup()
    _L3_gnn_in = {k: v for k, v in _L3_gnn_all.items() if k in ()}
    del _L3_gnn_all
    return {'x': x, 'src': src, 'dst': dst, 'edge_attr_2': edge_attr_2, 'edge_type_8': edge_type_8, 'edge_weight': edge_weight, 'L0_gnn_weight': _L0_gnn_in['weight'], 'L1_gnn_pre_w1': _L1_gnn_in['pre_w1'], 'L1_gnn_pre_b1': _L1_gnn_in['pre_b1'], 'L1_gnn_pre_w2': _L1_gnn_in['pre_w2'], 'L1_gnn_pre_b2': _L1_gnn_in['pre_b2'], 'L1_gnn_conv_w': _L1_gnn_in['conv_w'], 'L1_gnn_conv_b': _L1_gnn_in['conv_b'], 'L1_gnn_post_w1': _L1_gnn_in['post_w1'], 'L1_gnn_post_b1': _L1_gnn_in['post_b1'], 'L1_gnn_post_w2': _L1_gnn_in['post_w2'], 'L1_gnn_post_b2': _L1_gnn_in['post_b2'], 'L2_gnn_W1': _L2_gnn_in['W1'], 'L2_gnn_root1': _L2_gnn_in['root1'], 'L2_gnn_b1': _L2_gnn_in['b1'], 'L2_gnn_W2': _L2_gnn_in['W2'], 'L2_gnn_root2': _L2_gnn_in['root2'], 'L2_gnn_b2': _L2_gnn_in['b2']}

def reference(x, src, dst, edge_attr_2, edge_type_8, edge_weight, L0_gnn_weight, L1_gnn_pre_w1, L1_gnn_pre_b1, L1_gnn_pre_w2, L1_gnn_pre_b2, L1_gnn_conv_w, L1_gnn_conv_b, L1_gnn_post_w1, L1_gnn_post_b1, L1_gnn_post_w2, L1_gnn_post_b2, L2_gnn_W1, L2_gnn_root1, L2_gnn_b1, L2_gnn_W2, L2_gnn_root2, L2_gnn_b2):
    import jax
    import jax.numpy as jnp

    def _L0_gnn_ref(x, edge_index, edge_attr, weight):
        import jax, jax.numpy as jnp
        import numpy as np
        N_NODES = 100000
        N_EDGES = 25000
        F_IN = 16
        F_OUT = 16
        N_BASIS = 4

        def linear_basis(u, n):
            centers = jnp.linspace(-1.0, 1.0, n, dtype=u.dtype)
            dx = 2.0 / (n - 1)
            return jnp.maximum(0.0, 1.0 - jnp.abs(u[:, None] - centers[None, :]) / dx)
        "BasisConvLayer forward, mode='conv', linear basis, no bias/activations.\n\n            For each edge e=(i<-j): msg_e = sum_{u,v} b_u(dx) b_v(dy) * (x_j @ W[u,v]);\n            out[i] = sum over incoming edges of msg_e.\n            "
        row, col = (edge_index[0], edge_index[1])
        x_j = x[col]
        bx = linear_basis(edge_attr[:, 0], N_BASIS)
        by = linear_basis(edge_attr[:, 1], N_BASIS)
        t = (bx[:, :, None] * by[:, None, :]).reshape(-1, N_BASIS * N_BASIS)
        w_flat = weight.reshape(N_BASIS * N_BASIS, F_IN, F_OUT)
        msg = jnp.zeros((x_j.shape[0], F_OUT), dtype=x.dtype)
        for k in range(N_BASIS * N_BASIS):
            msg = msg + t[:, k, None] * (x_j @ w_flat[k])
        out = jax.ops.segment_sum(msg, row, num_segments=N_NODES)
        return out

    def _L1_gnn_ref(x, edge_index, pre_w1, pre_b1, pre_w2, pre_b2, conv_w, conv_b, post_w1, post_b1, post_w2, post_b2):
        import jax, jax.numpy as jnp
        import numpy as np
        N_NODES = 50000
        N_EDGES = 12500
        F_IN = 16
        F_OUT = 16
        HID = 256

        def _glorot(key, shape):
            fan_in, fan_out = (shape[0], shape[1])
            lim = np.sqrt(6.0 / (fan_in + fan_out)).astype(np.float32)
            return jax.random.uniform(key, shape, jnp.float32, -lim, lim)
        h = jax.nn.relu(x @ pre_w1 + pre_b1) @ pre_w2 + pre_b2
        src, dst = (edge_index[0], edge_index[1])
        msg = jax.nn.relu(h[src] @ conv_w + conv_b)
        agg = jax.ops.segment_sum(msg, dst, num_segments=h.shape[0])
        h = jnp.concatenate([h, agg], axis=-1)
        out = jax.nn.relu(h @ post_w1 + post_b1) @ post_w2 + post_b2
        return jnp.tanh(out)

    def _L2_gnn_ref(x, edge_index, edge_type, W1, root1, b1, W2, root2, b2):
        import jax, jax.numpy as jnp
        import numpy as np
        N_NODES = 100000
        N_EDGES = 50000
        NUM_REL = 8

        def _rgcn_layer(x, src, dst, edge_type, W, root, bias):
            out = x @ root + bias
            x_src = x[src]
            for r in range(W.shape[0]):
                mask = (edge_type == r).astype(x.dtype)
                s = jax.ops.segment_sum(x_src * mask[:, None], dst, num_segments=x.shape[0])
                cnt = jax.ops.segment_sum(mask, dst, num_segments=x.shape[0])
                agg = s / jnp.clip(cnt, 1.0)[:, None]
                out = out + agg @ W[r]
            return out
        src, dst = (edge_index[0], edge_index[1])
        h = _rgcn_layer(x, src, dst, edge_type, W1, root1, b1)
        h = jax.nn.relu(h)
        h = _rgcn_layer(h, src, dst, edge_type, W2, root2, b2)
        return h

    def _L3_gnn_ref(x, weights, row, col):
        import jax, jax.numpy as jnp
        import numpy as np
        N_NODES = 100000
        N_EDGES = 50000
        BATCH = 16
        LAYER_NUMBER = 4

        def step(y, _):
            msg = weights[:, None] * y[col]
            y_new = jax.ops.segment_sum(msg, row, num_segments=N_NODES)
            return (y_new, None)
        y, _ = jax.lax.scan(step, x, None, length=LAYER_NUMBER)
        return y
    edge_index = jnp.stack([src, dst])
    h = jnp.maximum(_layernorm(x, axis=-1), 0.0)
    x = x + _L0_gnn_ref(h, edge_index, edge_attr_2, L0_gnn_weight)
    h = jnp.maximum(_layernorm(x, axis=-1), 0.0)
    x = x + _L1_gnn_ref(h, edge_index, L1_gnn_pre_w1, L1_gnn_pre_b1, L1_gnn_pre_w2, L1_gnn_pre_b2, L1_gnn_conv_w, L1_gnn_conv_b, L1_gnn_post_w1, L1_gnn_post_b1, L1_gnn_post_w2, L1_gnn_post_b2)
    h = jnp.maximum(_layernorm(x, axis=-1), 0.0)
    x = x + _L2_gnn_ref(h, edge_index, edge_type_8, L2_gnn_W1, L2_gnn_root1, L2_gnn_b1, L2_gnn_W2, L2_gnn_root2, L2_gnn_b2)
    h = jnp.maximum(_layernorm(x, axis=-1), 0.0)
    x = x + _L3_gnn_ref(h, edge_weight, src, dst)
    return x

_drawn_inputs = setup_inputs


def setup_inputs(seed=0):
    import zlib

    import numpy as np

    out = dict(_drawn_inputs(seed))
    spreads = {'L1_gnn_pre_b1': (0.0, 0.1),
     'L1_gnn_pre_b2': (0.0, 0.1),
     'L1_gnn_conv_b': (0.0, 0.1),
     'L1_gnn_post_b1': (0.0, 0.1),
     'L1_gnn_post_b2': (0.0, 0.1),
     'L2_gnn_b1': (0.0, 0.1),
     'L2_gnn_b2': (0.0, 0.1)}
    factors = {}
    for name, (base, spread) in spreads.items():
        noise = np.random.default_rng([zlib.crc32(name.encode()), seed]).standard_normal(out[name].shape)
        drawn = base * np.exp(spread * noise) if base else spread * noise
        out[name] = jnp.asarray(drawn.astype(out[name].dtype))
    for name, factor in factors.items():
        out[name] = (out[name] * factor).astype(out[name].dtype)
    return out
```

```python
from contextlib import ExitStack

import concourse.bass as bass
from concourse import mybir

P = 128
NODES, EDGES, F, F2, HID, RELS, BASIS, STEPS = 100000, 50000, 16, 32, 256, 8, 4, 4
NODE_PARTS = 125
NODE_COLS = NODES // NODE_PARTS
COLS = 392
SLOTS = COLS * P
GROUP, RING = 8, 7
BODY = GROUP * RING
TURNS = COLS // BODY
FULL_PARTS = EDGES // COLS
REST = EDGES - FULL_PARTS * COLS
REC = 8
LO_BITS = 9
LO, HI = 1 << LO_BITS, 256
PAD_KEY = 196 << LO_BITS
SKIP = 1000000
CHUNK = 28
CG, CS = 4, 7
NCHUNK = 32
NG, NS = 4, 8
EPS = 1e-5

fp32, fp16, i32 = mybir.dt.float32, mybir.dt.float16, mybir.dt.int32
ALU = mybir.AluOpType
ACT = mybir.ActivationFunctionType
AX = mybir.AxisListType.X


class Chain:

    def __init__(self, eng, sem, turn=None, per_turn=0, before=0):
        self.eng, self.sem, self.n = eng, sem, before
        self.turn, self.per_turn = turn, per_turn

    def do(self, ins):
        ins.then_inc(self.sem, 1)
        self.n += 1
        return self

    def sync(self):
        base = 0 if self.turn is None else self.turn * self.per_turn
        self.eng.wait_ge(self.sem, base + self.n)


class Phase:

    spent = []
    MOST = 32

    def __init__(self, nc, name):
        self.nc, self.name, self.ctx, self.own = nc, name, ExitStack(), []
        if nc.free_len() - len(Phase.spent) < Phase.MOST:
            recycle(nc)

    def __enter__(self):
        return self

    def __exit__(self, *a):
        Phase.spent += self.own
        return self.ctx.__exit__(*a)

    def sb(self, name, shape, dt=fp32):
        return self.ctx.enter_context(self.nc.sbuf_tensor(f"{self.name}_{name}", shape, dt))

    def ps(self, name, shape, dt=fp32):
        return self.ctx.enter_context(self.nc.psum_tensor(f"{self.name}_{name}", shape, dt))

    def sem(self, name):
        sem = self.ctx.enter_context(self.nc.semaphore(f"{self.name}_{name}"))
        self.own.append(sem.num)
        return sem

    def block(self):
        return self.ctx.enter_context(self.nc.Block())


def recycle(nc):
    nums = sorted(Phase.spent)
    Phase.spent.clear()
    with nc.Block() as block:
        @block.sync
        def _(sp):
            first = 0
            for n in range(1, len(nums) + 1):
                if n == len(nums) or nums[n] != nums[n - 1] + 1:
                    sp.sem_clear(range(nums[first], nums[n - 1] + 1))
                    first = n


class PoolRing:

    def __init__(self, ctx, nc, name="all"):
        self.sems = [ctx.enter_context(nc.semaphore(f"pool_dma_{name}{g}")) for g in range(RING)]
        self.before = [0] * RING

    def done(self, eng, slot, count):
        eng.wait_ge(self.sems[slot], self.before[slot] + count)

    def end_phase(self, slots, count):
        for g in slots:
            self.before[g] += count


def node_rows(dram):
    return dram.rearrange("(p j) f -> p (j f)", p=NODE_PARTS)


def node_dma(eng, out, in_, sem):
    eng.dma_start(out[0:112], in_[0:112]).then_inc(sem, 16)
    eng.dma_start(out[112:NODE_PARTS], in_[112:NODE_PARTS]).then_inc(sem, 16)


def turns(eng, body, count=TURNS):
    body(0, True)
    with eng.Fori(1, count) as t:
        body(t, False)


def setup_phase(nc, d, s):
    with Phase(nc, "su") as ph:
        zero = ph.sb("zero", [P, 3400])
        keys = {n: ph.sb(n, [P, COLS], i32) for n in ("src", "dst", "typ")}
        wts = ph.sb("wts", [P, COLS])
        attr = ph.sb("attr", [P, COLS, 2])
        iota_i = ph.sb("iota_i", [P, LO], i32)
        row_i = ph.sb("row_i", [P, 1], i32)
        tri = ph.sb("tri", [P, P])
        filled, loaded, masked = ph.sem("filled"), ph.sem("loaded"), ph.sem("masked")
        zeroed, own, vown = ph.sem("zeroed"), ph.sem("own"), ph.sem("vown")
        block = ph.block()

        @block.gpsimd
        def _(pool):
            nc.gpsimd.memset(s["ident"][:], 0.0).then_inc(own, 1)
            nc.gpsimd.memset(tri[:], 1.0).then_inc(own, 1)
            nc.gpsimd.iota(iota_i[:], pattern=[[1, LO]], base=0, channel_multiplier=0).then_inc(masked, 1)
            nc.gpsimd.iota(row_i[:], pattern=[[0, 1]], base=0, channel_multiplier=1).then_inc(masked, 1)
            pool.wait_ge(own, 2)
            nc.gpsimd.affine_select(out=s["ident"][:], in_=s["ident"][:], compare_op=ALU.not_equal, fill=1.0,
                                    base=0, pattern=[[-1, P]], channel_multiplier=1).then_inc(masked, 1)
            nc.gpsimd.affine_select(out=tri[:], in_=tri[:], compare_op=ALU.is_gt, fill=0.0,
                                    base=0, pattern=[[1, P]], channel_multiplier=-1).then_inc(masked, 1)

        @block.vector
        def _(dve):
            nc.vector.memset(zero[:], 0.0).then_inc(filled, 1)
            nc.vector.memset(keys["src"][:], PAD_KEY).then_inc(filled, 1)
            nc.vector.memset(keys["dst"][:], PAD_KEY).then_inc(filled, 1)
            nc.vector.memset(keys["typ"][:], 0).then_inc(filled, 1)
            nc.vector.memset(wts[:], 0.0).then_inc(filled, 1)
            nc.vector.memset(attr[:], 0.0).then_inc(filled, 1)
            c = Chain(dve, vown)
            c.do(nc.vector.memset(s["rec_a"][:], 0.0))
            c.do(nc.vector.memset(s["rec_b"][:], 0.0))
            c.do(nc.vector.memset(s["ones16"][:], 1.0))
            c.do(nc.vector.memset(s["ones"][:], 1.0))
            dve.wait_ge(masked, 4)
            nc.vector.tensor_copy(s["row"][:], row_i[:])
            nc.vector.tensor_copy(s["iota"][:], iota_i[:, 0:32])
            nc.vector.tensor_copy(s["iota16"][:], iota_i[:])
            nc.vector.tensor_copy(s["earlier16"][:], tri[:])
            dve.wait_ge(loaded, 16 * 12)
            c.sync()
            for rec, key, other in (("rec_a", "src", "dst"), ("rec_b", "dst", "src")):
                nc.vector.tensor_copy(s[rec][:, :, 0], keys[key][:])
                nc.vector.tensor_scalar(s[rec][:, :, 1], keys[other][:], float(NODES - 1), None, ALU.min)
            nc.vector.tensor_copy(s["rec_a"][:, :, 2], wts[:])
            nc.vector.tensor_copy(s["rec_a"][:, :, 3:5], attr[:])
            nc.vector.tensor_copy(s["rec_b"][:, :, 2], keys["typ"][:])

        @block.sync
        def _(sp):
            sp.wait_ge(filled, 6)
            full = FULL_PARTS * COLS
            for tile, dram in ((keys["src"], d["src"]), (keys["dst"], d["dst"]), (keys["typ"], d["edge_type_8"]),
                               (wts, d["edge_weight"])):
                sp.dma_start(tile[0:FULL_PARTS, :], dram[0:full].rearrange("(p j) -> p j", j=COLS)).then_inc(loaded, 16)
                sp.dma_start(tile[FULL_PARTS:FULL_PARTS + 1, 0:REST],
                             dram[full:EDGES].rearrange("(p j) -> p j", p=1)).then_inc(loaded, 16)
            ea = d["edge_attr_2"]
            sp.dma_start(attr[0:FULL_PARTS, :, :], ea[0:full, :].rearrange("(p j) w -> p j w", j=COLS)).then_inc(loaded, 16)
            sp.dma_start(attr[FULL_PARTS:FULL_PARTS + 1, 0:REST, :],
                         ea[full:EDGES, :].rearrange("(p j) w -> p j w", p=1)).then_inc(loaded, 16)
            x_rows = node_rows(d["x"])
            node_dma(sp, s["x"][0:NODE_PARTS, :], x_rows, loaded)
            sp.wait_ge(loaded, 16 * 12)

        @block.scalar
        def _(act):
            act.wait_ge(filled, 1)
            n = 0
            for table in s["zero_tables"]:
                rows = node_rows(table)
                piece = 3200 if rows.shape[1] % 3200 == 0 else 3400
                for a in range(0, rows.shape[1], piece):
                    node_dma(act, rows[:, a:a + piece], zero[0:NODE_PARTS, 0:piece], zeroed)
                    n += 32
            for row in s["zero_rows"]:
                act.dma_start(row, zero[0:1, 0:row.shape[1]]).then_inc(zeroed, 16)
                n += 16
            act.wait_ge(zeroed, n)


def descent_phase(nc, s, flag, sorted_dst):
    with Phase(nc, "desc") as ph:
        after = ph.sb("after", [P, REC])
        falls = ph.sb("falls", [P, COLS])
        any_fall = ph.sb("any_fall", [P, 1])
        any16 = ph.sb("any16", [P, 1], fp16)
        total_ps = ph.ps("total_ps", [P, 8])
        padded, loaded, stored, own, found, counted = (ph.sem(n) for n in ("padded", "loaded", "stored", "own", "found", "counted"))
        block = ph.block()
        key = s["rec_b"][:, :, 0]

        @block.sync
        def _(sp):
            rows = sorted_dst.rearrange("(p j) w -> p j w", j=COLS)
            sp.dma_start(rows, s["rec_b"][:]).then_inc(stored, 16)
            sp.wait_ge(stored, 16)
            sp.wait_ge(padded, 1)
            sp.dma_start(after[0:P - 1, :], rows[1:P, 0, :]).then_inc(loaded, 16)

        @block.vector
        def _(dve):
            nc.vector.memset(after[:], PAD_KEY).then_inc(padded, 1)
            dve.wait_ge(loaded, 16)
            c = Chain(dve, own)
            c.do(nc.vector.tensor_tensor(falls[:, 0:COLS - 1], key[:, 0:COLS - 1], key[:, 1:COLS], ALU.is_gt))
            c.do(nc.vector.tensor_tensor(falls[:, COLS - 1:COLS], key[:, COLS - 1:COLS], after[:, 0:1], ALU.is_gt))
            c.sync()
            c.do(nc.vector.tensor_reduce(any_fall[:], falls[:], AX, ALU.max))
            c.sync()
            nc.vector.tensor_copy(any16[:], any_fall[:]).then_inc(found, 1)
            dve.wait_ge(counted, 1)
            c.do(nc.vector.tensor_copy(flag[:], total_ps[0:1, 0:1]))
            c.sync()

        @block.tensor
        def _(pe):
            pe.wait_ge(found, 1)
            nc.tensor.matmul(total_ps[:, 0:1], s["ones16"][:], any16[:], start=True, stop=True).then_inc(counted, 1)


def histogram_phase(nc, s, name, rec, scratch):
    with Phase(nc, name) as ph:
        ki = ph.sb("ki", [P, COLS], i32)
        digit = {"lo": ph.sb("lo", [P, COLS], i32), "hi": ph.sb("hi", [P, COLS], i32)}
        part = {n: ph.sb(n, [P, COLS], i32) for n in ("lo_a", "lo_b", "hi_a", "hi_b")}
        width = {"lo_a": 16, "lo_b": 32, "hi_a": 16, "hi_b": 16}
        hot = {n: ph.sb(n + "_hot", [P, BODY, w], fp16) for n, w in width.items()}
        zero16 = ph.sb("zero16", [P, 32], fp16)
        count_ps = {n: ph.ps(n + "_count", [16, 512]) for n in ("lo", "hi")}
        count = {"lo": ph.sb("count_lo", [16, 32]), "hi": ph.sb("count_hi", [16, 16])}
        flat = {"lo": ph.sb("flat_lo", [P, LO]), "hi": ph.sb("flat_hi", [P, HI])}
        start = ph.sb("start", [P, LO])
        start_i = ph.sb("start_i", [P, LO], i32)
        each_i = ph.sb("each_i", [P, LO], i32)
        over_i = ph.sb("over_i", [P, LO], i32)
        hot_built, hot_used, counted, flattened = ph.sem("hot_built"), ph.sem("hot_used"), ph.sem("counted"), ph.sem("flattened")
        own, taken, peown = ph.sem("own"), ph.sem("taken"), ph.sem("peown")
        split = {"lo": 32, "hi": 16}
        block = ph.block()

        @block.vector
        def _(dve):
            c = Chain(dve, own)
            c.do(nc.vector.tensor_copy(ki[:], rec[:, :, 0]))
            c.do(nc.vector.memset(zero16[:], 0.0))
            c.sync()
            c.do(nc.vector.tensor_scalar(digit["lo"][:], ki[:], LO - 1, None, ALU.bitwise_and))
            c.do(nc.vector.tensor_scalar(digit["hi"][:], ki[:], LO_BITS, None, ALU.logical_shift_right))
            c.sync()
            nc.vector.tensor_copy(s["digit_lo"][:], digit["lo"][:])
            nc.vector.tensor_copy(s["digit_hi"][:], digit["hi"][:])
            c.do(nc.vector.tensor_scalar(part["lo_a"][:], digit["lo"][:], 5, None, ALU.logical_shift_right))
            c.do(nc.vector.tensor_scalar(part["lo_b"][:], digit["lo"][:], 31, None, ALU.bitwise_and))
            c.do(nc.vector.tensor_scalar(part["hi_a"][:], digit["hi"][:], 4, None, ALU.logical_shift_right))
            c.do(nc.vector.tensor_scalar(part["hi_b"][:], digit["hi"][:], 15, None, ALU.bitwise_and))
            c.sync()

            def build(t, first):
                if not first:
                    dve.wait_ge(hot_used, t)
                for n, w in width.items():
                    nc.vector.tensor_tensor(
                        hot[n][:, :, :], s["iota"][:, 0:w].unsqueeze(1).to_broadcast([P, BODY, w]),
                        part[n][:, bass.ds(t * BODY, BODY)].unsqueeze(2).to_broadcast([P, BODY, w]),
                        ALU.is_equal).then_inc(hot_built, 1)

            turns(dve, build)
            dve.wait_ge(counted, 1)
            nc.vector.tensor_copy(count["lo"][:], count_ps["lo"][:, 0:32]).then_inc(taken, 1)
            nc.vector.tensor_copy(count["hi"][:], count_ps["hi"][:, 0:16]).then_inc(taken, 1)
            dve.wait_ge(flattened, 32)
            for n, base in (("lo", s["base_lo"]), ("hi", s["base_hi"])):
                w = flat[n].shape[1]
                c.do(nc.vector.tensor_tensor_scan(start[:, 0:w], s["ones"][:, 0:w], flat[n][:], 0.0, ALU.mult, ALU.add))
                c.sync()
                c.do(nc.vector.tensor_tensor(start_i[:, 0:w], start[:, 0:w], flat[n][:], ALU.subtract))
                c.sync()
                c.do(nc.vector.tensor_scalar(each_i[:, 0:w], start_i[:, 0:w], 7, None, ALU.logical_shift_right))
                c.do(nc.vector.tensor_scalar(over_i[:, 0:w], start_i[:, 0:w], P - 1, None, ALU.bitwise_and))
                c.sync()
                c.do(nc.vector.scalar_tensor_tensor(out=base[:], in0=over_i[:, 0:w], scalar=s["row"][:, 0:1],
                                                    in1=each_i[:, 0:w], op0=ALU.is_gt, op1=ALU.add))
                c.sync()

        @block.tensor
        def _(pe):
            pe.wait_ge(own, 2)
            for n in ("lo", "hi"):
                nc.tensor.matmul(count_ps[n][:, 0:split[n]], zero16[:, 0:16], zero16[:, 0:split[n]],
                                 start=True, stop=False)

            def add(t, first):
                pe.wait_ge(hot_built, 4 * t + 4)
                for k in range(BODY):
                    nc.tensor.matmul(count_ps["lo"][:, 0:32], hot["lo_a"][:, k, :], hot["lo_b"][:, k, :],
                                     start=False, stop=False)
                    last = nc.tensor.matmul(count_ps["hi"][:, 0:16], hot["hi_a"][:, k, :], hot["hi_b"][:, k, :],
                                            start=False, stop=False)
                last.then_inc(hot_used, 1)

            turns(pe, add)
            for n in ("lo", "hi"):
                last = nc.tensor.matmul(count_ps[n][:, 0:split[n]], zero16[:, 0:16], zero16[:, 0:split[n]],
                                        start=False, stop=True)
            last.then_inc(counted, 1)

        @block.sync
        def _(sp):
            sp.wait_ge(taken, 2)
            sp.dma_start(scratch["lo"].rearrange("(a b) -> a b", a=16), count["lo"][:]).then_inc(peown, 16)
            sp.dma_start(scratch["hi"].rearrange("(a b) -> a b", a=16), count["hi"][:]).then_inc(peown, 16)
            sp.wait_ge(peown, 32)
            sp.dma_start(flat["lo"][:], scratch["lo"].partition_broadcast(P)).then_inc(flattened, 16)
            sp.dma_start(flat["hi"][:], scratch["hi"].partition_broadcast(P)).then_inc(flattened, 16)
            sp.wait_ge(flattened, 32)


def sort_pass(nc, s, name, rec, digit, base, buckets, out, first):
    NO = 4
    with Phase(nc, name) as ph:
        hot = ph.sb("hot", [P, NO, buckets], fp16)
        seen = ph.sb("seen", [P, NO, buckets], fp16)
        junk = ph.sb("junk", [P, 2, buckets])
        rank = ph.sb("rank", [P, RING, GROUP])
        rank_i = ph.sb("rank_i", [P, GROUP], i32)
        row_i = ph.sb("row_i", [P, GROUP], i32)
        col_i = ph.sb("col_i", [P, GROUP], i32)
        place = ph.sb("place", [P, RING, GROUP], i32)
        data = ph.sb("data", [P, RING, GROUP * REC])
        sums = ph.ps("sums", [P, NO, 512])
        hot_built, seen_added = ph.sem("hot_built"), ph.sem("seen_added")
        summed, rank_read = ph.sem("summed"), ph.sem("rank_read")
        placed, staged, turn_sem, own = ph.sem("placed"), ph.sem("staged"), ph.sem("turn"), ph.sem("own")
        ring = s["ring"]
        LAG = 2
        OWN = RING * (4 if first else 1)
        block = ph.block()

        @block.vector
        def _(dve):
            nc.vector.tensor_copy(seen[:, 0, :], base[:]).then_inc(seen_added, 1)
            dve.wait_ge(seen_added, 1)

            def rank_columns(t, first_turn):
                c = Chain(dve, own, t, OWN)
                for k in range(BODY + LAG):
                    if k < BODY:
                        b = k % NO
                        if k >= NO or not first_turn:
                            dve.wait_ge(summed, t * BODY + k - NO + 1)
                        nc.vector.tensor_scalar(hot[:, b, :], s["iota16"][:, 0:buckets],
                                                digit[:, bass.ds(t * BODY + k, 1)], None,
                                                ALU.is_equal).then_inc(hot_built, 1)
                        dve.wait_ge(hot_built, t * BODY + k + 1)
                        nc.vector.tensor_tensor(seen[:, (b + 1) % NO, :], seen[:, b, :], hot[:, b, :],
                                                ALU.add).then_inc(seen_added, 1)
                        dve.wait_ge(seen_added, t * BODY + k + 2)
                    if k >= LAG:
                        j = k - LAG
                        g, m = j // GROUP, j % GROUP
                        dve.wait_ge(summed, t * BODY + j + 1)
                        if j >= 2 or not first_turn:
                            dve.wait_ge(rank_read, t * BODY + j - 1)
                        nc.vector.tensor_tensor_reduce(
                            out=junk[:, j % 2, :], in0=hot[:, j % NO, :], in1=sums[:, j % NO, 0:buckets], scale=1.0, scalar=0.0,
                            op0=ALU.mult, op1=ALU.add, accum_out=rank[:, g, m:m + 1]).then_inc(rank_read, 1)
                        if m == GROUP - 1:
                            if not first_turn:
                                ring.done(dve, g, 16 * GROUP * t)
                            dve.wait_ge(rank_read, t * BODY + j + 1)
                            if first:
                                c.do(nc.vector.tensor_copy(rank_i[:], rank[:, g, :]))
                                c.sync()
                                c.do(nc.vector.tensor_scalar(row_i[:], rank_i[:], P - 1, None, ALU.bitwise_and))
                                c.do(nc.vector.tensor_scalar(col_i[:], rank_i[:], 7, None, ALU.logical_shift_right))
                                c.sync()
                                c.do(nc.vector.scalar_tensor_tensor(out=place[:, g, :], in0=row_i[:], scalar=float(COLS),
                                                                    in1=col_i[:], op0=ALU.mult, op1=ALU.add))
                            else:
                                c.do(nc.vector.tensor_copy(place[:, g, :], rank[:, g, :]))
                            c.sync()
                            dve.sem_inc(placed, 1)

            turns(dve, rank_columns)

        @block.tensor
        def _(pe):
            def sum_columns(t, first_turn):
                for k in range(BODY):
                    b = k % NO
                    if k >= NO or not first_turn:
                        pe.wait_ge(rank_read, t * BODY + k - NO + 1)
                    pe.wait_ge(seen_added, t * BODY + k + 1)
                    pe.wait_ge(hot_built, t * BODY + k + 1)
                    dst = sums[:, b, 0:buckets]
                    nc.tensor.matmul(dst, s["ones16"][:], seen[:, b, :], start=True, stop=False)
                    nc.tensor.matmul(dst, s["earlier16"][:], hot[:, b, :], start=False, stop=True).then_inc(summed, 1)

            turns(pe, sum_columns)

        @block.scalar
        def _(act):
            def stage(t, first_turn):
                for g in range(RING):
                    if not first_turn:
                        ring.done(act, g, 16 * GROUP * t)
                    nc.scalar.copy(data[:, g, :].rearrange("p (k w) -> p k w", w=REC),
                                   rec[:, bass.ds(t * BODY + g * GROUP, GROUP), :]).then_inc(staged, 1)

            turns(act, stage)

        @block.gpsimd
        def _(pool):
            def move(t, first_turn):
                for g in range(RING):
                    pool.wait_ge(placed, RING * t + g + 1)
                    pool.sem_inc(turn_sem, 1)
                    pool.wait_ge(staged, RING * t + g + 1)
                    pool.sem_inc(turn_sem, 1)
                    for k in range(GROUP):
                        pool.indirect_dma_start(
                            out=out, out_offset=bass.IndirectOffsetOnAxis(ap=place[:, g, k:k + 1], axis=0),
                            in_=data[:, g, k * REC:(k + 1) * REC], in_offset=None).then_inc(ring.sems[g], 16)

            turns(pool, move)
            for g in range(RING):
                ring.done(pool, g, 16 * GROUP * TURNS)
    s["ring"].end_phase(range(RING), 16 * GROUP * TURNS)


def reload_phase(nc, s, name, rec, table):
    with Phase(nc, name) as ph:
        loaded, own = ph.sem("loaded"), ph.sem("own")
        ki = ph.sb("ki", [P, COLS], i32)
        block = ph.block()

        @block.sync
        def _(sp):
            sp.dma_start(rec[:], table.rearrange("(p j) w -> p j w", j=COLS)).then_inc(loaded, 16)

        @block.vector
        def _(dve):
            dve.wait_ge(loaded, 16)
            c = Chain(dve, own)
            c.do(nc.vector.tensor_copy(ki[:], rec[:, :, 0]))
            c.sync()
            c.do(nc.vector.tensor_scalar(ki[:], ki[:], LO_BITS, None, ALU.logical_shift_right))
            c.sync()
            c.do(nc.vector.tensor_copy(s["digit_hi"][:], ki[:]))
            c.sync()


def enter_phase(nc):
    with Phase(nc, "enter") as ph:
        entered = ph.sem("entered")
        block = ph.block()

        @block.sync
        def _(sp):
            sp.sem_inc(entered, 1)

        @block.gpsimd
        def _(pool):
            pool.wait_ge(entered, 1)

        @block.scalar
        def _(act):
            act.wait_ge(entered, 1)

        @block.vector
        def _(dve):
            dve.wait_ge(entered, 1)

        @block.tensor
        def _(pe):
            pe.wait_ge(entered, 1)


def sort_records(nc, s, n, rec, scratch, halfway, out):
    histogram_phase(nc, s, "hist_" + n, rec, scratch)
    sort_pass(nc, s, "low_" + n, rec, s["digit_lo"], s["base_lo"], LO, halfway, True)
    reload_phase(nc, s, "reload_" + n, rec, halfway)
    sort_pass(nc, s, "high_" + n, rec, s["digit_hi"], s["base_hi"], HI, out, False)


def order_phase(nc, s, name, table, o, payload):
    with Phase(nc, name) as ph:
        rec = ph.sb("rec", [P, COLS, REC])
        before, after = ph.sb("before", [P, REC]), ph.sb("after", [P, REC])
        key = o["key"]
        open_ = ph.sb("open", [P, COLS])
        flag = ph.sb("flag", [P, 2, F2])
        flag_ps = ph.ps("flag_ps", [F2, 2, P])
        cleared, loaded, own, flags, turned = (ph.sem(n) for n in ("cleared", "loaded", "own", "flags", "turned"))
        block = ph.block()
        rows = table.rearrange("(p j) w -> p j w", j=COLS)

        @block.sync
        def _(sp):
            sp.dma_start(rec[:], rows).then_inc(loaded, 16)
            sp.wait_ge(cleared, 2)
            sp.dma_start(before[1:P, :], rows[0:P - 1, COLS - 1, :]).then_inc(loaded, 16)
            sp.dma_start(after[0:P - 1, :], rows[1:P, 0, :]).then_inc(loaded, 16)

        @block.vector
        def _(dve):
            nc.vector.memset(before[:], -1.0).then_inc(cleared, 1)
            nc.vector.memset(after[:], -1.0).then_inc(cleared, 1)
            dve.wait_ge(loaded, 48)
            c = Chain(dve, own)
            c.do(nc.vector.memset(o["gather"][:, COLS:], 0))
            c.do(nc.vector.tensor_copy(key[:], rec[:, :, 0]))
            c.do(nc.vector.memset(o["same"][:, 0:1], 0.0))
            c.do(nc.vector.tensor_copy(o["other"][:], rec[:, :, 1]))
            for dst, field in payload:
                c.do(nc.vector.tensor_copy(dst, rec[:, :, field] if isinstance(field, int) else rec[:, :, field[0]:field[1]]))
            c.sync()
            c.do(nc.vector.tensor_copy(o["gather"][:, 0:COLS], o["other"][:]))
            c.do(nc.vector.tensor_tensor(o["same"][:, 1:COLS], key[:, 1:COLS], key[:, 0:COLS - 1], ALU.is_equal))
            c.do(nc.vector.tensor_tensor(open_[:, 0:COLS - 1], key[:, 0:COLS - 1], key[:, 1:COLS], ALU.is_equal))
            c.do(nc.vector.tensor_tensor(open_[:, COLS - 1:COLS], key[:, COLS - 1:COLS], after[:, 0:1], ALU.is_equal))
            c.do(nc.vector.tensor_scalar(o["first"][:], key[:], key[:, 0:1], None, ALU.is_equal))
            c.do(nc.vector.tensor_tensor(o["goes_on"][:], key[:, 0:1], before[:, 0:1], ALU.is_equal))
            c.sync()
            c.do(nc.vector.scalar_tensor_tensor(out=o["write"][:], in0=open_[:], scalar=float(SKIP), in1=key[:],
                                                op0=ALU.mult, op1=ALU.add))
            c.do(nc.vector.tensor_copy(flag[:, 0, :], o["goes_on"][:].to_broadcast([P, F2])))
            c.do(nc.vector.tensor_copy(flag[:, 1, :], o["first"][:, COLS - 1:COLS].to_broadcast([P, F2])))
            c.sync()
            dve.sem_inc(flags, 1)
            dve.wait_ge(turned, 1)
            c.do(nc.vector.tensor_copy(o["cross"][:], flag_ps[:, 0, :]))
            c.do(nc.vector.tensor_copy(o["span"][:], flag_ps[:, 1, :]))
            c.sync()

        @block.tensor
        def _(pe):
            pe.wait_ge(flags, 1)
            nc.tensor.transpose(flag_ps[:, 0, :], flag[:, 0, :], s["ident"][:])
            nc.tensor.transpose(flag_ps[:, 1, :], flag[:, 1, :], s["ident"][:]).then_inc(turned, 1)


def scan_turn(nc, dve, own, o, msgs, width, t, first):
    if not first:
        dve.wait_ge(own, t)
    cols = bass.ds(t * BODY, BODY)
    for f in range(width):
        before = 0.0 if first else msgs[:, bass.ds(t * BODY - 1, 1), f]
        last = nc.vector.tensor_tensor_scan(msgs[:, cols, f], o["same"][:, cols], msgs[:, cols, f], before,
                                            ALU.mult, ALU.add)
    last.then_inc(own, 1)


def message_phase(nc, s, name, table, fin, o, wpad, weights, fout, msgs):
    per = P // fin
    nt = GROUP // per
    terms = weights.shape[2]
    nw = terms * fout
    cpb = 512 // nw
    nb = GROUP // cpb
    with Phase(nc, name) as ph:
        idx = ph.sb("idx", [P, RING, GROUP], i32)
        rows = ph.sb("rows", [P, RING, GROUP * fin])
        rows_t = ph.sb("rows_t", [P, nt, P])
        prod = ph.sb("prod", [P, 2, 512])
        rows_ps = ph.ps("rows_ps", [P, 512])
        out_ps = ph.ps("out_ps", [P, nb, 512])
        staged, turned, copied = ph.sem("staged"), ph.sem("turned"), ph.sem("copied")
        bank_full, scaled, summed, tick = ph.sem("bank_full"), ph.sem("scaled"), ph.sem("summed"), ph.sem("tick")
        scanned, gather = ph.sem("scanned"), o["gather"]
        ring = s["ring"]
        block = ph.block()

        @block.gpsimd
        def _(pool):
            def fetch(t, first):
                for g in range(RING):
                    pool.wait_ge(staged, RING * t + g + 1)
                    pool.sem_inc(tick, 1)
                    if not first:
                        pool.wait_ge(turned, RING * (t - 1) + g + 1)
                        pool.sem_inc(tick, 1)
                    for k in range(GROUP):
                        pool.indirect_dma_start(
                            out=rows[:, g, k * fin:(k + 1) * fin], out_offset=None, in_=table,
                            in_offset=bass.IndirectOffsetOnAxis(ap=idx[:, g, k:k + 1], axis=0)).then_inc(ring.sems[g], 16)

            turns(pool, fetch)

        @block.scalar
        def _(act):
            for g in range(RING):
                nc.scalar.copy(idx[:, g, :], gather[:, g * GROUP:(g + 1) * GROUP]).then_inc(staged, 1)

            def stage(t, first):
                for g in range(RING):
                    ring.done(act, g, 16 * GROUP * (t + 1))
                    nc.scalar.copy(idx[:, g, :], gather[:, bass.ds((t + 1) * BODY + g * GROUP, GROUP)]).then_inc(staged, 1)
                    act.wait_ge(turned, RING * t + g + 1)
                    if g > 0 or not first:
                        act.wait_ge(bank_full, nb * (RING * t + g))
                    nc.scalar.copy(rows_t[:], rows_ps[:, 0:nt * P].rearrange("p (n e) -> p n e", e=P)).then_inc(copied, 1)

            turns(act, stage)

        @block.tensor
        def _(pe):
            def multiply(t, first):
                for g in range(RING):
                    ring.done(pe, g, 16 * GROUP * (t + 1))
                    if g > 0 or not first:
                        pe.wait_ge(copied, RING * t + g)
                    for n in range(nt):
                        last = nc.tensor.transpose(rows_ps[:, n * P:(n + 1) * P], rows[:, g, n * P:(n + 1) * P], s["ident"][:])
                    last.then_inc(turned, 1)
                    pe.wait_ge(copied, RING * t + g + 1)
                    for b in range(nb):
                        if g > 0 or not first:
                            pe.wait_ge(scaled, nb * (RING * t + g - 1) + b + 1)
                        for m in range(cpb):
                            k = b * cpb + m
                            last = nc.tensor.matmul(out_ps[:, b, m * nw:(m + 1) * nw], rows_t[:, k // per, :],
                                                    wpad[:, k % per, :], start=True, stop=True)
                        last.then_inc(bank_full, 1)

            turns(pe, multiply)

        @block.vector
        def _(dve):
            def combine(t, first):
                for g in range(RING):
                    for b in range(nb):
                        n = nb * (RING * t + g) + b
                        col = t * BODY + g * GROUP + b * cpb
                        dve.wait_ge(bank_full, n + 1)
                        if g * nb + b >= 2 or not first:
                            dve.wait_ge(summed, n - 1)
                        p = prod[:, (g * nb + b) % 2, :].rearrange("p (c r o) -> p c r o", r=terms, o=fout)
                        nc.vector.tensor_tensor(
                            p, out_ps[:, b, :].rearrange("p (c r o) -> p c r o", r=terms, o=fout),
                            weights[:, bass.ds(col, cpb), :].unsqueeze(3).to_broadcast([P, cpb, terms, fout]),
                            ALU.mult).then_inc(scaled, 1)
                        dve.wait_ge(scaled, n + 1)
                        nc.vector.tensor_reduce(msgs[:, bass.ds(col, cpb), 0:fout], p.rearrange("p c r o -> p c o r"),
                                                AX, ALU.add).then_inc(summed, 1)
                dve.wait_ge(summed, nb * RING * (t + 1))
                scan_turn(nc, dve, scanned, o, msgs, fout, t, first)

            turns(dve, combine)
    s["ring"].end_phase(range(RING), 16 * GROUP * TURNS)


def carry_phase(nc, s, name, o, msgs, width):
    with Phase(nc, name) as ph:
        into = ph.sb("into", [F2, P])
        mult = ph.sb("mult", [F2, P])
        carry_t = ph.sb("carry_t", [F2, P])
        carry = ph.sb("carry", [P, F2])
        last_ps, carry_ps = ph.ps("last_ps", [F2, 512]), ph.ps("carry_ps", [P, 512])
        own, scanned, turned, chained, back = (ph.sem(n) for n in ("own", "scanned", "turned", "chained", "back"))
        block = ph.block()
        w = width

        @block.vector
        def _(dve):
            c = Chain(dve, own)
            c.do(nc.vector.memset(into[:, 0:1], 0.0))
            c.do(nc.vector.memset(mult[:, 0:1], 0.0))
            c.do(nc.vector.tensor_tensor(mult[:, 1:P], o["cross"][:, 1:P], o["span"][:, 0:P - 1], ALU.mult))
            c.sync()
            dve.sem_inc(scanned, 1)
            dve.wait_ge(turned, 1)
            c.do(nc.vector.tensor_tensor(into[0:w, 1:P], o["cross"][0:w, 1:P], last_ps[0:w, 0:P - 1], ALU.mult))
            c.sync()
            c.do(nc.vector.tensor_tensor_scan(carry_t[0:w, :], mult[0:w, :], into[0:w, :], 0.0, ALU.mult, ALU.add))
            c.sync()
            dve.sem_inc(chained, 1)
            dve.wait_ge(back, 1)
            c.do(nc.vector.tensor_copy(carry[:, 0:w], carry_ps[:, 0:w]))
            c.sync()
            for f in range(w):
                c.do(nc.vector.scalar_tensor_tensor(out=msgs[:, :, f], in0=o["first"][:], scalar=carry[:, f:f + 1],
                                                    in1=msgs[:, :, f], op0=ALU.mult, op1=ALU.add))
            c.sync()

        @block.tensor
        def _(pe):
            pe.wait_ge(scanned, 1)
            nc.tensor.transpose(last_ps[0:w, 0:P], msgs[:, COLS - 1, 0:w], s["ident"][:]).then_inc(turned, 1)
            pe.wait_ge(chained, 1)
            nc.tensor.transpose(carry_ps[:, 0:w], carry_t[0:w, :], s["ident"][0:w, 0:w]).then_inc(back, 1)


def write_phase(nc, s, name, o, msgs, width, table):
    with Phase(nc, name) as ph:
        idx = ph.sb("idx", [P, RING, GROUP], i32)
        data = ph.sb("data", [P, RING, GROUP * width])
        staged, tick = ph.sem("staged"), ph.sem("tick")
        ring = s["ring"]
        block = ph.block()

        @block.scalar
        def _(act):
            def stage(t, first):
                for g in range(RING):
                    if not first:
                        ring.done(act, g, 16 * GROUP * t)
                    col = bass.ds(t * BODY + g * GROUP, GROUP)
                    nc.scalar.copy(idx[:, g, :], o["write"][:, col]).then_inc(staged, 1)
                    nc.scalar.copy(data[:, g, :].rearrange("p (k w) -> p k w", w=width), msgs[:, col, :]).then_inc(staged, 1)

            turns(act, stage)

        @block.gpsimd
        def _(pool):
            def put(t, first):
                for g in range(RING):
                    pool.wait_ge(staged, 2 * (RING * t + g + 1))
                    pool.sem_inc(tick, 1)
                    for k in range(GROUP):
                        pool.indirect_dma_start(
                            out=table, out_offset=bass.IndirectOffsetOnAxis(ap=idx[:, g, k:k + 1], axis=0),
                            in_=data[:, g, k * width:(k + 1) * width], in_offset=None,
                            bounds_check=NODES - 1, oob_is_err=False).then_inc(ring.sems[g], 16)

            turns(pool, put)
            for g in range(RING):
                ring.done(pool, g, 16 * GROUP * TURNS)
    s["ring"].end_phase(range(RING), 16 * GROUP * TURNS)


def norm_phase(nc, s, name, add_table, out_table):
    PIECE = 160
    W = PIECE * F
    NP = NODE_COLS // PIECE
    N = NODE_PARTS
    with Phase(nc, name) as ph:
        wa, wh = (F if t is None else t.shape[1] for t in (add_table, out_table))
        add = ph.sb("add", [N, 2, PIECE * wa])
        cent = ph.sb("cent", [N, 2, W])
        square = ph.sb("square", [N, W])
        h = ph.sb("h", [N, 2, PIECE * wh])
        mean, var, inv = ph.sb("mean", [N, PIECE]), ph.sb("var", [N, PIECE]), ph.sb("inv", [N, PIECE])
        root, step = ph.sb("root", [N, PIECE]), ph.sb("step", [N, PIECE])
        own, centred, squared, varied, rooted, done = (ph.sem(n) for n in ("own", "centred", "squared", "varied", "rooted", "done"))
        landed = [ph.sem(f"landed{b}") for b in range(2)]
        stored = [ph.sem(f"stored{b}") for b in range(2)]
        used = ph.sem("used")
        block = ph.block()
        src = None if add_table is None else node_rows(add_table)
        dst = node_rows(out_table)
        by_node = lambda ap: ap.rearrange("p (n f) -> p n f", f=F)
        spread = lambda ap: ap.unsqueeze(2).to_broadcast([N, PIECE, F])

        @block.sync
        def _(sp):
            for i in range(NP):
                if src is not None:
                    if i >= 2:
                        sp.wait_ge(used, i - 1)
                    node_dma(sp, add[:, i % 2, :], src[:, i * PIECE * wa:(i + 1) * PIECE * wa], landed[i % 2])

        @block.vector
        def _(dve):
            c = Chain(dve, own)
            for i in range(NP):
                x = s["x"][0:N, i * W:(i + 1) * W]
                if src is not None:
                    dve.wait_ge(landed[i % 2], 32 * (i // 2 + 1))
                    more = add[:, i % 2, :].rearrange("p (n f) -> p n f", f=wa)
                    if wa > F:
                        nc.vector.tensor_copy(s["place"][0:N, i * PIECE:(i + 1) * PIECE], more[:, :, F])
                    nc.vector.tensor_tensor(by_node(x), by_node(x), more[:, :, 0:F], ALU.add).then_inc(used, 1)
                    dve.wait_ge(used, i + 1)
                c.do(nc.vector.tensor_reduce(mean[:], by_node(x), AX, ALU.add))
                c.sync()
                c.do(nc.vector.tensor_scalar(mean[:], mean[:], 1.0 / F, None, ALU.mult))
                c.sync()
                nc.vector.tensor_tensor(by_node(cent[:, i % 2, :]), by_node(x), spread(mean[:]),
                                        ALU.subtract).then_inc(centred, 1)
                dve.wait_ge(squared, i + 1)
                c.do(nc.vector.tensor_reduce(var[:], by_node(square[:]), AX, ALU.add))
                c.sync()
                nc.vector.tensor_scalar(var[:], var[:], 1.0 / F, EPS, ALU.mult, ALU.add).then_inc(varied, 1)
                dve.wait_ge(rooted, i + 1)
                c.do(nc.vector.reciprocal(inv[:], root[:]))
                c.sync()
                c.do(nc.vector.tensor_tensor(step[:], inv[:], inv[:], ALU.mult))
                c.sync()
                c.do(nc.vector.tensor_tensor(step[:], step[:], var[:], ALU.mult))
                c.sync()
                c.do(nc.vector.tensor_scalar(step[:], step[:], -0.5, 1.5, ALU.mult, ALU.add))
                c.sync()
                c.do(nc.vector.tensor_tensor(inv[:], inv[:], step[:], ALU.mult))
                c.sync()
                if i >= 2:
                    dve.wait_ge(stored[i % 2], 32 * (i // 2))
                res = h[:, i % 2, :].rearrange("p (n f) -> p n f", f=wh)
                if wh > F:
                    nc.vector.tensor_copy(res[:, :, F], s["place"][0:N, i * PIECE:(i + 1) * PIECE])
                nc.vector.scalar_tensor_tensor(out=res[:, :, 0:F], in0=by_node(cent[:, i % 2, :]), scalar=0.0,
                                               in1=spread(inv[:]), op0=ALU.max, op1=ALU.mult).then_inc(done, 1)
                dve.wait_ge(done, i + 1)

        @block.scalar
        def _(act):
            for i in range(NP):
                act.wait_ge(centred, i + 1)
                if i >= 1:
                    act.wait_ge(varied, i)
                nc.scalar.activation(square[:], cent[:, i % 2, :], ACT.Square).then_inc(squared, 1)
                act.wait_ge(varied, i + 1)
                nc.scalar.activation(root[:], var[:], ACT.Sqrt).then_inc(rooted, 1)
                act.wait_ge(done, i + 1)
                node_dma(act, dst[:, i * PIECE * wh:(i + 1) * PIECE * wh], h[:, i % 2, :], stored[i % 2])
            for b in range(2):
                act.wait_ge(stored[b], 32 * ((NP + 1 - b) // 2))


def basis_phase(nc, s, attr, basis, place):
    B = BASIS
    with Phase(nc, "hat") as ph:
        hat = ph.sb("hat", [P, 2, COLS, B])
        away = ph.sb("away", [P, 2, COLS, B])
        shift = ph.sb("shift", [P, B])
        place_i = ph.sb("place_i", [P, COLS], i32)
        numbered = ph.sem("numbered")
        own, set_, far, near = ph.sem("own"), ph.sem("set"), ph.sem("far"), ph.sem("near")
        block = ph.block()

        @block.vector
        def _(dve):
            dve.wait_ge(numbered, 1)
            nc.vector.tensor_copy(place, place_i[:])
            for u in range(B):
                nc.vector.memset(shift[:, u:u + 1], 1.0 - u * 2.0 / (B - 1)).then_inc(set_, 1)
            dve.wait_ge(near, 1)
            nc.vector.tensor_tensor(basis[:].rearrange("p e (u v) -> p e u v", v=B),
                                    hat[:, 0, :, :].unsqueeze(3).to_broadcast([P, COLS, B, B]),
                                    hat[:, 1, :, :].unsqueeze(2).to_broadcast([P, COLS, B, B]), ALU.mult).then_inc(own, 1)
            dve.wait_ge(own, 1)

        @block.gpsimd
        def _(pool):
            nc.gpsimd.iota(place_i[:], pattern=[[1, COLS]], base=1, channel_multiplier=COLS).then_inc(numbered, 1)

        @block.scalar
        def _(act):
            act.wait_ge(set_, B)
            for a in range(2):
                for u in range(B):
                    nc.scalar.activation(away[:, a, :, u], attr[:, :, a], ACT.Abs, bias=shift[:, u:u + 1]).then_inc(far, 1)
            act.wait_ge(far, 2 * B)
            nc.scalar.activation(hat[:], away[:], ACT.Relu, bias=s["ones"][:, 0:1], scale=-(B - 1) / 2.0).then_inc(near, 1)


def pad_phase(nc, name, tiles, places):
    with Phase(nc, name) as ph:
        zeroed, loaded = ph.sem("zeroed"), ph.sem("loaded")
        block = ph.block()

        @block.vector
        def _(dve):
            for tile in tiles:
                nc.vector.memset(tile, 0.0).then_inc(zeroed, 1)

        @block.sync
        def _(sp):
            sp.wait_ge(zeroed, len(tiles))
            for place, source in places:
                sp.dma_start(place, source).then_inc(loaded, 16)
            if places:
                sp.wait_ge(loaded, 16 * len(places))


def wait(eng, sem, value):
    if not isinstance(value, int) or value > 0:
        eng.wait_ge(sem, value)


def fold_phase(nc, s, d, w):
    H2 = HID // P
    with Phase(nc, "fold") as ph:
        pre = ph.sb("pre", [P, H2, HID])
        pre_t = ph.sb("pre_t", [P, H2, HID])
        right = {"msg": ph.sb("conv", [P, H2, HID]), "self": ph.sb("post", [P, H2, HID])}
        pre_b = ph.sb("pre_b", [P, H2])
        bias = {"msg": ph.sb("conv_b", [P, H2]), "self": ph.sb("post_b", [P, H2])}
        turn_ps = ph.ps("turn_ps", [P, H2, HID])
        prod_ps = {n: ph.ps(n + "_ps", [P, H2, HID]) for n in ("msg", "self")}
        bias_ps = ph.ps("bias_ps", [P, 8])
        loaded, turned, copied, made, own = (ph.sem(n) for n in ("loaded", "turned", "copied", "made", "own"))
        block = ph.block()
        mats = ((pre[:], d["L1_gnn_pre_w2"]), (right["msg"][:], d["L1_gnn_conv_w"]),
                (right["self"][:], d["L1_gnn_post_w1"][0:HID, :]), (w["agg"][:], d["L1_gnn_post_w1"][HID:, :]))
        vecs = ((pre_b, d["L1_gnn_pre_b2"]), (bias["msg"], d["L1_gnn_conv_b"]), (bias["self"], d["L1_gnn_post_b1"]),
                (w["pre_b1"], d["L1_gnn_pre_b1"]))

        @block.sync
        def _(sp):
            for tile, m in mats:
                sp.dma_start(tile, m.rearrange("(h p) o -> p h o", p=P)).then_inc(loaded, 16)
            for tile, v in vecs:
                for h in range(H2):
                    sp.dma_start(tile[:, h:h + 1], v[h * P:(h + 1) * P].rearrange("(p a) -> p a", a=1)).then_inc(loaded, 16)
            sp.wait_ge(loaded, 16 * (4 + 4 * H2))

        @block.tensor
        def _(pe):
            pe.wait_ge(loaded, 16 * (4 + 4 * H2))
            for k in range(H2):
                for i in range(H2):
                    last = nc.tensor.transpose(turn_ps[:, k, i * P:(i + 1) * P], pre[:, i, k * P:(k + 1) * P], s["ident"][:])
            last.then_inc(turned, 1)
            pe.wait_ge(copied, 1)
            col = 0
            for n in ("msg", "self"):
                for i in range(H2):
                    for k in range(H2):
                        nc.tensor.matmul(prod_ps[n][:, i, :], pre_t[:, k, i * P:(i + 1) * P], right[n][:, k, :],
                                         start=(k == 0), stop=(k == H2 - 1))
                for o in range(H2):
                    for k in range(H2):
                        last = nc.tensor.matmul(bias_ps[:, col:col + 1], right[n][:, k, o * P:(o + 1) * P],
                                                pre_b[:, k:k + 1], start=(k == 0), stop=(k == H2 - 1))
                    col += 1
            last.then_inc(made, 1)

        @block.vector
        def _(dve):
            dve.wait_ge(turned, 1)
            nc.vector.tensor_copy(pre_t[:], turn_ps[:]).then_inc(copied, 1)
            dve.wait_ge(made, 1)
            for m, n in enumerate(("msg", "self")):
                nc.vector.tensor_copy(w[n][:], prod_ps[n][:])
                nc.vector.tensor_tensor(w[n + "_b"][:], bias_ps[:, m * H2:(m + 1) * H2], bias[n][:], ALU.add)


def node_mlp_phase(nc, s, w, table, out):
    N, W, R5 = NODE_PARTS, NCHUNK * F, 5
    NT = NODE_COLS // NCHUNK // R5
    M = NG * N
    with Phase(nc, "nmlp") as ph:
        rows = ph.sb("rows", [N, R5, W])
        rows_t = ph.sb("rows_t", [P, M])
        hid = ph.sb("hid", [P, 2, 2, M])
        mid = ph.sb("mid", [P, 2, 2, M])
        res = ph.sb("res", [P, M])
        res_rows = ph.sb("res_rows", [N, R5, W])
        rows_ps, hid_ps, mid_ps = ph.ps("rows_ps", [P, 512]), ph.ps("hid_ps", [P, 2, 512]), ph.ps("mid_ps", [P, 2, 512])
        res_ps, back_ps = ph.ps("res_ps", [P, 512]), ph.ps("back_ps", [P, 512])
        turned, rows_ok, hid_made, hid_ok = ph.sem("turned"), ph.sem("rows_ok"), ph.sem("hid_made"), ph.sem("hid_ok")
        mid_made, mid_ok, added, res_ok = ph.sem("mid_made"), ph.sem("mid_ok"), ph.sem("added"), ph.sem("res_ok")
        back, back_ok, tick = ph.sem("back"), ph.sem("back_ok"), ph.sem("tick")
        landed = [ph.sem(f"landed{k}") for k in range(R5)]
        ring = s["ring"]
        block = ph.block()
        src, dst = node_rows(table), node_rows(out)

        @block.sync
        def _(sp):
            def load(t, first):
                for k in range(R5):
                    wait(sp, turned, R5 * (t - 1) + k + 1)
                    node_dma(sp, rows[:, k, :], src[:, bass.ds((t * R5 + k) * W, W)], landed[k])

            turns(sp, load, NT)

        @block.tensor
        def _(pe):
            def steps(t, first):
                def transpose(k):
                    c = R5 * t + k
                    pe.wait_ge(landed[k], 32 * (t + 1))
                    wait(pe, rows_ok, c)
                    for g in range(NG):
                        last = nc.tensor.transpose(rows_ps[:, g * N:(g + 1) * N], rows[:, k, g * P:(g + 1) * P],
                                                   s["ident"][0:N, 0:N])
                    last.then_inc(turned, 1)

                def hidden(k, q):
                    u = NS * (R5 * t + k) + q
                    pe.wait_ge(rows_ok, R5 * t + k + 1)
                    wait(pe, hid_ok, u)
                    for h in range(2):
                        last = nc.tensor.matmul(hid_ps[:, h, 0:M], w["pre_w1"][:, q, h * P:(h + 1) * P], rows_t[:],
                                                start=True, stop=True)
                    last.then_inc(hid_made, 1)

                def middle(k, q):
                    u = NS * (R5 * t + k) + q
                    pe.wait_ge(hid_ok, u + 1)
                    wait(pe, mid_ok, u)
                    for h in range(2):
                        for j in range(2):
                            last = nc.tensor.matmul(mid_ps[:, h, 0:M], w["self"][:, j, h * P:(h + 1) * P],
                                                    hid[:, q % 2, j, :], start=(j == 0), stop=(j == 1))
                    last.then_inc(mid_made, 1)

                def result(k, q):
                    u = NS * (R5 * t + k) + q
                    pe.wait_ge(mid_ok, u + 1)
                    if q == 0:
                        wait(pe, res_ok, R5 * t + k)
                    for j in range(2):
                        last = nc.tensor.matmul(res_ps[:, 0:M], w["post_w2"][:, j, q, :], mid[:, q % 2, j, :],
                                                start=(q == 0 and j == 0), stop=(q == NS - 1 and j == 1))
                    last.then_inc(added, 1)

                def finish(k):
                    c = R5 * t + k
                    result(k, NS - 1)
                    pe.wait_ge(res_ok, c + 1)
                    wait(pe, back_ok, c)
                    for g in range(NG):
                        last = nc.tensor.transpose(back_ps[0:N, g * P:(g + 1) * P], res[:, g * N:(g + 1) * N], s["ident"][:])
                    last.then_inc(back, 1)

                for k in range(R5):
                    transpose(k)
                    hidden(k, 0)
                    if k > 0:
                        finish(k - 1)
                    for q in range(NS):
                        if q < NS - 1:
                            hidden(k, q + 1)
                        middle(k, q)
                        if q > 0:
                            result(k, q - 1)
                finish(R5 - 1)

            turns(pe, steps, NT)

        @block.scalar
        def _(act):
            def steps(t, first):
                def tanh(k):
                    c = R5 * t + k
                    act.wait_ge(added, NS * (c + 1))
                    wait(act, back, c)
                    nc.scalar.activation(res[:], res_ps[:, 0:M], ACT.Tanh, bias=w["post_b2"][:, 0:1]).then_inc(res_ok, 1)

                for k in range(R5):
                    c = R5 * t + k
                    act.wait_ge(turned, c + 1)
                    wait(act, hid_made, NS * c)
                    nc.scalar.copy(rows_t[:], rows_ps[:, 0:M]).then_inc(rows_ok, 1)
                    for q in range(NS):
                        u = NS * c + q
                        act.wait_ge(hid_made, u + 1)
                        wait(act, mid_made, u - 1)
                        for h in range(2):
                            last = nc.scalar.activation(hid[:, q % 2, h, :], hid_ps[:, h, 0:M], ACT.Relu,
                                                        bias=w["pre_b1"][:, h:h + 1])
                        last.then_inc(hid_ok, 1)
                        if q == 0 and k > 0:
                            tanh(k - 1)
                tanh(R5 - 1)

            turns(act, steps, NT)

        @block.vector
        def _(dve):
            def steps(t, first):
                def give_back(k):
                    dve.wait_ge(back, R5 * t + k + 1)
                    if not first:
                        ring.done(dve, k, 16 * t)
                    nc.vector.tensor_copy(res_rows[:, k, :], back_ps[0:N, :]).then_inc(back_ok, 1)

                for k in range(R5):
                    if k > 0:
                        give_back(k - 1)
                    for q in range(NS):
                        u = NS * (R5 * t + k) + q
                        dve.wait_ge(mid_made, u + 1)
                        wait(dve, added, u - 1)
                        for h in range(2):
                            last = nc.vector.tensor_scalar(mid[:, q % 2, h, :], mid_ps[:, h, 0:M], w["self_b"][:, h:h + 1], 0.0,
                                                           ALU.add, ALU.max)
                        last.then_inc(mid_ok, 1)
                give_back(R5 - 1)

            turns(dve, steps, NT)

        @block.gpsimd
        def _(pool):
            def store(t, first):
                for k in range(R5):
                    pool.wait_ge(back_ok, R5 * t + k + 1)
                    pool.sem_inc(tick, 1)
                    pool.dma_start(dst[:, bass.ds((t * R5 + k) * W, W)], res_rows[:, k, :]).then_inc(ring.sems[k], 16)

            turns(pool, store, NT)
            for k in range(R5):
                ring.done(pool, k, 16 * NT)
    s["ring"].end_phase(range(5), 16 * (NODE_COLS // NCHUNK // 5))


def tile_order_phase(nc, s, name, o, flats, same_flat, tiles):
    Q, B = 98, COLS // 98
    with Phase(nc, name) as ph:
        clamped = ph.sb("clamped", [P, COLS])
        same16 = ph.sb("same16", [P, COLS], mybir.dt.bfloat16)
        back = ph.sb("back", [Q, 3, B, P])
        turned_ps = ph.ps("turned_ps", [P, 3, 512])
        made, out, landed, turned, own = (ph.sem(n) for n in ("made", "out", "landed", "turned", "own"))
        block = ph.block()

        @block.vector
        def _(dve):
            c = Chain(dve, own)
            c.do(nc.vector.tensor_scalar(clamped[:], o["key"][:], float(NODES - 1), None, ALU.min))
            c.do(nc.vector.tensor_copy(same16[:, 1:COLS], o["same"][:, 1:COLS]))
            c.do(nc.vector.tensor_copy(same16[:, 0:1], o["goes_on"][:]))
            c.sync()
            dve.sem_inc(made, 1)
            dve.wait_ge(turned, 1)
            for a in range(3):
                nc.vector.tensor_copy(tiles[a][:, 0:COLS], turned_ps[:, a, 0:COLS])
                nc.vector.memset(tiles[a][:, COLS:], 0)

        @block.sync
        def _(sp):
            sp.wait_ge(made, 1)
            for a, src in enumerate((o["other"], clamped, o["write"])):
                sp.dma_start(flats[a].rearrange("(p j) -> p j", j=COLS), src[:]).then_inc(out, 16)
            sp.dma_start(same_flat.rearrange("(p j) -> p j", j=COLS), same16[:]).then_inc(out, 16)
            sp.wait_ge(out, 64)
            for a in range(3):
                sp.dma_start(back[:, a, :, :], flats[a].rearrange("(b q p) -> q b p", q=Q, p=P)).then_inc(landed, 16)
            sp.wait_ge(landed, 48)

        @block.tensor
        def _(pe):
            pe.wait_ge(landed, 48)
            for a in range(3):
                for b in range(B):
                    last = nc.tensor.transpose(turned_ps[:, a, b * Q:(b + 1) * Q], back[:, a, b, :], s["ident"][0:Q, 0:Q])
            last.then_inc(turned, 1)


def edge_mlp_phase(nc, s, w, table, tiles, same_flat, out):
    E, G, Q = CHUNK * P, CG, CS
    KF = Q * F
    PIECES = E // 512
    with Phase(nc, "emlp") as ph:
        idx = ph.sb("idx", [P, 2, 2, CHUNK], i32)
        idx_out = ph.sb("idx_out", [P, 2, CHUNK], i32)
        rows = ph.sb("rows", [P, 2, 2, CHUNK * F])
        rows_t = ph.sb("rows_t", [KF, 2, 2, 512])
        same = ph.sb("same", [P, E], mybir.dt.bfloat16)
        hid = ph.sb("hid", [P, 2, 2, 512])
        msgs = ph.sb("msgs", [P, 2, 2, E])
        mid = ph.sb("mid", [P, 2, 2, 512])
        res = ph.sb("res", [KF, 512])
        res_rows = ph.sb("res_rows", [P, 2, CHUNK * F])
        rows_ps, hid_ps, mid_ps = ph.ps("rows_ps", [P, 512]), ph.ps("hid_ps", [P, 2, 512]), ph.ps("mid_ps", [P, 2, 512])
        res_ps, back_ps = ph.ps("res_ps", [P, 512]), ph.ps("back_ps", [P, 512])
        staged, tick, turned, rows_ok = ph.sem("staged"), ph.sem("tick"), ph.sem("turned"), ph.sem("rows_ok")
        hid_made = {n: ph.sem(n + "_hid_made") for n in "mz"}
        hid_ok = {n: ph.sem(n + "_hid_ok") for n in "mz"}
        mid_made = {n: ph.sem(n + "_mid_made") for n in "mz"}
        mid_ok = {n: ph.sem(n + "_mid_ok") for n in "mz"}
        scanned, added, res_ok, back, back_ok = (ph.sem(n) for n in ("scanned", "added", "res_ok", "back", "back_ok"))
        ring = s["ring"]
        same_in = ph.sem("same_in")
        block = ph.block()
        NC = COLS // CHUNK
        ROUND = 16 * CHUNK

        def alone(c):
            return isinstance(c, int) and c == 1

        @block.sync
        def _(sp):
            def load(t, first):
                for b in range(2):
                    c = 2 * t + b
                    wait(sp, scanned, PIECES * c)
                    sp.dma_start(same[:], same_flat[bass.ds(c * E, E)].partition_broadcast(P)).then_inc(same_in, 16)

            turns(sp, load)

        @block.gpsimd
        def _(pool):
            def put(c, b):
                pool.wait_ge(back_ok, c + 1)
                pool.sem_inc(tick, 1)
                for k in range(CHUNK):
                    pool.indirect_dma_start(
                        out=out, out_offset=bass.IndirectOffsetOnAxis(ap=idx_out[:, b, k:k + 1], axis=0),
                        in_=res_rows[:, b, k * F:(k + 1) * F], in_offset=None,
                        bounds_check=NODES - 1, oob_is_err=False).then_inc(ring.sems[4 + b], 16)

            def fetch(c, b):
                pool.wait_ge(staged, c + 1)
                pool.sem_inc(tick, 1)
                if not isinstance(c, int) or c >= 2:
                    pool.wait_ge(turned, 2 * (c - 1))
                    pool.sem_inc(tick, 1)
                for e in range(2):
                    for k in range(CHUNK):
                        pool.indirect_dma_start(
                            out=rows[:, b, e, k * F:(k + 1) * F], out_offset=None, in_=table,
                            in_offset=bass.IndirectOffsetOnAxis(ap=idx[:, b, e, k:k + 1], axis=0)).then_inc(ring.sems[2 * b + e], 16)

            def steps(t, first, last):
                for b in range(2):
                    if not first:
                        put(2 * t + b - 2, b)
                    if not (last and b == 1):
                        fetch(2 * t + b + 1, 1 - b)

            fetch(0, 0)
            steps(0, True, False)
            with pool.Fori(1, TURNS - 1) as t:
                steps(t, False, False)
            steps(TURNS - 1, False, True)
            for b in range(2):
                put(NC - 2 + b, b)
            for b in range(2):
                ring.done(pool, 4 + b, ROUND * TURNS)

        @block.tensor
        def _(pe):
            def transpose(c, b, t):
                for e in range(2):
                    ring.done(pe, 2 * b + e, ROUND * (t + 1))
                    wait(pe, rows_ok, 2 * c + e)
                    for g in range(G):
                        last = nc.tensor.transpose(rows_ps[0:KF, g * P:(g + 1) * P], rows[:, b, e, g * KF:(g + 1) * KF],
                                                   s["ident"][:])
                    last.then_inc(turned, 1)

            def hidden(kind, c, b, q):
                u = Q * c + q
                if kind == "m":
                    pe.wait_ge(rows_ok, 2 * c + 1)
                    if q == 0:
                        wait(pe, hid_ok["z"], Q * (c - 1))
                        if alone(c):
                            pe.wait_ge(hid_ok["m"], Q)
                else:
                    pe.wait_ge(rows_ok, 2 * c + 2)
                    if q == 0:
                        wait(pe, hid_ok["m"], Q * (c + 1) if isinstance(c, int) and c == NC - 1 else Q * (c + 2))
                if q > 0:
                    pe.wait_ge(hid_ok[kind], u)
                for h in range(2):
                    last = nc.tensor.matmul(hid_ps[:, h, :], w["pre_w1"][0:KF, q, h * P:(h + 1) * P],
                                            rows_t[:, b, 0 if kind == "m" else 1, :], start=True, stop=True)
                last.then_inc(hid_made[kind], 1)

            def middle(kind, c, b, q):
                u = Q * c + q
                slot = q % 2 if kind == "m" else (q + 1) % 2
                pe.wait_ge(hid_ok[kind], u + 1)
                if q == 0:
                    if kind == "m":
                        wait(pe, mid_ok["z"], Q * (c - 1))
                        if alone(c):
                            pe.wait_ge(mid_ok["m"], Q)
                    else:
                        wait(pe, mid_ok["m"], Q * (c + 1) if isinstance(c, int) and c == NC - 1 else Q * (c + 2))
                        pe.wait_ge(scanned, PIECES * (c + 1))
                else:
                    pe.wait_ge(mid_ok[kind], u)
                for h in range(2):
                    for j in range(2):
                        last = nc.tensor.matmul(mid_ps[:, h, :], w["msg" if kind == "m" else "self"][:, j, h * P:(h + 1) * P],
                                                hid[:, slot, j, :], start=(j == 0), stop=(kind == "m" and j == 1))
                    if kind == "z":
                        for j in range(2):
                            sums = msgs[:, b, j, :].rearrange("p (g q e) -> p g q e", q=Q, e=P)[:, :, q, :]
                            last = nc.tensor.matmul(mid_ps[:, h, :], w["agg"][:, j, h * P:(h + 1) * P], sums,
                                                    start=False, stop=(j == 1))
                last.then_inc(mid_made[kind], 1)

            def result(c, b, q):
                u = Q * c + q
                pe.wait_ge(mid_ok["z"], u + 1)
                if q == 0:
                    wait(pe, res_ok, c)
                for j in range(2):
                    last = nc.tensor.matmul(res_ps[0:KF, :], w["post_w2"][:, j, q, 0:KF], mid[:, q % 2, j, :],
                                            start=(q == 0 and j == 0), stop=(q == Q - 1 and j == 1))
                last.then_inc(added, 1)

            def run(items):
                hidden(*items[0])
                for n, item in enumerate(items):
                    if n + 1 < len(items):
                        hidden(*items[n + 1])
                    middle(*item)
                    if item[0] == "z" and item[3] > 0:
                        result(item[1], item[2], item[3] - 1)
                if items[-1][0] == "z":
                    _, c, b, q = items[-1]
                    result(c, b, q)
                    pe.wait_ge(res_ok, c + 1)
                    wait(pe, back_ok, c)
                    for g in range(G):
                        last = nc.tensor.transpose(back_ps[:, g * KF:(g + 1) * KF], res[:, g * P:(g + 1) * P],
                                                   s["ident"][0:KF, 0:KF])
                    last.then_inc(back, 1)

            def steps(t, first):
                for b in range(2):
                    c = 2 * t + b
                    transpose(c, b, t)
                    items = [("m", c, b, q) for q in range(Q)]
                    if not (first and b == 0):
                        items += [("z", c - 1, 1 - b, q) for q in range(Q)]
                    run(items)

            turns(pe, steps)
            run([("z", NC - 1, 1, q) for q in range(Q)])

        @block.scalar
        def _(act):
            def evacuate(kind, c, q):
                u = Q * c + q
                slot = q % 2 if kind == "m" else (q + 1) % 2
                act.wait_ge(hid_made[kind], u + 1)
                if q >= 2:
                    act.wait_ge(mid_made[kind], u - 1)
                elif kind == "m":
                    wait(act, mid_made["z"], Q * (c - 1) - 1 + q)
                    if alone(c):
                        act.wait_ge(mid_made["m"], Q)
                else:
                    last_m = Q * (c + 1) if isinstance(c, int) and c == NC - 1 else Q * (c + 2)
                    act.wait_ge(mid_made["m"], last_m - 1 + q)
                for h in range(2):
                    last = nc.scalar.activation(hid[:, slot, h, :], hid_ps[:, h, :], ACT.Relu, bias=w["pre_b1"][:, h:h + 1])
                last.then_inc(hid_ok[kind], 1)

            def tanh(c):
                act.wait_ge(added, Q * (c + 1))
                wait(act, back, c)
                nc.scalar.activation(res[:], res_ps[0:KF, :], ACT.Tanh, bias=w["post_b2"][0:KF, 0:1]).then_inc(res_ok, 1)

            def steps(t, first):
                for b in range(2):
                    c = 2 * t + b
                    for e in range(2):
                        act.wait_ge(turned, 2 * c + e + 1)
                        wait(act, hid_made["m" if e == 0 else "z"], Q * (c - 1))
                        nc.scalar.copy(rows_t[:, b, e, :], rows_ps[0:KF, :]).then_inc(rows_ok, 1)
                    for q in range(Q):
                        evacuate("m", c, q)
                    if not (first and b == 0):
                        for q in range(Q):
                            evacuate("z", c - 1, q)
                        tanh(c - 1)

            turns(act, steps)
            for q in range(Q):
                evacuate("z", NC - 1, q)
            tanh(NC - 1)

        @block.vector
        def _(dve):
            def stage(c, b, turns_before):
                for e in range(2):
                    if not isinstance(turns_before, int) or turns_before > 0:
                        ring.done(dve, 2 * b + e, ROUND * turns_before)
                for e in range(2):
                    last = nc.vector.tensor_copy(idx[:, b, e, :], tiles[e][:, bass.ds(c * CHUNK, CHUNK)])
                last.then_inc(staged, 1)

            def message(c, b, q):
                u = Q * c + q
                dve.wait_ge(mid_made["m"], u + 1)
                if q == 0:
                    wait(dve, mid_made["z"], Q * (c - 1))
                for h in range(2):
                    place = msgs[:, b, h, :].rearrange("p (g q e) -> p g q e", q=Q, e=P)[:, :, q, :]
                    last = nc.vector.tensor_scalar(place, mid_ps[:, h, :].rearrange("p (g e) -> p g e", e=P),
                                                   w["msg_b"][:, h:h + 1], 0.0, ALU.add, ALU.max)
                last.then_inc(mid_ok["m"], 1)

            def scan(c, b, t, n, very_first):
                if n == 0:
                    dve.wait_ge(same_in, 16 * (c + 1))
                    dve.wait_ge(mid_ok["m"], Q * (c + 1))
                wait(dve, scanned, PIECES * c + n)
                a = 512 * n
                for h in range(2):
                    before = msgs[:, b, h, a - 1:a] if n else (0.0 if very_first else msgs[:, 1 - b, h, E - 1:E])
                    last = nc.vector.tensor_tensor_scan(msgs[:, b, h, a:a + 512], same[:, a:a + 512],
                                                        msgs[:, b, h, a:a + 512], before, ALU.mult, ALU.add)
                last.then_inc(scanned, 1)

            def middle(c, q):
                u = Q * c + q
                dve.wait_ge(mid_made["z"], u + 1)
                wait(dve, added, u - 1)
                for h in range(2):
                    last = nc.vector.tensor_scalar(mid[:, q % 2, h, :], mid_ps[:, h, :], w["self_b"][:, h:h + 1], 0.0,
                                                   ALU.add, ALU.max)
                last.then_inc(mid_ok["z"], 1)

            def give_back(c, b, turns_before):
                dve.wait_ge(back, c + 1)
                if not isinstance(turns_before, int) or turns_before > 0:
                    ring.done(dve, 4 + b, ROUND * turns_before)
                nc.vector.tensor_copy(idx_out[:, b, :], tiles[2][:, bass.ds(c * CHUNK, CHUNK)])
                nc.vector.tensor_copy(res_rows[:, b, :], back_ps[:, 0:CHUNK * F]).then_inc(back_ok, 1)

            def steps(t, first):
                for b in range(2):
                    c = 2 * t + b
                    for q in range(Q):
                        message(c, b, q)
                    stage(c + 2, b, t + 1)
                    for n in range(PIECES):
                        if not (first and b == 0):
                            middle(c - 1, n)
                        scan(c, b, t, n, first and b == 0)
                    if not (first and b == 0):
                        give_back(c - 1, 1 - b, t if b == 1 else t - 1)

            for b in range(2):
                stage(b, b, 0)
            turns(dve, steps)
            for q in range(Q):
                middle(NC - 1, q)
            give_back(NC - 1, 1, TURNS - 1)
    s["ring"].end_phase(range(6), 16 * COLS // 2)


def mean_weight_phase(nc, s, o, kind, weights):
    R = RELS
    with Phase(nc, "mean") as ph:
        hot = ph.sb("hot", [P, COLS, R])
        seen = ph.sb("seen", [P, COLS, R])
        after = ph.sb("after", [P, COLS])
        in_last = ph.sb("in_last", [P, COLS])
        own_count = ph.sb("own_count", [P, COLS])
        into, mult, carry_t = ph.sb("into", [R, P]), ph.sb("mult", [R, P]), ph.sb("carry_t", [R, P])
        carry = ph.sb("carry", [P, R])
        edge_ps, carry_ps = ph.ps("edge_ps", [R, 512]), ph.ps("carry_ps", [P, 512])
        own, ready, turned, chained, back = (ph.sem(n) for n in ("own", "ready", "turned", "chained", "back"))
        block = ph.block()

        @block.vector
        def _(dve):
            c = Chain(dve, own)
            c.do(nc.vector.tensor_tensor(hot[:], s["iota"][:, 0:R].unsqueeze(1).to_broadcast([P, COLS, R]),
                                         kind[:].unsqueeze(2).to_broadcast([P, COLS, R]), ALU.is_equal))
            c.do(nc.vector.tensor_copy(after[:, 0:COLS - 1], o["same"][:, 1:COLS]))
            c.do(nc.vector.memset(after[:, COLS - 1:COLS], 0.0))
            c.do(nc.vector.tensor_scalar(in_last[:], o["key"][:], o["key"][:, COLS - 1:COLS], None, ALU.is_equal))
            c.do(nc.vector.memset(into[:], 0.0))
            c.do(nc.vector.memset(mult[:], 0.0))
            c.sync()
            for r in range(R):
                c.do(nc.vector.tensor_tensor_scan(seen[:, :, r], o["same"][:], hot[:, :, r], 0.0, ALU.mult, ALU.add))
            c.do(nc.vector.tensor_tensor(mult[:, 1:P], o["cross"][0:R, 1:P], o["span"][0:R, 0:P - 1], ALU.mult))
            c.sync()
            dve.sem_inc(ready, 1)
            dve.wait_ge(turned, 1)
            c.do(nc.vector.tensor_tensor(into[:, 1:P], o["cross"][0:R, 1:P], edge_ps[:, 0:P - 1], ALU.mult))
            c.sync()
            c.do(nc.vector.tensor_tensor_scan(carry_t[:], mult[:], into[:], 0.0, ALU.mult, ALU.add))
            c.sync()
            dve.sem_inc(chained, 1)
            dve.wait_ge(back, 1)
            c.do(nc.vector.tensor_copy(carry[:], carry_ps[:, 0:R]))
            c.sync()
            for r in range(R):
                c.do(nc.vector.scalar_tensor_tensor(out=seen[:, :, r], in0=o["first"][:], scalar=carry[:, r:r + 1],
                                                    in1=seen[:, :, r], op0=ALU.mult, op1=ALU.add))
            c.sync()
            for r in range(R):
                c.do(nc.vector.tensor_tensor_scan(seen[:, ::-1, r], after[:, ::-1], seen[:, ::-1, r], 0.0, ALU.mult, ALU.max))
            c.do(nc.vector.memset(into[:], 0.0))
            c.do(nc.vector.memset(mult[:], 0.0))
            c.sync()
            c.do(nc.vector.tensor_tensor(mult[:, 0:P - 1], o["cross"][0:R, 1:P], o["span"][0:R, 1:P], ALU.mult))
            dve.sem_inc(ready, 1)
            dve.wait_ge(turned, 2)
            c.do(nc.vector.tensor_tensor(into[:, 0:P - 1], o["cross"][0:R, 1:P], edge_ps[:, 1:P], ALU.mult))
            c.sync()
            c.do(nc.vector.tensor_tensor_scan(carry_t[:, ::-1], mult[:, ::-1], into[:, ::-1], 0.0, ALU.mult, ALU.max))
            c.sync()
            dve.sem_inc(chained, 1)
            dve.wait_ge(back, 2)
            c.do(nc.vector.tensor_copy(carry[:], carry_ps[:, 0:R]))
            c.sync()
            for r in range(R):
                c.do(nc.vector.scalar_tensor_tensor(out=seen[:, :, r], in0=in_last[:], scalar=carry[:, r:r + 1],
                                                    in1=seen[:, :, r], op0=ALU.mult, op1=ALU.max))
            c.sync()
            c.do(nc.vector.tensor_tensor(seen[:], seen[:], hot[:], ALU.mult))
            c.sync()
            c.do(nc.vector.tensor_reduce(own_count[:], seen[:], AX, ALU.add))
            c.sync()
            c.do(nc.vector.reciprocal(own_count[:], own_count[:]))
            c.sync()
            c.do(nc.vector.tensor_tensor(weights[:], hot[:], own_count[:].unsqueeze(2).to_broadcast([P, COLS, R]), ALU.mult))
            c.sync()

        @block.tensor
        def _(pe):
            for n in range(2):
                pe.wait_ge(ready, n + 1)
                col = COLS - 1 if n == 0 else 0
                nc.tensor.transpose(edge_ps[:, 0:P], seen[:, col, :], s["ident"][:]).then_inc(turned, 1)
                pe.wait_ge(chained, n + 1)
                nc.tensor.transpose(carry_ps[:, 0:R], carry_t[:], s["ident"][0:R, 0:R]).then_inc(back, 1)


def node_relation_phase(nc, s, w, table, agg, mid_table):
    N, R5 = NODE_PARTS, 5
    W1, W2 = NCHUNK * F, NCHUNK * F2
    NT = NODE_COLS // NCHUNK // R5
    with Phase(nc, "nrel") as ph:
        rows = ph.sb("rows", [N, R5, W1])
        sums = ph.sb("sums", [N, R5, W2])
        rows_t = ph.sb("rows_t", [P, NG * N])
        mid = ph.sb("mid", [N, R5, W2])
        mid_t = ph.sb("mid_t", [P, 2 * NG * N])
        rows_ps = ph.ps("rows_ps", [P, 512])
        mid_ps = ph.ps("mid_ps", [P, 2, 512])
        mid_t_ps = ph.ps("mid_t_ps", [P, 2, 512])
        out_ps = ph.ps("out_ps", [P, 512])
        turned, rows_ok, mid_made, mid_sum, mid_ok = (ph.sem(n) for n in ("turned", "rows_ok", "mid_made", "mid_sum", "mid_ok"))
        mid_turned, mid_t_ok, out_made, out_ok, tick = (ph.sem(n) for n in ("mid_turned", "mid_t_ok", "out_made", "out_ok", "tick"))
        landed = [ph.sem(f"landed{k}") for k in range(R5)]
        ring = s["ring"]
        block = ph.block()
        src, agg_rows, dst = node_rows(table), node_rows(agg), node_rows(mid_table)

        @block.sync
        def _(sp):
            def load(t, first):
                for k in range(R5):
                    wait(sp, mid_sum, R5 * (t - 1) + k + 1)
                    node_dma(sp, rows[:, k, :], src[:, bass.ds((t * R5 + k) * W1, W1)], landed[k])
                    node_dma(sp, sums[:, k, :], agg_rows[:, bass.ds((t * R5 + k) * W2, W2)], landed[k])

            turns(sp, load, NT)

        @block.tensor
        def _(pe):
            def steps(t, first):
                for k in range(R5):
                    c = R5 * t + k
                    pe.wait_ge(landed[k], 64 * (t + 1))
                    wait(pe, rows_ok, c)
                    for g in range(NG):
                        last = nc.tensor.transpose(rows_ps[:, g * N:(g + 1) * N], rows[:, k, g * P:(g + 1) * P],
                                                   s["ident"][0:N, 0:N])
                    last.then_inc(turned, 1)
                    pe.wait_ge(rows_ok, c + 1)
                    wait(pe, mid_sum, c)
                    for g in range(NG):
                        dst_ps = mid_ps[0:N, g // 2, (g % 2) * 256:(g % 2 + 1) * 256]
                        nc.tensor.matmul(dst_ps, rows_t[:, g * N:(g + 1) * N], w["root1"][:], start=True, stop=False)
                        last = nc.tensor.matmul(dst_ps, s["ones"][0:1, 0:N], w["b1"][0:1, :], start=False, stop=True)
                    last.then_inc(mid_made, 1)
                    pe.wait_ge(mid_ok, c + 1)
                    wait(pe, mid_t_ok, c)
                    for g in range(2 * NG):
                        last = nc.tensor.transpose(mid_t_ps[:, g // 4, (g % 4) * N:(g % 4 + 1) * N], mid[:, k, g * P:(g + 1) * P],
                                                   s["ident"][0:N, 0:N])
                    last.then_inc(mid_turned, 1)
                    pe.wait_ge(mid_t_ok, c + 1)
                    wait(pe, out_ok, c)
                    for g in range(2 * NG):
                        dst_ps = out_ps[0:N, g * 64:(g + 1) * 64]
                        nc.tensor.matmul(dst_ps, mid_t[:, g * N:(g + 1) * N], w["root2"][:], start=True, stop=False)
                        last = nc.tensor.matmul(dst_ps, s["ones"][0:1, 0:N], w["b2"][0:1, :], start=False, stop=True)
                    last.then_inc(out_made, 1)

            turns(pe, steps, NT)

        @block.scalar
        def _(act):
            def steps(t, first):
                for k in range(R5):
                    c = R5 * t + k
                    act.wait_ge(turned, c + 1)
                    wait(act, mid_made, c)
                    nc.scalar.copy(rows_t[:], rows_ps[:, 0:NG * N]).then_inc(rows_ok, 1)
                    act.wait_ge(mid_sum, c + 1)
                    nc.scalar.activation(mid[:, k, :], mid[:, k, :], ACT.Relu).then_inc(mid_ok, 1)
                    act.wait_ge(mid_turned, c + 1)
                    wait(act, out_made, c)
                    nc.scalar.copy(mid_t[:].rearrange("p (b m) -> p b m", b=2), mid_t_ps[:, :, 0:4 * N]).then_inc(mid_t_ok, 1)

            turns(act, steps, NT)

        @block.vector
        def _(dve):
            def steps(t, first):
                for k in range(R5):
                    c = R5 * t + k
                    dve.wait_ge(mid_made, c + 1)
                    if not first:
                        ring.done(dve, k, 16 * t)
                    nc.vector.tensor_tensor(mid[:, k, :], mid_ps[0:N, :, :].rearrange("p b m -> p (b m)"), sums[:, k, :],
                                            ALU.add).then_inc(mid_sum, 1)
                    dve.wait_ge(out_made, c + 1)
                    x = s["x"][0:N, bass.ds(c * W1, W1)]
                    nc.vector.tensor_tensor(x, x, out_ps[0:N, :], ALU.add).then_inc(out_ok, 1)

            turns(dve, steps, NT)

        @block.gpsimd
        def _(pool):
            def store(t, first):
                for k in range(R5):
                    pool.wait_ge(mid_ok, R5 * t + k + 1)
                    pool.sem_inc(tick, 1)
                    pool.dma_start(dst[:, bass.ds((t * R5 + k) * W2, W2)], mid[:, k, :]).then_inc(ring.sems[k], 16)

            turns(pool, store, NT)
            for k in range(R5):
                ring.done(pool, k, 16 * NT)
    s["ring"].end_phase(range(5), 16 * (NODE_COLS // NCHUNK // 5))


def propagate_phase(nc, s, name, table, gather, weight, o, msgs, next_gather=None):
    width = F if next_gather is None else F + 1
    with Phase(nc, name) as ph:
        idx = ph.sb("idx", [P, RING, GROUP], i32)
        rows = ph.sb("rows", [P, RING, GROUP * width])
        staged, used, tick, scaled, scanned = (ph.sem(n) for n in ("staged", "used", "tick", "scaled", "scanned"))
        ring = s["ring"]
        block = ph.block()

        @block.gpsimd
        def _(pool):
            def fetch(t, first):
                for g in range(RING):
                    pool.wait_ge(staged, RING * t + g + 1)
                    pool.sem_inc(tick, 1)
                    if not first:
                        pool.wait_ge(used, RING * (t - 1) + g + 1)
                        pool.sem_inc(tick, 1)
                    for k in range(GROUP):
                        pool.indirect_dma_start(
                            out=rows[:, g, k * width:(k + 1) * width], out_offset=None, in_=table,
                            in_offset=bass.IndirectOffsetOnAxis(ap=idx[:, g, k:k + 1], axis=0)).then_inc(ring.sems[g], 16)

            turns(pool, fetch)

        @block.scalar
        def _(act):
            for g in range(RING):
                nc.scalar.copy(idx[:, g, :], gather[:, g * GROUP:(g + 1) * GROUP]).then_inc(staged, 1)

            def stage(t, first):
                for g in range(RING):
                    ring.done(act, g, 16 * GROUP * (t + 1))
                    nc.scalar.copy(idx[:, g, :], gather[:, bass.ds((t + 1) * BODY + g * GROUP, GROUP)]).then_inc(staged, 1)

            turns(act, stage)

        @block.vector
        def _(dve):
            def scale(t, first):
                for g in range(RING):
                    ring.done(dve, g, 16 * GROUP * (t + 1))
                    col = bass.ds(t * BODY + g * GROUP, GROUP)
                    row = rows[:, g, :].rearrange("p (k f) -> p k f", f=width)
                    if next_gather is not None:
                        nc.vector.tensor_copy(next_gather[:, col], row[:, :, F])
                    nc.vector.tensor_tensor(msgs[:, col, 0:F], row[:, :, 0:F],
                                            weight[:, col].unsqueeze(2).to_broadcast([P, GROUP, F]), ALU.mult).then_inc(used, 1)
                dve.wait_ge(used, RING * (t + 1))
                scan_turn(nc, dve, scanned, o, msgs, F, t, first)

            turns(dve, scale)

    s["ring"].end_phase(range(RING), 16 * GROUP * TURNS)


def keep_phase(nc, name, msgs, table):
    with Phase(nc, name) as ph:
        stored = ph.sem("stored")
        block = ph.block()

        @block.sync
        def _(sp):
            sp.dma_start(table[1:1 + SLOTS, :].rearrange("(p j) f -> p j f", j=COLS), msgs[:, :, 0:F]).then_inc(stored, 16)
            sp.wait_ge(stored, 16)


def finish_phase(nc, s, table, out):
    PARTS, N = 5, NODE_PARTS
    W = NODE_COLS * F // PARTS
    with Phase(nc, "fin") as ph:
        add = ph.sb("add", [N, PARTS, W])
        summed, stored = ph.sem("summed"), ph.sem("stored")
        landed = [ph.sem(f"landed{i}") for i in range(PARTS)]
        block = ph.block()
        src, dst = node_rows(table), node_rows(out)

        @block.sync
        def _(sp):
            for i in range(PARTS):
                node_dma(sp, add[:, i, :], src[:, i * W:(i + 1) * W], landed[i])
            for i in range(PARTS):
                sp.wait_ge(summed, i + 1)
                node_dma(sp, dst[:, i * W:(i + 1) * W], add[:, i, :], stored)
            sp.wait_ge(stored, 32 * PARTS)

        @block.vector
        def _(dve):
            for i in range(PARTS):
                dve.wait_ge(landed[i], 32)
                nc.vector.tensor_tensor(add[:, i, :], s["x"][0:N, i * W:(i + 1) * W], add[:, i, :], ALU.add).then_inc(summed, 1)


def graph_kernel(nc, d, out):
    ctx = ExitStack()
    internal = lambda name, shape, dt=fp32: nc.dram_tensor(name, shape, dt, kind="Internal").ap()
    tables = {n: internal("t_" + n, (NODES, w)) for n, w in
              (("h0", F), ("agg0", F + 1), ("h1", F), ("mlp", F), ("h2", F), ("agg2", F2), ("mid", F2), ("agg3", F),
               ("y0", F + 1), ("y4", F))}
    steps = [internal(f"step{n}", (SLOTS + 1, F)) for n in range(STEPS - 1)]
    scratch = {"lo": internal("count_lo", (LO,)), "hi": internal("count_hi", (HI,))}
    sorted_once, sorted_src, sorted_dst = (internal(n, (SLOTS, REC)) for n in ("sorted_once", "sorted_src", "sorted_dst"))
    flats = [internal(f"flat{a}", (SLOTS,)) for a in range(3)]
    same_flat = internal("same_flat", (SLOTS,), mybir.dt.bfloat16)

    with ctx:
        def sb(name, shape, dt=fp32, to=ctx):
            return to.enter_context(nc.sbuf_tensor(name, shape, dt))

        Phase.spent.clear()
        s = dict(ring=PoolRing(ctx, nc), ident=sb("ident", [P, P]), ones=sb("ones", [P, LO]), iota=sb("iota", [P, 32]), x=sb("x_nodes", [P, NODE_COLS * F]),
                 zero_tables=[tables[n] for n in ("agg0", "agg2", "agg3", "y4")], zero_rows=[t[0:1, :] for t in steps])
        s["place"] = sb("place", [P, NODE_COLS])
        orders = []
        for n in "ba":
            orders.append(dict(
                same=sb(n + "_same", [P, COLS]),
                first=sb(n + "_first", [P, COLS]), write=sb(n + "_write", [P, COLS]),
                gather=sb(n + "_gather", [P, COLS + BODY], i32), goes_on=sb(n + "_goes_on", [P, 1]),
                cross=sb(n + "_cross", [F2, P]), span=sb(n + "_span", [F2, P])))
        by_dst, by_src = orders
        weight = sb("weight", [P, COLS])
        kind = sb("kind", [P, COLS])
        by_dst.update(key=sb("b_key", [P, COLS]), other=sb("b_other", [P, COLS]))
        early = ctx.enter_context(ExitStack())
        by_src.update(key=sb("a_key", [P, COLS], fp32, early), other=sb("a_other", [P, COLS], fp32, early))
        attr = sb("attr", [P, COLS, 2], fp32, early)

        with ExitStack() as part:
            t = lambda name, shape, dt=fp32: sb(name, shape, dt, part)
            s.update(iota16=t("iota16", [P, LO], fp16), earlier16=t("earlier16", [P, P], fp16), ones16=t("ones16", [P, P], fp16),
                     rec_a=t("rec_a", [P, COLS, REC]), rec_b=t("rec_b", [P, COLS, REC]), digit_lo=t("digit_lo", [P, COLS]),
                     digit_hi=t("digit_hi", [P, COLS]), row=t("row", [P, 1]),
                     base_lo=t("base_lo", [P, LO], fp16), base_hi=t("base_hi", [P, HI], fp16))
            setup_phase(nc, d, s)
            flag = t("flag", [1, 1], i32)
            descent_phase(nc, s, flag, sorted_dst)
            sort_records(nc, s, "a", s["rec_a"], scratch, sorted_once, sorted_src)
            recycle(nc)
            unsorted = nc.values_load(flag[0:1, 0:1])
            with nc.If(unsorted != 0):
                enter_phase(nc)
                sort_records(nc, dict(s, ring=PoolRing(ctx, nc, "general")), "b", s["rec_b"], scratch, sorted_once, sorted_dst)
        order_phase(nc, s, "order_a", sorted_src, by_src, [(weight[:], 2), (attr[:], (3, 5))])
        order_phase(nc, s, "order_b", sorted_dst, by_dst, [(kind[:], 2)])

        norm_phase(nc, s, "norm0", None, tables["h0"])
        with ExitStack() as part:
            t = lambda name, shape, dt=fp32: sb(name, shape, dt, part)
            basis, msgs, wpad = t("basis", [P, COLS, BASIS * BASIS]), t("msgs0", [P, COLS, F + 1]), t("wpad0", [P, 8, 256])
            basis_phase(nc, s, attr, basis, msgs[:, :, F])
            flat_w = d["L0_gnn_weight"].rearrange("u v i o -> i (u v) o")
            pad_phase(nc, "pad0", [wpad[:]],
                      [(wpad[F * q:F * (q + 1), q, :].rearrange("p (k o) -> p k o", o=F), flat_w) for q in range(8)])
            message_phase(nc, s, "msg0", tables["h0"], F, by_src, wpad, basis, F, msgs)
            carry_phase(nc, s, "scan0", by_src, msgs, F)
            write_phase(nc, s, "write0", by_src, msgs, F + 1, tables["agg0"])
        early.close()
        norm_phase(nc, s, "norm1", tables["agg0"], tables["h1"])

        with ExitStack() as part:
            t = lambda name, shape, dt=fp32: sb(name, shape, dt, part)
            w = dict(msg=t("w_msg", [P, 2, HID]), self=t("w_self", [P, 2, HID]), agg=t("w_agg", [P, 2, HID]),
                     msg_b=t("w_msg_b", [P, 2]), self_b=t("w_self_b", [P, 2]), pre_b1=t("w_pre_b1", [P, 2]),
                     pre_w1=t("w_pre_w1", [P, 8, HID]), post_w2=t("w_post_w2", [P, 2, 8, P]), post_b2=t("w_post_b2", [P, 1]))
            fold_phase(nc, s, d, w)
            places = []
            for q in range(8):
                rows = slice(F * q, F * (q + 1))
                places.append((w["pre_w1"][rows, q, :], d["L1_gnn_pre_w1"]))
                for h in range(2):
                    places.append((w["post_w2"][:, h, q, rows], d["L1_gnn_post_w2"][h * P:(h + 1) * P, :]))
                places.append((w["post_b2"][rows, :], d["L1_gnn_post_b2"].rearrange("(p a) -> p a", a=1)))
            pad_phase(nc, "pad1", [w["pre_w1"][:], w["post_w2"][:]], places)
            node_mlp_phase(nc, s, w, tables["h1"], tables["mlp"])
            tiles = [t(f"tile_{a}", [P, COLS + BODY], i32) for a in ("src", "dst", "write")]
            tile_order_phase(nc, s, "tiles", by_dst, flats, same_flat, tiles)
            edge_mlp_phase(nc, s, w, tables["h1"], tiles, same_flat, tables["mlp"])
        norm_phase(nc, s, "norm2", tables["mlp"], tables["h2"])

        with ExitStack() as part:
            t = lambda name, shape, dt=fp32: sb(name, shape, dt, part)
            mean = t("mean_weight", [P, COLS, RELS])
            mean_weight_phase(nc, s, by_dst, kind, mean)
            with ExitStack() as half:
                msgs, wpad = sb("msgs2", [P, COLS, F2], fp32, half), sb("wpad2", [P, 8, 256], fp32, half)
                pad_phase(nc, "pad2", [wpad[:]],
                          [(wpad[F * q:F * (q + 1), q, :].rearrange("p (r o) -> p r o", o=F2),
                            d["L2_gnn_W1"].rearrange("r i o -> i r o")) for q in range(8)])
                message_phase(nc, s, "msg2", tables["h2"], F, by_dst, wpad, mean, F2, msgs)
                carry_phase(nc, s, "scan2", by_dst, msgs, F2)
                write_phase(nc, s, "write2", by_dst, msgs, F2, tables["agg2"])
            with ExitStack() as half:
                h = lambda name, shape: sb(name, shape, fp32, half)
                w = dict(root1=h("w_root1", [P, 8 * F2]), root2=h("w_root2", [P, 4 * F]), b1=h("w_b1", [1, 8 * F2]), b2=h("w_b2", [1, 4 * F]))
                row = lambda v: v.rearrange("(a f) -> a f", a=1)
                pad_phase(nc, "pad3", [w["root1"][:], w["root2"][:]],
                          [(w["root1"][F * q:F * (q + 1), F2 * q:F2 * (q + 1)], d["L2_gnn_root1"]) for q in range(8)] +
                          [(w["root2"][F2 * q:F2 * (q + 1), F * q:F * (q + 1)], d["L2_gnn_root2"]) for q in range(4)] +
                          [(w["b1"][:, F2 * q:F2 * (q + 1)], row(d["L2_gnn_b1"])) for q in range(8)] +
                          [(w["b2"][:, F * q:F * (q + 1)], row(d["L2_gnn_b2"])) for q in range(4)])
                node_relation_phase(nc, s, w, tables["h2"], tables["agg2"], tables["mid"])
            with ExitStack() as half:
                msgs, wpad = sb("msgs3", [P, COLS, F], fp32, half), sb("wpad3", [P, 4, 128], fp32, half)
                pad_phase(nc, "pad4", [wpad[:]],
                          [(wpad[F2 * q:F2 * (q + 1), q, :].rearrange("p (r o) -> p r o", o=F),
                            d["L2_gnn_W2"].rearrange("r i o -> i r o")) for q in range(4)])
                message_phase(nc, s, "msg3", tables["mid"], F2, by_dst, wpad, mean, F, msgs)
                carry_phase(nc, s, "scan3", by_dst, msgs, F)
                write_phase(nc, s, "write3", by_dst, msgs, F, tables["agg3"])
        norm_phase(nc, s, "norm3", tables["agg3"], tables["y0"])

        with ExitStack() as part:
            msgs = sb("msgs4", [P, COLS, F], fp32, part)
            places = sb("places", [P, COLS + BODY], i32, part)
            pad_phase(nc, "pad5", [places[:]], [])
            propagate_phase(nc, s, "prop0", tables["y0"], by_src["gather"], weight, by_src, msgs, places)
            carry_phase(nc, s, "carry40", by_src, msgs, F)
            for n in range(1, STEPS):
                keep_phase(nc, f"keep{n}", msgs, steps[n - 1])
                propagate_phase(nc, s, f"prop{n}", steps[n - 1], places, weight, by_src, msgs)
                carry_phase(nc, s, f"carry4{n}", by_src, msgs, F)
            write_phase(nc, s, "write4", by_src, msgs, F, tables["y4"])
        finish_phase(nc, s, tables["y4"], out)


_INS = ["x", "src", "dst", "edge_attr_2", "edge_type_8", "edge_weight", "L0_gnn_weight",
        "L1_gnn_pre_w1", "L1_gnn_pre_b1", "L1_gnn_pre_w2", "L1_gnn_pre_b2", "L1_gnn_conv_w", "L1_gnn_conv_b",
        "L1_gnn_post_w1", "L1_gnn_post_b1", "L1_gnn_post_w2", "L1_gnn_post_b2",
        "L2_gnn_W1", "L2_gnn_root1", "L2_gnn_b1", "L2_gnn_W2", "L2_gnn_root2", "L2_gnn_b2"]


def kernel(**inputs):
    import numpy as _np
    import concourse.bacc as _bacc
    from concourse.bass_utils import run_bass_kernel_spmd as _run

    nc = _bacc.Bacc("TRN2", target_bir_lowering=False, num_devices=1)
    arrays, d = {}, {}
    for name in _INS:
        a = _np.ascontiguousarray(inputs[name])
        arrays[f"in_{name}"] = a
        d[name] = nc.dram_tensor(f"in_{name}", a.shape, mybir.dt.from_np(a.dtype), kind="ExternalInput").ap()
    out = nc.dram_tensor("out_x", (NODES, F), fp32, kind="ExternalOutput").ap()
    graph_kernel(nc, d, out)
    r = _run(nc, [arrays], core_ids=[0])
    return r.results[0]["out_x"]
```

```python
from contextlib import ExitStack

import concourse.bass as bass
from concourse import mybir

P = 128
NODES, EDGES, F, F2, HID, RELS, BASIS, STEPS = 100000, 50000, 16, 32, 256, 8, 4, 4
NODE_PARTS = 125
NODE_COLS = NODES // NODE_PARTS
COLS = 392
SLOTS = COLS * P
GROUP, RING = 8, 7
BODY = GROUP * RING
TURNS = COLS // BODY
FULL_PARTS = EDGES // COLS
REST = EDGES - FULL_PARTS * COLS
REC = 8
LO_BITS = 9
LO, HI = 1 << LO_BITS, 256
PAD_KEY = 196 << LO_BITS
SKIP = 1000000
CHUNK = 28
CG, CS = 4, 7
NCHUNK = 32
NG, NS = 4, 8
EPS = 1e-5

fp32, fp16, bf16, i32 = mybir.dt.float32, mybir.dt.float16, mybir.dt.bfloat16, mybir.dt.int32
ALU = mybir.AluOpType
ACT = mybir.ActivationFunctionType
AX = mybir.AxisListType.X


class Chain:

    def __init__(self, eng, sem, turn=None, per_turn=0, before=0):
        self.eng, self.sem, self.n = eng, sem, before
        self.turn, self.per_turn = turn, per_turn

    def do(self, ins):
        ins.then_inc(self.sem, 1)
        self.n += 1
        return self

    def sync(self):
        base = 0 if self.turn is None else self.turn * self.per_turn
        self.eng.wait_ge(self.sem, base + self.n)


class Phase:

    spent = []
    MOST = 32

    def __init__(self, nc, name):
        self.nc, self.name, self.ctx, self.own = nc, name, ExitStack(), []
        if nc.free_len() - len(Phase.spent) < Phase.MOST:
            recycle(nc)

    def __enter__(self):
        return self

    def __exit__(self, *a):
        Phase.spent += self.own
        return self.ctx.__exit__(*a)

    def sb(self, name, shape, dt=fp32):
        return self.ctx.enter_context(self.nc.sbuf_tensor(f"{self.name}_{name}", shape, dt))

    def ps(self, name, shape, dt=fp32):
        return self.ctx.enter_context(self.nc.psum_tensor(f"{self.name}_{name}", shape, dt))

    def sem(self, name):
        sem = self.ctx.enter_context(self.nc.semaphore(f"{self.name}_{name}"))
        self.own.append(sem.num)
        return sem

    def block(self):
        return self.ctx.enter_context(self.nc.Block())


def recycle(nc):
    nums = sorted(Phase.spent)
    Phase.spent.clear()
    with nc.Block() as block:
        @block.sync
        def _(sp):
            first = 0
            for n in range(1, len(nums) + 1):
                if n == len(nums) or nums[n] != nums[n - 1] + 1:
                    sp.sem_clear(range(nums[first], nums[n - 1] + 1))
                    first = n


class PoolRing:

    def __init__(self, ctx, nc, name="all"):
        self.sems = [ctx.enter_context(nc.semaphore(f"pool_dma_{name}{g}")) for g in range(RING)]
        self.before = [0] * RING

    def done(self, eng, slot, count):
        eng.wait_ge(self.sems[slot], self.before[slot] + count)

    def end_phase(self, slots, count):
        for g in slots:
            self.before[g] += count


def node_rows(dram):
    return dram.rearrange("(p j) f -> p (j f)", p=NODE_PARTS)


def node_dma(eng, out, in_, sem):
    eng.dma_start(out[0:112], in_[0:112]).then_inc(sem, 16)
    eng.dma_start(out[112:NODE_PARTS], in_[112:NODE_PARTS]).then_inc(sem, 16)


def turns(eng, body, count=TURNS):
    body(0, True)
    with eng.Fori(1, count) as t:
        body(t, False)


class NormSteps:

    def __init__(self, ph, nc, s, piece, add_table, out_table):
        N = NODE_PARTS
        self.nc, self.s, self.piece = nc, s, piece
        self.src = add_table
        self.dst = node_rows(out_table)
        self.wide = F if add_table is None else add_table.shape[1]
        if add_table is not None:
            self.more = ph.sb("norm_add", [N, piece * self.wide])
        self.h, self.cent, self.square = (ph.sb("norm_" + n, [N, piece * F]) for n in ("h", "cent", "square"))
        self.mean, self.var, self.inv, self.root, self.newton = (
            ph.sb("norm_" + n, [N, piece]) for n in ("mean", "var", "inv", "root", "newton"))
        self.landed, self.used, self.own, self.centred, self.squared, self.varied, self.rooted, self.done, self.stored, self.tick = (
            ph.sem("norm_" + n) for n in ("landed", "used", "own", "centred", "squared", "varied", "rooted", "done", "stored", "tick"))

    def load(self, sp, i):
        w = self.piece * self.wide
        wait(sp, self.used, i)
        node_dma(sp, self.more[:], node_rows(self.src)[:, bass.ds(i * w, w)], self.landed)

    def store(self, sp, i):
        w = self.piece * F
        sp.wait_ge(self.done, i + 1)
        node_dma(sp, self.dst[:, bass.ds(i * w, w)], self.h[:], self.stored)

    def dve(self, dve, i):
        nc, piece, OWN = self.nc, self.piece, 7
        x = self.s["x"][0:NODE_PARTS, bass.ds(i * (piece * F), piece * F)]
        by_node = lambda ap: ap.rearrange("p (n f) -> p n f", f=F)
        spread = lambda ap: ap.unsqueeze(2).to_broadcast([NODE_PARTS, piece, F])

        def own(n, make):
            wait(dve, self.own, OWN * i + n)
            make().then_inc(self.own, 1)

        def add():
            if self.src is not None:
                dve.wait_ge(self.landed, 32 * (i + 1))
                more = self.more[:].rearrange("p (n f) -> p n f", f=self.wide)
                if self.wide > F:
                    nc.vector.tensor_copy(self.s["place"][0:NODE_PARTS, bass.ds(i * piece, piece)], more[:, :, F])
                nc.vector.tensor_tensor(by_node(x), by_node(x), more[:, :, 0:F], ALU.add).then_inc(self.used, 1)

        def total():
            if self.src is not None:
                dve.wait_ge(self.used, i + 1)
            wait(dve, self.own, OWN * i)
            dve.sem_inc(self.tick, 1)
            nc.vector.tensor_reduce(self.mean[:], by_node(x), AX, ALU.add).then_inc(self.own, 1)

        def centre():
            dve.wait_ge(self.own, OWN * i + 2)
            wait(dve, self.done, i)
            nc.vector.tensor_tensor(by_node(self.cent[:]), by_node(x), spread(self.mean[:]), ALU.subtract).then_inc(self.centred, 1)

        def variance():
            dve.wait_ge(self.squared, i + 1)
            own(2, lambda: nc.vector.tensor_reduce(self.var[:], by_node(self.square[:]), AX, ALU.add))

        def with_eps():
            dve.wait_ge(self.own, OWN * i + 3)
            nc.vector.tensor_scalar(self.var[:], self.var[:], 1.0 / F, EPS, ALU.mult, ALU.add).then_inc(self.varied, 1)

        def invert():
            dve.wait_ge(self.rooted, i + 1)
            own(3, lambda: nc.vector.reciprocal(self.inv[:], self.root[:]))

        def finish():
            dve.wait_ge(self.own, OWN * i + 7)
            wait(dve, self.stored, 32 * i)
            nc.vector.scalar_tensor_tensor(out=by_node(self.h[:]), in0=by_node(self.cent[:]), scalar=0.0,
                                           in1=spread(self.inv[:]), op0=ALU.max, op1=ALU.mult).then_inc(self.done, 1)

        def last_newton():
            own(6, lambda: nc.vector.scalar_tensor_tensor(out=self.inv[:], in0=self.newton[:], scalar=1.5, in1=self.inv[:],
                                                          op0=ALU.add, op1=ALU.mult))

        return [add, total, lambda: own(1, lambda: nc.vector.tensor_scalar(self.mean[:], self.mean[:], 1.0 / F, None, ALU.mult)),
                centre, variance, with_eps, invert,
                lambda: own(4, lambda: nc.vector.tensor_tensor(self.newton[:], self.inv[:], self.inv[:], ALU.mult)),
                lambda: own(5, lambda: nc.vector.scalar_tensor_tensor(out=self.newton[:], in0=self.newton[:], scalar=-0.5,
                                                                      in1=self.var[:], op0=ALU.mult, op1=ALU.mult)),
                last_newton, finish]

    def act(self, act, i):
        nc = self.nc

        def square():
            act.wait_ge(self.centred, i + 1)
            wait(act, self.varied, i)
            nc.scalar.activation(self.square[:], self.cent[:], ACT.Square).then_inc(self.squared, 1)

        def root():
            act.wait_ge(self.varied, i + 1)
            nc.scalar.activation(self.root[:], self.var[:], ACT.Sqrt).then_inc(self.rooted, 1)

        return [square, root]


def wait(eng, sem, value):
    if not isinstance(value, int) or value > 0:
        eng.wait_ge(sem, value)


def setup_phase(nc, d, s):
    with Phase(nc, "su") as ph:
        keys = {n: ph.sb(n, [P, COLS], i32) for n in ("src", "dst", "typ")}
        wts = ph.sb("wts", [P, COLS])
        attr = ph.sb("attr", [P, COLS, 2])
        iota_i = ph.sb("iota_i", [P, LO], i32)
        row_i = ph.sb("row_i", [P, 1], i32)
        tri = ph.sb("tri", [P, P])
        filled, loaded, masked = ph.sem("filled"), ph.sem("loaded"), ph.sem("masked")
        own, vown = ph.sem("own"), ph.sem("vown")
        block = ph.block()

        @block.gpsimd
        def _(pool):
            nc.gpsimd.memset(s["ident"][:], 0.0).then_inc(own, 1)
            nc.gpsimd.memset(tri[:], 1.0).then_inc(own, 1)
            nc.gpsimd.iota(iota_i[:], pattern=[[1, LO]], base=0, channel_multiplier=0).then_inc(masked, 1)
            nc.gpsimd.iota(row_i[:], pattern=[[0, 1]], base=0, channel_multiplier=1).then_inc(masked, 1)
            pool.wait_ge(own, 2)
            nc.gpsimd.affine_select(out=s["ident"][:], in_=s["ident"][:], compare_op=ALU.not_equal, fill=1.0,
                                    base=0, pattern=[[-1, P]], channel_multiplier=1).then_inc(masked, 1)
            nc.gpsimd.affine_select(out=tri[:], in_=tri[:], compare_op=ALU.is_gt, fill=0.0,
                                    base=0, pattern=[[1, P]], channel_multiplier=-1).then_inc(masked, 1)

        @block.vector
        def _(dve):
            nc.vector.memset(keys["src"][:], PAD_KEY).then_inc(filled, 1)
            nc.vector.memset(keys["dst"][:], PAD_KEY).then_inc(filled, 1)
            nc.vector.memset(keys["typ"][:], 0).then_inc(filled, 1)
            nc.vector.memset(wts[:], 0.0).then_inc(filled, 1)
            nc.vector.memset(attr[:], 0.0).then_inc(filled, 1)
            c = Chain(dve, vown)
            c.do(nc.vector.memset(s["zero"][:], 0.0))
            c.do(nc.vector.memset(s["rec_a"][:], 0.0))
            c.do(nc.vector.memset(s["rec_b"][:], 0.0))
            c.do(nc.vector.memset(s["ones16"][:], 1.0))
            c.do(nc.vector.memset(s["ones"][:], 1.0))
            dve.wait_ge(masked, 4)
            nc.vector.tensor_copy(s["row"][:], row_i[:])
            nc.vector.tensor_copy(s["ident16"][:], s["ident"][:])
            nc.vector.tensor_copy(s["iota"][:], iota_i[:, 0:32])
            nc.vector.tensor_copy(s["iota16"][:], iota_i[:])
            nc.vector.tensor_copy(s["earlier16"][:], tri[:])
            dve.wait_ge(loaded, 16 * 12)
            c.sync()
            for rec, key, other in (("rec_a", "src", "dst"), ("rec_b", "dst", "src")):
                nc.vector.tensor_copy(s[rec][:, :, 0], keys[key][:])
                nc.vector.tensor_scalar(s[rec][:, :, 1], keys[other][:], float(NODES - 1), None, ALU.min)
            nc.vector.tensor_copy(s["rec_a"][:, :, 2], wts[:])
            nc.vector.tensor_copy(s["rec_a"][:, :, 3:5], attr[:])
            nc.vector.tensor_copy(s["rec_b"][:, :, 2], keys["typ"][:])

        @block.sync
        def _(sp):
            sp.wait_ge(filled, 5)
            full = FULL_PARTS * COLS
            for tile, dram in ((keys["src"], d["src"]), (keys["dst"], d["dst"]), (keys["typ"], d["edge_type_8"]),
                               (wts, d["edge_weight"])):
                sp.dma_start(tile[0:FULL_PARTS, :], dram[0:full].rearrange("(p j) -> p j", j=COLS)).then_inc(loaded, 16)
                sp.dma_start(tile[FULL_PARTS:FULL_PARTS + 1, 0:REST],
                             dram[full:EDGES].rearrange("(p j) -> p j", p=1)).then_inc(loaded, 16)
            ea = d["edge_attr_2"]
            sp.dma_start(attr[0:FULL_PARTS, :, :], ea[0:full, :].rearrange("(p j) w -> p j w", j=COLS)).then_inc(loaded, 16)
            sp.dma_start(attr[FULL_PARTS:FULL_PARTS + 1, 0:REST, :],
                         ea[full:EDGES, :].rearrange("(p j) w -> p j w", p=1)).then_inc(loaded, 16)
            x_rows = node_rows(d["x"])
            node_dma(sp, s["x"][0:NODE_PARTS, :], x_rows, loaded)
            sp.wait_ge(loaded, 16 * 12)


def descent_phase(nc, s, flag, sorted_dst):
    with Phase(nc, "desc") as ph:
        after = ph.sb("after", [P, REC])
        falls = ph.sb("falls", [P, COLS])
        any_fall = ph.sb("any_fall", [P, 1])
        any16 = ph.sb("any16", [P, 1], fp16)
        total_ps = ph.ps("total_ps", [P, 8])
        padded, loaded, stored, own, found, counted = (ph.sem(n) for n in ("padded", "loaded", "stored", "own", "found", "counted"))
        block = ph.block()
        key = s["rec_b"][:, :, 0]

        @block.sync
        def _(sp):
            rows = sorted_dst.rearrange("(p j) w -> p j w", j=COLS)
            sp.dma_start(rows, s["rec_b"][:]).then_inc(stored, 16)
            sp.wait_ge(stored, 16)
            sp.wait_ge(padded, 1)
            sp.dma_start(after[0:P - 1, :], rows[1:P, 0, :]).then_inc(loaded, 16)

        @block.vector
        def _(dve):
            nc.vector.memset(after[:], PAD_KEY).then_inc(padded, 1)
            dve.wait_ge(loaded, 16)
            c = Chain(dve, own)
            c.do(nc.vector.tensor_tensor(falls[:, 0:COLS - 1], key[:, 0:COLS - 1], key[:, 1:COLS], ALU.is_gt))
            c.do(nc.vector.tensor_tensor(falls[:, COLS - 1:COLS], key[:, COLS - 1:COLS], after[:, 0:1], ALU.is_gt))
            c.sync()
            c.do(nc.vector.tensor_reduce(any_fall[:], falls[:], AX, ALU.max))
            c.sync()
            nc.vector.tensor_copy(any16[:], any_fall[:]).then_inc(found, 1)
            dve.wait_ge(counted, 1)
            c.do(nc.vector.tensor_copy(flag[:], total_ps[0:1, 0:1]))
            c.sync()

        @block.tensor
        def _(pe):
            pe.wait_ge(found, 1)
            nc.tensor.matmul(total_ps[:, 0:1], s["ones16"][:], any16[:], start=True, stop=True).then_inc(counted, 1)


def histogram_phase(nc, s, name, rec, scratch):
    with Phase(nc, name) as ph:
        ki = ph.sb("ki", [P, COLS], i32)
        digit = {"lo": ph.sb("lo", [P, COLS], i32), "hi": ph.sb("hi", [P, COLS], i32)}
        part = {n: ph.sb(n, [P, COLS], i32) for n in ("lo_a", "lo_b", "hi_a", "hi_b")}
        width = {"lo_a": 16, "lo_b": 32, "hi_a": 16, "hi_b": 16}
        hot = {n: ph.sb(n + "_hot", [P, BODY, w], fp16) for n, w in width.items()}
        zero16 = ph.sb("zero16", [P, 32], fp16)
        count_ps = {n: ph.ps(n + "_count", [16, 512]) for n in ("lo", "hi")}
        count = {"lo": ph.sb("count_lo", [16, 32]), "hi": ph.sb("count_hi", [16, 16])}
        flat = {"lo": ph.sb("flat_lo", [P, LO]), "hi": ph.sb("flat_hi", [P, HI])}
        start = ph.sb("start", [P, LO])
        start_i = ph.sb("start_i", [P, LO], i32)
        each_i = ph.sb("each_i", [P, LO], i32)
        over_i = ph.sb("over_i", [P, LO], i32)
        hot_built, hot_used, counted, flattened = ph.sem("hot_built"), ph.sem("hot_used"), ph.sem("counted"), ph.sem("flattened")
        own, taken, peown = ph.sem("own"), ph.sem("taken"), ph.sem("peown")
        split = {"lo": 32, "hi": 16}
        block = ph.block()

        @block.vector
        def _(dve):
            c = Chain(dve, own)
            c.do(nc.vector.tensor_copy(ki[:], rec[:, :, 0]))
            c.do(nc.vector.memset(zero16[:], 0.0))
            c.sync()
            c.do(nc.vector.tensor_scalar(digit["lo"][:], ki[:], LO - 1, None, ALU.bitwise_and))
            c.do(nc.vector.tensor_scalar(digit["hi"][:], ki[:], LO_BITS, None, ALU.logical_shift_right))
            c.sync()
            nc.vector.tensor_scalar(s["minus_lo"][:], digit["lo"][:], -1.0, None, ALU.mult)
            nc.vector.tensor_scalar(s["minus_hi"][:], digit["hi"][:], -1.0, None, ALU.mult)
            c.do(nc.vector.tensor_scalar(part["lo_a"][:], digit["lo"][:], 5, None, ALU.logical_shift_right))
            c.do(nc.vector.tensor_scalar(part["lo_b"][:], digit["lo"][:], 31, None, ALU.bitwise_and))
            c.do(nc.vector.tensor_scalar(part["hi_a"][:], digit["hi"][:], 4, None, ALU.logical_shift_right))
            c.do(nc.vector.tensor_scalar(part["hi_b"][:], digit["hi"][:], 15, None, ALU.bitwise_and))
            c.sync()

            def build(t, first):
                if not first:
                    dve.wait_ge(hot_used, t)
                for n, w in width.items():
                    nc.vector.tensor_tensor(
                        hot[n][:, :, :], s["iota"][:, 0:w].unsqueeze(1).to_broadcast([P, BODY, w]),
                        part[n][:, bass.ds(t * BODY, BODY)].unsqueeze(2).to_broadcast([P, BODY, w]),
                        ALU.is_equal).then_inc(hot_built, 1)

            turns(dve, build)
            dve.wait_ge(counted, 1)
            nc.vector.tensor_copy(count["lo"][:], count_ps["lo"][:, 0:32]).then_inc(taken, 1)
            nc.vector.tensor_copy(count["hi"][:], count_ps["hi"][:, 0:16]).then_inc(taken, 1)
            dve.wait_ge(flattened, 32)
            for n, base in (("lo", s["base_lo"]), ("hi", s["base_hi"])):
                w = flat[n].shape[1]
                c.do(nc.vector.tensor_tensor_scan(start[:, 0:w], s["ones"][:, 0:w], flat[n][:], 0.0, ALU.mult, ALU.add))
                c.sync()
                c.do(nc.vector.tensor_tensor(start_i[:, 0:w], start[:, 0:w], flat[n][:], ALU.subtract))
                c.sync()
                c.do(nc.vector.tensor_scalar(each_i[:, 0:w], start_i[:, 0:w], 7, None, ALU.logical_shift_right))
                c.do(nc.vector.tensor_scalar(over_i[:, 0:w], start_i[:, 0:w], P - 1, None, ALU.bitwise_and))
                c.sync()
                c.do(nc.vector.scalar_tensor_tensor(out=base[:], in0=over_i[:, 0:w], scalar=s["row"][:, 0:1],
                                                    in1=each_i[:, 0:w], op0=ALU.is_gt, op1=ALU.add))
                c.sync()

        @block.tensor
        def _(pe):
            pe.wait_ge(own, 2)
            for n in ("lo", "hi"):
                nc.tensor.matmul(count_ps[n][:, 0:split[n]], zero16[:, 0:16], zero16[:, 0:split[n]],
                                 start=True, stop=False)

            def add(t, first):
                pe.wait_ge(hot_built, 4 * t + 4)
                for k in range(BODY):
                    nc.tensor.matmul(count_ps["lo"][:, 0:32], hot["lo_a"][:, k, :], hot["lo_b"][:, k, :],
                                     start=False, stop=False)
                    last = nc.tensor.matmul(count_ps["hi"][:, 0:16], hot["hi_a"][:, k, :], hot["hi_b"][:, k, :],
                                            start=False, stop=False)
                last.then_inc(hot_used, 1)

            turns(pe, add)
            for n in ("lo", "hi"):
                last = nc.tensor.matmul(count_ps[n][:, 0:split[n]], zero16[:, 0:16], zero16[:, 0:split[n]],
                                        start=False, stop=True)
            last.then_inc(counted, 1)

        @block.sync
        def _(sp):
            sp.wait_ge(taken, 2)
            sp.dma_start(scratch["lo"].rearrange("(a b) -> a b", a=16), count["lo"][:]).then_inc(peown, 16)
            sp.dma_start(scratch["hi"].rearrange("(a b) -> a b", a=16), count["hi"][:]).then_inc(peown, 16)
            sp.wait_ge(peown, 32)
            sp.dma_start(flat["lo"][:], scratch["lo"].partition_broadcast(P)).then_inc(flattened, 16)
            sp.dma_start(flat["hi"][:], scratch["hi"].partition_broadcast(P)).then_inc(flattened, 16)
            sp.wait_ge(flattened, 32)


def zero_tables(sp, s, zeroed):
    n = 0
    for table in s["zero_tables"]:
        rows = node_rows(table)
        piece = 3200 if rows.shape[1] % 3200 == 0 else 3400
        for a in range(0, rows.shape[1], piece):
            node_dma(sp, rows[:, a:a + piece], s["zero"][0:NODE_PARTS, 0:piece], zeroed)
            n += 32
    for row in s["zero_rows"]:
        sp.dma_start(row, s["zero"][0:1, 0:row.shape[1]]).then_inc(zeroed, 16)
        n += 16
    sp.wait_ge(zeroed, n)


def sort_pass(nc, s, name, rec, minus_digit, base, buckets, out, first, aside=None, normed=None):
    NO, SHARE, NJ = 8, 4, 4
    with Phase(nc, name) as ph:
        hot = ph.sb("hot", [P, NO, buckets], fp16)
        away = ph.sb("away", [P, 2, buckets], fp16)
        seen = ph.sb("seen", [P, NO, buckets], fp16)
        junk = ph.sb("junk", [P, NJ, buckets])
        digit = ph.sb("digit", [P, COLS // SHARE])
        rank = ph.sb("rank", [P, RING, GROUP])
        rank_i = ph.sb("rank_i", [P, GROUP], i32)
        row_i = ph.sb("row_i", [P, GROUP], i32)
        col_i = ph.sb("col_i", [P, GROUP], i32)
        place = ph.sb("place", [P, RING, GROUP], i32)
        data = ph.sb("data", [P, RING, GROUP * REC])
        sums = ph.ps("sums", [P, NO, 512])
        hot_by_act, hot_by_dve, seen_added = ph.sem("hot_by_act"), ph.sem("hot_by_dve"), ph.sem("seen_added")
        summed, rank_read = ph.sem("summed"), ph.sem("rank_read")
        away_ok, made = ph.sem("away_ok"), ph.sem("made")
        placed, staged, turn_sem, own = ph.sem("placed"), ph.sem("staged"), ph.sem("turn"), ph.sem("own")
        ring = s["ring"]
        LAG = 3
        OWN = RING * 3 if first else 0
        DVE_AT = (0, 4, 8, 12, 28, 30, 42, 44, 46, 48, 50)
        ACT_AT = (24, 40)
        norm = None if normed is None else NormSteps(ph, nc, s, NODE_COLS // (TURNS + 1), None, normed)
        block = ph.block()

        def wait_hot(eng, t, k):
            if k % SHARE == SHARE - 1:
                eng.wait_ge(hot_by_dve, t * (BODY // SHARE) + k // SHARE + 1)
            else:
                eng.wait_ge(hot_by_act, t * (BODY // SHARE * (SHARE - 1)) + k // SHARE * (SHARE - 1) + k % SHARE + 1)

        @block.vector
        def _(dve):
            nc.vector.tensor_scalar(digit[:], minus_digit[:].rearrange("p (n f) -> p n f", f=SHARE)[:, :, SHARE - 1], -1.0, None,
                                    ALU.mult).then_inc(made, 1)
            nc.vector.tensor_copy(seen[:, 0, :], base[:]).then_inc(seen_added, 1)
            dve.wait_ge(made, 1)
            if norm:
                for step in norm.dve(dve, 0):
                    step()

            def rank_columns(t, first_turn):
                c, todo = Chain(dve, own, t, OWN), []
                steps = dict(zip(DVE_AT, norm.dve(dve, t + 1))) if norm else {}
                for k in range(BODY + LAG):
                    if k < BODY:
                        b = k % NO
                        if k >= NO or not first_turn:
                            dve.wait_ge(summed, t * BODY + k - NO + 1)
                        if k % SHARE == SHARE - 1:
                            nc.vector.tensor_scalar(hot[:, b, :], s["iota16"][:, 0:buckets],
                                                    digit[:, bass.ds(t * (BODY // SHARE) + k // SHARE, 1)], None,
                                                    ALU.is_equal).then_inc(hot_by_dve, 1)
                        wait_hot(dve, t, k)
                        dve.wait_ge(seen_added, t * BODY + k + 1)
                        nc.vector.tensor_tensor(seen[:, (b + 1) % NO, :], seen[:, b, :], hot[:, b, :],
                                                ALU.add).then_inc(seen_added, 1)
                    if k in steps:
                        steps[k]()
                    if k >= LAG:
                        j = k - LAG
                        g, m = j // GROUP, j % GROUP
                        dve.wait_ge(summed, t * BODY + j + 1)
                        if j >= NJ or not first_turn:
                            dve.wait_ge(rank_read, t * BODY + j - NJ + 1)
                        nc.vector.tensor_tensor_reduce(
                            out=junk[:, j % NJ, :], in0=hot[:, j % NO, :], in1=sums[:, j % NO, 0:buckets], scale=1.0, scalar=0.0,
                            op0=ALU.mult, op1=ALU.add, accum_out=rank[:, g, m:m + 1]).then_inc(rank_read, 1)
                        if todo:
                            todo.pop(0)()
                        if m == GROUP - 1:
                            todo = index_steps(c, t, g, j, first_turn)
                for step in todo:
                    step()

            def index_steps(c, t, g, j, first_turn):
                def whole():
                    if not first_turn:
                        ring.done(dve, g, 16 * GROUP * t)
                    dve.wait_ge(rank_read, t * BODY + j + 1)
                    if first:
                        c.do(nc.vector.tensor_copy(rank_i[:], rank[:, g, :]))
                    else:
                        nc.vector.tensor_copy(place[:, g, :], rank[:, g, :]).then_inc(placed, 1)

                def cut():
                    c.sync()
                    c.do(nc.vector.tensor_scalar(row_i[:], rank_i[:], P - 1, None, ALU.bitwise_and))
                    c.do(nc.vector.tensor_scalar(col_i[:], rank_i[:], 7, None, ALU.logical_shift_right))

                def join():
                    c.sync()
                    nc.vector.scalar_tensor_tensor(out=place[:, g, :], in0=row_i[:], scalar=float(COLS),
                                                   in1=col_i[:], op0=ALU.mult, op1=ALU.add).then_inc(placed, 1)

                return [whole, cut, join] if first else [whole]

            turns(dve, rank_columns)

        @block.tensor
        def _(pe):
            def sum_columns(t, first_turn):
                for k in range(BODY):
                    b = k % NO
                    if k >= NO or not first_turn:
                        pe.wait_ge(rank_read, t * BODY + k - NO + 1)
                    pe.wait_ge(seen_added, t * BODY + k + 1)
                    wait_hot(pe, t, k)
                    dst = sums[:, b, 0:buckets]
                    nc.tensor.matmul(dst, s["ones16"][:], seen[:, b, :], start=True, stop=False)
                    nc.tensor.matmul(dst, s["earlier16"][:], hot[:, b, :], start=False, stop=True).then_inc(summed, 1)

            turns(pe, sum_columns)

        @block.scalar
        def _(act):
            mine = [k for k in range(BODY) if k % SHARE < SHARE - 1]

            if norm:
                for step in norm.act(act, 0):
                    step()

            def columns(t, first_turn):
                steps = dict(zip(ACT_AT, norm.act(act, t + 1))) if norm else {}

                def distance(n):
                    if n >= 2:
                        act.wait_ge(hot_by_act, t * len(mine) + n - 1)
                    elif not first_turn:
                        act.wait_ge(hot_by_act, t * len(mine))
                    nc.scalar.activation(away[:, n % 2, :], s["iota16"][:, 0:buckets], ACT.Abs,
                                         bias=minus_digit[:, bass.ds(t * BODY + mine[n], 1)]).then_inc(away_ok, 1)

                distance(0)
                for n, k in enumerate(mine):
                    if k in steps:
                        steps[k]()
                    g = k // GROUP
                    if k % GROUP == 0:
                        if not first_turn:
                            ring.done(act, g, 16 * GROUP * t)
                        nc.scalar.copy(data[:, g, :].rearrange("p (k w) -> p k w", w=REC),
                                       rec[:, bass.ds(t * BODY + g * GROUP, GROUP), :]).then_inc(staged, 1)
                    if n + 1 < len(mine):
                        distance(n + 1)
                    if k >= NO or not first_turn:
                        act.wait_ge(rank_read, t * BODY + k - NO + 1)
                    act.wait_ge(away_ok, t * len(mine) + n + 1)
                    nc.scalar.activation(hot[:, k % NO, :], away[:, n % 2, :], ACT.Relu, bias=s["ones"][:, 0:1],
                                         scale=-1.0).then_inc(hot_by_act, 1)

            turns(act, columns)

        if aside is not None:
            @block.sync
            def _(sp):
                aside(sp)

        if norm:
            @block.sync
            def _(sp):
                norm.store(sp, 0)
                turns(sp, lambda t, first: norm.store(sp, t + 1))
                sp.wait_ge(norm.stored, 32 * (TURNS + 1))

        @block.gpsimd
        def _(pool):
            def move(t, first_turn):
                for g in range(RING):
                    pool.wait_ge(placed, RING * t + g + 1)
                    pool.sem_inc(turn_sem, 1)
                    pool.wait_ge(staged, RING * t + g + 1)
                    pool.sem_inc(turn_sem, 1)
                    for k in range(GROUP):
                        pool.indirect_dma_start(
                            out=out, out_offset=bass.IndirectOffsetOnAxis(ap=place[:, g, k:k + 1], axis=0),
                            in_=data[:, g, k * REC:(k + 1) * REC], in_offset=None).then_inc(ring.sems[g], 16)

            turns(pool, move)
            for g in range(RING):
                ring.done(pool, g, 16 * GROUP * TURNS)
    s["ring"].end_phase(range(RING), 16 * GROUP * TURNS)


def reload_phase(nc, s, name, rec, table):
    with Phase(nc, name) as ph:
        loaded, own = ph.sem("loaded"), ph.sem("own")
        ki = ph.sb("ki", [P, COLS], i32)
        block = ph.block()

        @block.sync
        def _(sp):
            sp.dma_start(rec[:], table.rearrange("(p j) w -> p j w", j=COLS)).then_inc(loaded, 16)

        @block.vector
        def _(dve):
            dve.wait_ge(loaded, 16)
            c = Chain(dve, own)
            c.do(nc.vector.tensor_copy(ki[:], rec[:, :, 0]))
            c.sync()
            c.do(nc.vector.tensor_scalar(ki[:], ki[:], LO_BITS, None, ALU.logical_shift_right))
            c.sync()
            c.do(nc.vector.tensor_scalar(s["minus_hi"][:], ki[:], -1.0, None, ALU.mult))
            c.sync()


def enter_phase(nc):
    with Phase(nc, "enter") as ph:
        entered = ph.sem("entered")
        block = ph.block()

        @block.sync
        def _(sp):
            sp.sem_inc(entered, 1)

        @block.gpsimd
        def _(pool):
            pool.wait_ge(entered, 1)

        @block.scalar
        def _(act):
            act.wait_ge(entered, 1)

        @block.vector
        def _(dve):
            dve.wait_ge(entered, 1)

        @block.tensor
        def _(pe):
            pe.wait_ge(entered, 1)


def sort_records(nc, s, n, rec, scratch, halfway, out, aside=None, normed=None):
    histogram_phase(nc, s, "hist_" + n, rec, scratch)
    sort_pass(nc, s, "low_" + n, rec, s["minus_lo"], s["base_lo"], LO, halfway, True, aside)
    reload_phase(nc, s, "reload_" + n, rec, halfway)
    sort_pass(nc, s, "high_" + n, rec, s["minus_hi"], s["base_hi"], HI, out, False, normed=normed)


def order_phase(nc, s, name, table, o, payload):
    with Phase(nc, name) as ph:
        rec = ph.sb("rec", [P, COLS, REC])
        before, after = ph.sb("before", [P, REC]), ph.sb("after", [P, REC])
        key = o["key"]
        open_ = ph.sb("open", [P, COLS])
        flag = ph.sb("flag", [P, 2, F2])
        flag_ps = ph.ps("flag_ps", [F2, 2, P])
        cleared, loaded, own, flags, turned = (ph.sem(n) for n in ("cleared", "loaded", "own", "flags", "turned"))
        block = ph.block()
        rows = table.rearrange("(p j) w -> p j w", j=COLS)

        @block.sync
        def _(sp):
            sp.dma_start(rec[:], rows).then_inc(loaded, 16)
            sp.wait_ge(cleared, 2)
            sp.dma_start(before[1:P, :], rows[0:P - 1, COLS - 1, :]).then_inc(loaded, 16)
            sp.dma_start(after[0:P - 1, :], rows[1:P, 0, :]).then_inc(loaded, 16)

        @block.vector
        def _(dve):
            nc.vector.memset(before[:], -1.0).then_inc(cleared, 1)
            nc.vector.memset(after[:], -1.0).then_inc(cleared, 1)
            dve.wait_ge(loaded, 48)
            c = Chain(dve, own)
            c.do(nc.vector.memset(o["gather"][:, COLS:], 0))
            c.do(nc.vector.tensor_copy(key[:], rec[:, :, 0]))
            c.do(nc.vector.memset(o["same"][:, 0:1], 0.0))
            c.do(nc.vector.tensor_copy(o["other"][:], rec[:, :, 1]))
            for dst, field in payload:
                c.do(nc.vector.tensor_copy(dst, rec[:, :, field] if isinstance(field, int) else rec[:, :, field[0]:field[1]]))
            c.sync()
            c.do(nc.vector.tensor_copy(o["gather"][:, 0:COLS], o["other"][:]))
            c.do(nc.vector.tensor_tensor(o["same"][:, 1:COLS], key[:, 1:COLS], key[:, 0:COLS - 1], ALU.is_equal))
            c.do(nc.vector.tensor_tensor(open_[:, 0:COLS - 1], key[:, 0:COLS - 1], key[:, 1:COLS], ALU.is_equal))
            c.do(nc.vector.tensor_tensor(open_[:, COLS - 1:COLS], key[:, COLS - 1:COLS], after[:, 0:1], ALU.is_equal))
            c.do(nc.vector.tensor_scalar(o["first"][:], key[:], key[:, 0:1], None, ALU.is_equal))
            c.do(nc.vector.tensor_tensor(o["goes_on"][:], key[:, 0:1], before[:, 0:1], ALU.is_equal))
            c.sync()
            c.do(nc.vector.scalar_tensor_tensor(out=o["write"][:], in0=open_[:], scalar=float(SKIP), in1=key[:],
                                                op0=ALU.mult, op1=ALU.add))
            c.do(nc.vector.tensor_copy(flag[:, 0, :], o["goes_on"][:].to_broadcast([P, F2])))
            c.do(nc.vector.tensor_copy(flag[:, 1, :], o["first"][:, COLS - 1:COLS].to_broadcast([P, F2])))
            c.sync()
            dve.sem_inc(flags, 1)
            dve.wait_ge(turned, 1)
            c.do(nc.vector.tensor_copy(o["cross"][:], flag_ps[:, 0, :]))
            c.do(nc.vector.tensor_copy(o["span"][:], flag_ps[:, 1, :]))
            c.sync()

        @block.tensor
        def _(pe):
            pe.wait_ge(flags, 1)
            nc.tensor.transpose(flag_ps[:, 0, :], flag[:, 0, :], s["ident"][:])
            nc.tensor.transpose(flag_ps[:, 1, :], flag[:, 1, :], s["ident"][:]).then_inc(turned, 1)


def scan_turn(nc, dve, own, o, msgs, width, t, first):
    if not first:
        dve.wait_ge(own, t)
    cols = bass.ds(t * BODY, BODY)
    for f in range(width):
        before = 0.0 if first else msgs[:, bass.ds(t * BODY - 1, 1), f]
        last = nc.vector.tensor_tensor_scan(msgs[:, cols, f], o["same"][:, cols], msgs[:, cols, f], before,
                                            ALU.mult, ALU.add)
    last.then_inc(own, 1)


def message_phase(nc, s, name, table, fin, o, wpad, weights, fout, msgs):
    per = P // fin
    nt = GROUP // per
    terms = weights.shape[2]
    nw = terms * fout
    cpb = 512 // nw
    nb = GROUP // cpb
    with Phase(nc, name) as ph:
        idx = ph.sb("idx", [P, RING, GROUP], i32)
        rows = ph.sb("rows", [P, RING, GROUP * fin])
        rows_t = ph.sb("rows_t", [P, nt, P])
        prod = ph.sb("prod", [P, 2, 512])
        rows_ps = ph.ps("rows_ps", [P, 512])
        out_ps = ph.ps("out_ps", [P, nb, 512])
        staged, turned, copied = ph.sem("staged"), ph.sem("turned"), ph.sem("copied")
        bank_full, scaled, summed, tick = ph.sem("bank_full"), ph.sem("scaled"), ph.sem("summed"), ph.sem("tick")
        scanned, gather = ph.sem("scanned"), o["gather"]
        ring = s["ring"]
        block = ph.block()

        @block.gpsimd
        def _(pool):
            def fetch(t, first):
                for g in range(RING):
                    pool.wait_ge(staged, RING * t + g + 1)
                    pool.sem_inc(tick, 1)
                    if not first:
                        pool.wait_ge(turned, RING * (t - 1) + g + 1)
                        pool.sem_inc(tick, 1)
                    for k in range(GROUP):
                        pool.indirect_dma_start(
                            out=rows[:, g, k * fin:(k + 1) * fin], out_offset=None, in_=table,
                            in_offset=bass.IndirectOffsetOnAxis(ap=idx[:, g, k:k + 1], axis=0)).then_inc(ring.sems[g], 16)

            turns(pool, fetch)

        @block.scalar
        def _(act):
            for g in range(RING):
                nc.scalar.copy(idx[:, g, :], gather[:, g * GROUP:(g + 1) * GROUP]).then_inc(staged, 1)

            def stage(t, first):
                for g in range(RING):
                    ring.done(act, g, 16 * GROUP * (t + 1))
                    nc.scalar.copy(idx[:, g, :], gather[:, bass.ds((t + 1) * BODY + g * GROUP, GROUP)]).then_inc(staged, 1)
                    act.wait_ge(turned, RING * t + g + 1)
                    if g > 0 or not first:
                        act.wait_ge(bank_full, nb * (RING * t + g))
                    nc.scalar.copy(rows_t[:], rows_ps[:, 0:nt * P].rearrange("p (n e) -> p n e", e=P)).then_inc(copied, 1)

            turns(act, stage)

        @block.tensor
        def _(pe):
            def multiply(t, first):
                for g in range(RING):
                    ring.done(pe, g, 16 * GROUP * (t + 1))
                    if g > 0 or not first:
                        pe.wait_ge(copied, RING * t + g)
                    for n in range(nt):
                        last = nc.tensor.transpose(rows_ps[:, n * P:(n + 1) * P], rows[:, g, n * P:(n + 1) * P], s["ident"][:])
                    last.then_inc(turned, 1)
                    pe.wait_ge(copied, RING * t + g + 1)
                    for b in range(nb):
                        if g > 0 or not first:
                            pe.wait_ge(scaled, nb * (RING * t + g - 1) + b + 1)
                        for m in range(cpb):
                            k = b * cpb + m
                            last = nc.tensor.matmul(out_ps[:, b, m * nw:(m + 1) * nw], rows_t[:, k // per, :],
                                                    wpad[:, k % per, :], start=True, stop=True)
                        last.then_inc(bank_full, 1)

            turns(pe, multiply)

        @block.vector
        def _(dve):
            def combine(t, first):
                for g in range(RING):
                    for b in range(nb):
                        n = nb * (RING * t + g) + b
                        col = t * BODY + g * GROUP + b * cpb
                        dve.wait_ge(bank_full, n + 1)
                        if g * nb + b >= 2 or not first:
                            dve.wait_ge(summed, n - 1)
                        p = prod[:, (g * nb + b) % 2, :].rearrange("p (c r o) -> p c r o", r=terms, o=fout)
                        nc.vector.tensor_tensor(
                            p, out_ps[:, b, :].rearrange("p (c r o) -> p c r o", r=terms, o=fout),
                            weights[:, bass.ds(col, cpb), :].unsqueeze(3).to_broadcast([P, cpb, terms, fout]),
                            ALU.mult).then_inc(scaled, 1)
                        dve.wait_ge(scaled, n + 1)
                        nc.vector.tensor_reduce(msgs[:, bass.ds(col, cpb), 0:fout], p.rearrange("p c r o -> p c o r"),
                                                AX, ALU.add).then_inc(summed, 1)
                dve.wait_ge(summed, nb * RING * (t + 1))
                scan_turn(nc, dve, scanned, o, msgs, fout, t, first)

            turns(dve, combine)
    s["ring"].end_phase(range(RING), 16 * GROUP * TURNS)


def carry_phase(nc, s, name, o, msgs, width):
    with Phase(nc, name) as ph:
        into = ph.sb("into", [F2, P])
        mult = ph.sb("mult", [F2, P])
        carry_t = ph.sb("carry_t", [F2, P])
        carry = ph.sb("carry", [P, F2])
        last_ps, carry_ps = ph.ps("last_ps", [F2, 512]), ph.ps("carry_ps", [P, 512])
        own, scanned, turned, chained, back = (ph.sem(n) for n in ("own", "scanned", "turned", "chained", "back"))
        block = ph.block()
        w = width

        @block.vector
        def _(dve):
            c = Chain(dve, own)
            c.do(nc.vector.memset(into[:, 0:1], 0.0))
            c.do(nc.vector.memset(mult[:, 0:1], 0.0))
            c.do(nc.vector.tensor_tensor(mult[:, 1:P], o["cross"][:, 1:P], o["span"][:, 0:P - 1], ALU.mult))
            c.sync()
            dve.sem_inc(scanned, 1)
            dve.wait_ge(turned, 1)
            c.do(nc.vector.tensor_tensor(into[0:w, 1:P], o["cross"][0:w, 1:P], last_ps[0:w, 0:P - 1], ALU.mult))
            c.sync()
            c.do(nc.vector.tensor_tensor_scan(carry_t[0:w, :], mult[0:w, :], into[0:w, :], 0.0, ALU.mult, ALU.add))
            c.sync()
            dve.sem_inc(chained, 1)
            dve.wait_ge(back, 1)
            c.do(nc.vector.tensor_copy(carry[:, 0:w], carry_ps[:, 0:w]))
            c.sync()
            for f in range(w):
                c.do(nc.vector.scalar_tensor_tensor(out=msgs[:, :, f], in0=o["first"][:], scalar=carry[:, f:f + 1],
                                                    in1=msgs[:, :, f], op0=ALU.mult, op1=ALU.add))
            c.sync()

        @block.tensor
        def _(pe):
            pe.wait_ge(scanned, 1)
            nc.tensor.transpose(last_ps[0:w, 0:P], msgs[:, COLS - 1, 0:w], s["ident"][:]).then_inc(turned, 1)
            pe.wait_ge(chained, 1)
            nc.tensor.transpose(carry_ps[:, 0:w], carry_t[0:w, :], s["ident"][0:w, 0:w]).then_inc(back, 1)


def write_phase(nc, s, name, o, msgs, width, table, beside=None):
    with Phase(nc, name) as ph:
        idx = ph.sb("idx", [P, RING, GROUP], i32)
        data = ph.sb("data", [P, RING, GROUP * width])
        staged, tick = ph.sem("staged"), ph.sem("tick")
        ring = s["ring"]
        block = ph.block()
        if beside is not None:
            beside(ph, block)

        @block.scalar
        def _(act):
            def stage(t, first):
                for g in range(RING):
                    if not first:
                        ring.done(act, g, 16 * GROUP * t)
                    col = bass.ds(t * BODY + g * GROUP, GROUP)
                    nc.scalar.copy(idx[:, g, :], o["write"][:, col]).then_inc(staged, 1)
                    nc.scalar.copy(data[:, g, :].rearrange("p (k w) -> p k w", w=width), msgs[:, col, :]).then_inc(staged, 1)

            turns(act, stage)

        @block.gpsimd
        def _(pool):
            def put(t, first):
                for g in range(RING):
                    pool.wait_ge(staged, 2 * (RING * t + g + 1))
                    pool.sem_inc(tick, 1)
                    for k in range(GROUP):
                        pool.indirect_dma_start(
                            out=table, out_offset=bass.IndirectOffsetOnAxis(ap=idx[:, g, k:k + 1], axis=0),
                            in_=data[:, g, k * width:(k + 1) * width], in_offset=None,
                            bounds_check=NODES - 1, oob_is_err=False).then_inc(ring.sems[g], 16)

            turns(pool, put)
            for g in range(RING):
                ring.done(pool, g, 16 * GROUP * TURNS)
    s["ring"].end_phase(range(RING), 16 * GROUP * TURNS)


def norm_phase(nc, s, name, add_table, out_table):
    PIECE = 100
    W = PIECE * F
    NP = NODE_COLS // PIECE
    N = NODE_PARTS
    with Phase(nc, name) as ph:
        wa, wh = (F if t is None else t.shape[1] for t in (add_table, out_table))
        add = ph.sb("add", [N, 2, PIECE * wa])
        cent = ph.sb("cent", [N, 2, W])
        square = ph.sb("square", [N, 2, W])
        h = ph.sb("h", [N, 2, PIECE * wh])
        mean, var, inv, root, step = (ph.sb(n, [N, PIECE]) for n in ("mean", "var", "inv", "root", "step"))
        own, centred, squared, varied, rooted, done = (ph.sem(n) for n in ("own", "centred", "squared", "varied", "rooted", "done"))
        landed = [ph.sem(f"landed{b}") for b in range(2)]
        stored = [ph.sem(f"stored{b}") for b in range(2)]
        used = ph.sem("used")
        block = ph.block()
        src = None if add_table is None else node_rows(add_table)
        dst = node_rows(out_table)
        by_node = lambda ap: ap.rearrange("p (n f) -> p n f", f=F)
        spread = lambda ap: ap.unsqueeze(2).to_broadcast([N, PIECE, F])

        @block.sync
        def _(sp):
            for i in range(NP):
                if src is not None:
                    if i >= 2:
                        sp.wait_ge(used, i - 1)
                    node_dma(sp, add[:, i % 2, :], src[:, i * PIECE * wa:(i + 1) * PIECE * wa], landed[i % 2])

        @block.vector
        def _(dve):
            c = Chain(dve, own)

            def centre(i):
                x = s["x"][0:N, i * W:(i + 1) * W]
                if src is not None:
                    dve.wait_ge(landed[i % 2], 32 * (i // 2 + 1))
                    more = add[:, i % 2, :].rearrange("p (n f) -> p n f", f=wa)
                    if wa > F:
                        nc.vector.tensor_copy(s["place"][0:N, i * PIECE:(i + 1) * PIECE], more[:, :, F])
                    nc.vector.tensor_tensor(by_node(x), by_node(x), more[:, :, 0:F], ALU.add).then_inc(used, 1)
                    dve.wait_ge(used, i + 1)
                c.do(nc.vector.tensor_reduce(mean[:], by_node(x), AX, ALU.add))
                c.sync()
                c.do(nc.vector.tensor_scalar(mean[:], mean[:], 1.0 / F, None, ALU.mult))
                c.sync()
                nc.vector.tensor_tensor(by_node(cent[:, i % 2, :]), by_node(x), spread(mean[:]),
                                        ALU.subtract).then_inc(centred, 1)

            def scale(i):
                dve.wait_ge(squared, i + 1)
                c.do(nc.vector.tensor_reduce(var[:], by_node(square[:, i % 2, :]), AX, ALU.add))
                c.sync()
                nc.vector.tensor_scalar(var[:], var[:], 1.0 / F, EPS, ALU.mult, ALU.add).then_inc(varied, 1)
                dve.wait_ge(rooted, i + 1)
                c.do(nc.vector.reciprocal(inv[:], root[:]))
                c.sync()
                c.do(nc.vector.tensor_tensor(step[:], inv[:], inv[:], ALU.mult))
                c.sync()
                c.do(nc.vector.tensor_tensor(step[:], step[:], var[:], ALU.mult))
                c.sync()
                c.do(nc.vector.tensor_scalar(step[:], step[:], -0.5, 1.5, ALU.mult, ALU.add))
                c.sync()
                c.do(nc.vector.tensor_tensor(inv[:], inv[:], step[:], ALU.mult))
                c.sync()
                if i >= 2:
                    dve.wait_ge(stored[i % 2], 32 * (i // 2))
                res = h[:, i % 2, :].rearrange("p (n f) -> p n f", f=wh)
                if wh > F:
                    nc.vector.tensor_copy(res[:, :, F], s["place"][0:N, i * PIECE:(i + 1) * PIECE])
                nc.vector.scalar_tensor_tensor(out=res[:, :, 0:F], in0=by_node(cent[:, i % 2, :]), scalar=0.0,
                                               in1=spread(inv[:]), op0=ALU.max, op1=ALU.mult).then_inc(done, 1)
                dve.wait_ge(done, i + 1)

            centre(0)
            for i in range(NP):
                if i + 1 < NP:
                    centre(i + 1)
                scale(i)

        @block.scalar
        def _(act):
            def squares(i):
                act.wait_ge(centred, i + 1)
                nc.scalar.activation(square[:, i % 2, :], cent[:, i % 2, :], ACT.Square).then_inc(squared, 1)

            squares(0)
            for i in range(NP):
                if i + 1 < NP:
                    squares(i + 1)
                act.wait_ge(varied, i + 1)
                nc.scalar.activation(root[:], var[:], ACT.Sqrt).then_inc(rooted, 1)
                act.wait_ge(done, i + 1)
                node_dma(act, dst[:, i * PIECE * wh:(i + 1) * PIECE * wh], h[:, i % 2, :], stored[i % 2])
            for b in range(2):
                act.wait_ge(stored[b], 32 * ((NP + 1 - b) // 2))


def basis_phase(nc, s, attr, basis, place):
    B = BASIS
    with Phase(nc, "hat") as ph:
        hat = ph.sb("hat", [P, 2, COLS, B])
        away = ph.sb("away", [P, 2, COLS, B])
        shift = ph.sb("shift", [P, B])
        place_i = ph.sb("place_i", [P, COLS], i32)
        numbered = ph.sem("numbered")
        own, set_, far, near = ph.sem("own"), ph.sem("set"), ph.sem("far"), ph.sem("near")
        block = ph.block()

        @block.vector
        def _(dve):
            dve.wait_ge(numbered, 1)
            nc.vector.tensor_copy(place, place_i[:])
            for u in range(B):
                nc.vector.memset(shift[:, u:u + 1], 1.0 - u * 2.0 / (B - 1)).then_inc(set_, 1)
            dve.wait_ge(near, 1)
            nc.vector.tensor_tensor(basis[:].rearrange("p e (u v) -> p e u v", v=B),
                                    hat[:, 0, :, :].unsqueeze(3).to_broadcast([P, COLS, B, B]),
                                    hat[:, 1, :, :].unsqueeze(2).to_broadcast([P, COLS, B, B]), ALU.mult).then_inc(own, 1)
            dve.wait_ge(own, 1)

        @block.gpsimd
        def _(pool):
            nc.gpsimd.iota(place_i[:], pattern=[[1, COLS]], base=1, channel_multiplier=COLS).then_inc(numbered, 1)

        @block.scalar
        def _(act):
            act.wait_ge(set_, B)
            for a in range(2):
                for u in range(B):
                    nc.scalar.activation(away[:, a, :, u], attr[:, :, a], ACT.Abs, bias=shift[:, u:u + 1]).then_inc(far, 1)
            act.wait_ge(far, 2 * B)
            nc.scalar.activation(hat[:], away[:], ACT.Relu, bias=s["ones"][:, 0:1], scale=-(B - 1) / 2.0).then_inc(near, 1)


def pad_phase(nc, name, tiles, places):
    with Phase(nc, name) as ph:
        zeroed, loaded = ph.sem("zeroed"), ph.sem("loaded")
        block = ph.block()

        @block.vector
        def _(dve):
            for tile in tiles:
                nc.vector.memset(tile, 0.0).then_inc(zeroed, 1)

        @block.sync
        def _(sp):
            sp.wait_ge(zeroed, len(tiles))
            for place, source in places:
                sp.dma_start(place, source).then_inc(loaded, 16)
            if places:
                sp.wait_ge(loaded, 16 * len(places))


def split_steps(nc, x, stack):
    part = lambda a, n: stack[:, :, a * F:(a + n) * F].rearrange("p c (n f) -> p c n f", f=F)
    spread = lambda n: x.unsqueeze(2).to_broadcast([x.shape[0], x.shape[1], n, F])
    return [lambda: nc.vector.tensor_copy(part(0, 3), spread(3)),
            lambda: nc.vector.tensor_tensor(x, x, stack[:, :, 0:F], ALU.subtract),
            lambda: nc.vector.tensor_copy(part(3, 3), spread(3)),
            lambda: nc.vector.tensor_tensor(x, x, stack[:, :, 3 * F:4 * F], ALU.subtract),
            lambda: nc.vector.tensor_copy(part(6, 2), spread(2))]


class Split:

    def __init__(self, eng, own, done):
        self.eng, self.own, self.done = eng, own, done

    def start(self, steps, count):
        self.steps, self.count, self.n = steps, count, 0

    def step(self):
        last = len(self.steps) - 1
        wait(self.eng, self.own, last * self.count + self.n)
        ins = self.steps[self.n]()
        ins.then_inc(self.own if self.n < last else self.done, 1)
        self.n += 1

    def finish(self):
        while self.n < len(self.steps):
            self.step()


def split_phase(nc, name, rows, width, loads, out, copies, ones=None):
    with Phase(nc, name) as ph:
        full = ph.sb("full", [rows, width])
        parts = ph.sb("parts", [rows, 3, width], bf16)
        loaded, own, split, laid = (ph.sem(n) for n in ("loaded", "own", "split", "laid"))
        block = ph.block()

        @block.sync
        def _(sp):
            for columns, source in loads:
                sp.dma_start(full[:, columns], source).then_inc(loaded, 16)
            sp.wait_ge(split, 1)
            for n in range(copies):
                sp.dma_start(out[rows * n:rows * (n + 1), :], parts[:, n % 3, :]).then_inc(laid, 16)
            sp.wait_ge(laid, 16 * copies)

        @block.vector
        def _(dve):
            if ones is not None:
                nc.vector.memset(ones, 1.0)
            dve.wait_ge(loaded, 16 * len(loads))
            c = Chain(dve, own)
            for n in range(3):
                c.do(nc.vector.tensor_copy(parts[:, n, :], full[:]))
                c.sync()
                if n < 2:
                    c.do(nc.vector.tensor_tensor(full[:], full[:], parts[:, n, :], ALU.subtract))
                    c.sync()
            dve.sem_inc(split, 1)


def fold_phase(nc, s, d, w):
    H2 = HID // P
    with Phase(nc, "fold") as ph:
        pre = ph.sb("pre", [P, H2, HID])
        pre_t = ph.sb("pre_t", [P, H2, HID])
        right = {"msg": ph.sb("conv", [P, H2, HID]), "self": ph.sb("post", [P, H2, HID])}
        pre_b = ph.sb("pre_b", [P, H2])
        bias = {"msg": ph.sb("conv_b", [P, H2]), "self": ph.sb("post_b", [P, H2])}
        turn_ps = ph.ps("turn_ps", [P, H2, HID])
        prod_ps = {n: ph.ps(n + "_ps", [P, H2, HID]) for n in ("msg", "self")}
        bias_ps = ph.ps("bias_ps", [P, 8])
        loaded, turned, copied, made, own = (ph.sem(n) for n in ("loaded", "turned", "copied", "made", "own"))
        block = ph.block()
        mats = ((pre[:], d["L1_gnn_pre_w2"]), (right["msg"][:], d["L1_gnn_conv_w"]),
                (right["self"][:], d["L1_gnn_post_w1"][0:HID, :]), (w["agg"][:], d["L1_gnn_post_w1"][HID:, :]))
        vecs = ((pre_b, d["L1_gnn_pre_b2"]), (bias["msg"], d["L1_gnn_conv_b"]), (bias["self"], d["L1_gnn_post_b1"]),
                (w["pre_b1"], d["L1_gnn_pre_b1"]))

        @block.sync
        def _(sp):
            for tile, m in mats:
                sp.dma_start(tile, m.rearrange("(h p) o -> p h o", p=P)).then_inc(loaded, 16)
            for tile, v in vecs:
                for h in range(H2):
                    sp.dma_start(tile[:, h:h + 1], v[h * P:(h + 1) * P].rearrange("(p a) -> p a", a=1)).then_inc(loaded, 16)
            sp.wait_ge(loaded, 16 * (4 + 4 * H2))

        @block.tensor
        def _(pe):
            pe.wait_ge(loaded, 16 * (4 + 4 * H2))
            for k in range(H2):
                for i in range(H2):
                    last = nc.tensor.transpose(turn_ps[:, k, i * P:(i + 1) * P], pre[:, i, k * P:(k + 1) * P], s["ident"][:])
            last.then_inc(turned, 1)
            pe.wait_ge(copied, 1)
            col = 0
            for n in ("msg", "self"):
                for i in range(H2):
                    for k in range(H2):
                        nc.tensor.matmul(prod_ps[n][:, i, :], pre_t[:, k, i * P:(i + 1) * P], right[n][:, k, :],
                                         start=(k == 0), stop=(k == H2 - 1))
                for o in range(H2):
                    for k in range(H2):
                        last = nc.tensor.matmul(bias_ps[:, col:col + 1], right[n][:, k, o * P:(o + 1) * P],
                                                pre_b[:, k:k + 1], start=(k == 0), stop=(k == H2 - 1))
                    col += 1
            last.then_inc(made, 1)

        @block.vector
        def _(dve):
            dve.wait_ge(turned, 1)
            nc.vector.tensor_copy(pre_t[:], turn_ps[:]).then_inc(copied, 1)
            dve.wait_ge(made, 1)
            for m, n in enumerate(("msg", "self")):
                nc.vector.tensor_copy(w[n][:], prod_ps[n][:])
                nc.vector.tensor_tensor(w[n + "_b"][:], bias_ps[:, m * H2:(m + 1) * H2], bias[n][:], ALU.add)


def node_mlp_phase(nc, s, w, add_table, table, out, tiles, idx, edge_rows):
    N, W, R5 = NODE_PARTS, NCHUNK * F, 5
    NT = NODE_COLS // NCHUNK // R5
    M = NG * N
    UNITS = R5 * NS
    with Phase(nc, "nmlp") as ph:
        norm = NormSteps(ph, nc, s, R5 * NCHUNK, add_table, table)
        rows = norm.h[:].rearrange("p (k w) -> p k w", k=R5)
        stack = ph.sb("stack", [N, 3, NCHUNK, P], bf16)
        rows_t = ph.sb("rows_t", [P, 2, M], bf16)
        hid = ph.sb("hid", [P, 2, 2, M])
        mid = ph.sb("mid", [P, 2, 2, M])
        res = ph.sb("res", [P, M])
        res_rows = ph.sb("res_rows", [N, R5, W])
        rows_ps, hid_ps, mid_ps = ph.ps("rows_ps", [P, 2, 1024], bf16), ph.ps("hid_ps", [P, 2, 512]), ph.ps("mid_ps", [P, 2, 512])
        res_ps, back_ps = ph.ps("res_ps", [P, 512]), ph.ps("back_ps", [P, 512])
        turned, rows_ok, hid_made, hid_ok = ph.sem("turned"), ph.sem("rows_ok"), ph.sem("hid_made"), ph.sem("hid_ok")
        mid_made, mid_ok, added, res_ok = ph.sem("mid_made"), ph.sem("mid_ok"), ph.sem("added"), ph.sem("res_ok")
        back, back_ok, tick = ph.sem("back"), ph.sem("back_ok"), ph.sem("tick")
        split, own = ph.sem("split"), ph.sem("own")
        idx_staged = ph.sem("idx_staged")
        ring = s["ring"]
        block = ph.block()
        dst = node_rows(out)

        def turns_and_last(eng, body):
            body(0, True, False)
            with eng.Fori(1, NT - 1) as t:
                body(t, False, False)
            body(NT - 1, False, True)

        @block.sync
        def _(sp):
            norm.load(sp, 0)
            norm.load(sp, 1)
            norm.store(sp, 0)

            def move(t):
                norm.load(sp, t + 1)
                norm.store(sp, t)

            with sp.Fori(1, NT - 1) as t:
                move(t)
            norm.store(sp, NT - 1)
            sp.wait_ge(norm.stored, 32 * NT)

        @block.tensor
        def _(pe):
            def transpose(t, v):
                k, q = v // NS, v % NS
                c, u = R5 * t + k, UNITS * t + v
                if q == 0:
                    pe.wait_ge(split, c + 1)
                wait(pe, rows_ok, u - 1)
                for g in range(NG):
                    last = nc.tensor.transpose(rows_ps[:, v % 2, g * P:g * P + N], stack[:, k % 3, g * NS + q, :],
                                               s["ident16"][0:N, 0:N])
                last.then_inc(turned, 1)

            def hidden(t, v):
                u = UNITS * t + v
                pe.wait_ge(rows_ok, u + 1)
                wait(pe, hid_ok, u)
                for h in range(2):
                    last = nc.tensor.matmul(hid_ps[:, h, 0:M], w["stack"][:, h * P:(h + 1) * P], rows_t[:, v % 2, :],
                                            start=True, stop=True)
                last.then_inc(hid_made, 1)

            def middle(t, v):
                u = UNITS * t + v
                pe.wait_ge(hid_ok, u + 1)
                for h in range(2):
                    wait(pe, mid_ok, 2 * u - 1 + h)
                    for j in range(2):
                        last = nc.tensor.matmul(mid_ps[:, h, 0:M], w["self"][:, j, h * P:(h + 1) * P],
                                                hid[:, v % 2, j, :], start=(j == 0), stop=(j == 1))
                    last.then_inc(mid_made, 1)

            def result(t, v):
                k, q = v // NS, v % NS
                pe.wait_ge(mid_ok, 2 * (UNITS * t + v + 1))
                if q == 0:
                    wait(pe, res_ok, R5 * t + k)
                for j in range(2):
                    last = nc.tensor.matmul(res_ps[:, 0:M], w["post_w2"][:, j, q, :], mid[:, v % 2, j, :],
                                            start=(q == 0 and j == 0), stop=(q == NS - 1 and j == 1))
                last.then_inc(added, 1)

            def finish(t, k):
                c = R5 * t + k
                pe.wait_ge(res_ok, c + 1)
                wait(pe, back_ok, c)
                for g in range(NG):
                    last = nc.tensor.transpose(back_ps[0:N, g * P:(g + 1) * P], res[:, g * N:(g + 1) * N], s["ident"][:])
                last.then_inc(back, 1)

            def steps(t, first):
                transpose(t, 0)
                transpose(t, 1)
                hidden(t, 0)
                for v in range(UNITS):
                    if v + 2 < UNITS:
                        transpose(t, v + 2)
                    if v + 1 < UNITS:
                        hidden(t, v + 1)
                    middle(t, v)
                    if v >= 1:
                        result(t, v - 1)
                    if v >= 2 and (v - 1) % NS == 0:
                        finish(t, (v - 2) // NS)
                result(t, UNITS - 1)
                finish(t, R5 - 1)

            turns(pe, steps, NT)

        @block.scalar
        def _(act):
            def copy(t, v):
                u = UNITS * t + v
                act.wait_ge(turned, u + 1)
                wait(act, hid_made, u - 1)
                nc.scalar.copy(rows_t[:, v % 2, :].rearrange("p (g n) -> p g n", n=N),
                               rows_ps[:, v % 2, 0:NG * P].rearrange("p (g n) -> p g n", n=P)[:, :, 0:N]).then_inc(rows_ok, 1)

            def evacuate(t, v):
                u = UNITS * t + v
                act.wait_ge(hid_made, u + 1)
                wait(act, mid_made, 2 * (u - 1))
                for h in range(2):
                    last = nc.scalar.activation(hid[:, v % 2, h, :], hid_ps[:, h, 0:M], ACT.Relu,
                                                bias=w["pre_b1"][:, h:h + 1])
                last.then_inc(hid_ok, 1)

            def tanh(t, k):
                c = R5 * t + k
                act.wait_ge(added, NS * (c + 1))
                wait(act, back, c)
                nc.scalar.activation(res[:], res_ps[:, 0:M], ACT.Tanh, bias=w["post_b2"][:, 0:1]).then_inc(res_ok, 1)

            def steps(t, first, last):
                if first:
                    for step in norm.act(act, 0):
                        step()
                square, root = norm.act(act, t + 1)
                copy(t, 0)
                copy(t, 1)
                evacuate(t, 0)
                for v in range(UNITS):
                    if v + 2 < UNITS:
                        copy(t, v + 2)
                    if v + 1 < UNITS:
                        evacuate(t, v + 1)
                    if v >= 1 and v % NS == 0:
                        tanh(t, v // NS - 1)
                    if v == 12 and not last:
                        square()
                    if v == 20 and not last:
                        root()
                tanh(t, R5 - 1)

            turns_and_last(act, steps)

        @block.vector
        def _(dve):
            splits = Split(dve, own, split)

            def start_split(t, k):
                c = R5 * t + k
                dve.wait_ge(norm.stored, 32 * (t + 1))
                wait(dve, turned, NS * (c - 1))
                splits.start(split_steps(nc, rows[:, k, :].rearrange("p (c f) -> p c f", f=F),
                                         stack[:, k % 3, :, :]), c)

            def give_back(t, k, first):
                dve.wait_ge(back, R5 * t + k + 1)
                if not first:
                    ring.done(dve, 2 + k, 16 * t)
                nc.vector.tensor_copy(res_rows[:, k, :], back_ps[0:N, :]).then_inc(back_ok, 1)

            def steps(t, first, last):
                if first:
                    for e in range(2):
                        last_copy = nc.vector.tensor_copy(idx[:, 0, e, :], tiles[e][:, 0:CHUNK])
                    last_copy.then_inc(idx_staged, 1)
                    for step in norm.dve(dve, 0):
                        step()
                    start_split(0, 0)
                    splits.finish()
                ahead = {} if last else dict(zip((0, 2, 4, 6, 16, 17, 24, 25, 26, 27, 4 * NS), norm.dve(dve, t + 1)))
                for v in range(UNITS):
                    k, q = v // NS, v % NS
                    u = UNITS * t + v
                    for h in range(2):
                        dve.wait_ge(mid_made, 2 * u + h + 1)
                        if h == 0:
                            wait(dve, added, u - 1)
                        nc.vector.tensor_scalar(mid[:, v % 2, h, :], mid_ps[:, h, 0:M], w["self_b"][:, h:h + 1], 0.0,
                                                ALU.add, ALU.max).then_inc(mid_ok, 1)
                    if v in ahead:
                        if v == 4 * NS:
                            dve.wait_ge(split, R5 * (t + 1))
                        ahead[v]()
                    if k < R5 - 1 or not last:
                        nt, nk = (t, k + 1) if k < R5 - 1 else (t + 1, 0)
                        at = 3 if nk == 0 else 0
                        if q == at:
                            start_split(nt, nk)
                        if at <= q < at + 5:
                            splits.step()
                    if k > 0 and q == 2:
                        give_back(t, k - 1, first)
                give_back(t, R5 - 1, first)

            turns_and_last(dve, steps)

        @block.gpsimd
        def _(pool):
            def store(t, k):
                pool.wait_ge(back_ok, R5 * t + k + 1)
                pool.sem_inc(tick, 1)
                pool.dma_start(dst[:, bass.ds((t * R5 + k) * W, W)], res_rows[:, k, :]).then_inc(ring.sems[2 + k], 16)

            with pool.Fori(0, NT - 1) as t:
                for k in range(R5):
                    store(t, k)
            store(NT - 1, 0)
            pool.wait_ge(norm.stored, 32 * NT)
            pool.sem_inc(tick, 1)
            pool.wait_ge(idx_staged, 1)
            pool.sem_inc(tick, 1)
            for e in range(2):
                for k in range(CHUNK):
                    pool.indirect_dma_start(
                        out=edge_rows[:, 0, e, k * F:(k + 1) * F], out_offset=None, in_=table,
                        in_offset=bass.IndirectOffsetOnAxis(ap=idx[:, 0, e, k:k + 1], axis=0)).then_inc(ring.sems[e], 16)
            for k in range(1, R5):
                store(NT - 1, k)
            for k in range(R5):
                ring.done(pool, 2 + k, 16 * NT)
    s["ring"].end_phase(range(2, 7), 16 * (NODE_COLS // NCHUNK // 5))


def tile_order_phase(nc, s, name, o, flats, same_flat, tiles):
    Q, B = 98, COLS // 98
    with Phase(nc, name) as ph:
        clamped = ph.sb("clamped", [P, COLS])
        same16 = ph.sb("same16", [P, COLS], bf16)
        back = ph.sb("back", [Q, 3, B, P])
        turned_ps = ph.ps("turned_ps", [P, 3, 512])
        made, out, landed, turned, own = (ph.sem(n) for n in ("made", "out", "landed", "turned", "own"))
        block = ph.block()

        @block.vector
        def _(dve):
            c = Chain(dve, own)
            c.do(nc.vector.tensor_scalar(clamped[:], o["key"][:], float(NODES - 1), None, ALU.min))
            c.do(nc.vector.tensor_copy(same16[:, 1:COLS], o["same"][:, 1:COLS]))
            c.do(nc.vector.tensor_copy(same16[:, 0:1], o["goes_on"][:]))
            c.sync()
            dve.sem_inc(made, 1)
            dve.wait_ge(turned, 1)
            for a in range(3):
                nc.vector.tensor_copy(tiles[a][:, 0:COLS], turned_ps[:, a, 0:COLS])
                nc.vector.memset(tiles[a][:, COLS:], 0)

        @block.sync
        def _(sp):
            sp.wait_ge(made, 1)
            for a, src in enumerate((o["other"], clamped, o["write"])):
                sp.dma_start(flats[a].rearrange("(p j) -> p j", j=COLS), src[:]).then_inc(out, 16)
            sp.dma_start(same_flat.rearrange("(p j) -> p j", j=COLS), same16[:]).then_inc(out, 16)
            sp.wait_ge(out, 64)
            for a in range(3):
                sp.dma_start(back[:, a, :, :], flats[a].rearrange("(b q p) -> q b p", q=Q, p=P)).then_inc(landed, 16)
            sp.wait_ge(landed, 48)

        @block.tensor
        def _(pe):
            pe.wait_ge(landed, 48)
            for a in range(3):
                for b in range(B):
                    last = nc.tensor.transpose(turned_ps[:, a, b * Q:(b + 1) * Q], back[:, a, b, :], s["ident"][0:Q, 0:Q])
            last.then_inc(turned, 1)


def edge_mlp_phase(nc, s, w, table, tiles, same_flat, out, idx, rows):
    E, G, Q = CHUNK * P, CG, CS
    KF = Q * F
    PIECES = E // 512
    NC = COLS // CHUNK
    ROUND = 16 * CHUNK
    LAST = NC - 1

    def order(kind, c, q):
        if kind == "m":
            return q if isinstance(c, int) and c == 0 else 2 * Q * c - Q + q
        return 2 * Q * NC - Q + q if isinstance(c, int) and c == LAST else 2 * Q * (c + 1) + q

    def slot(kind, c, q):
        odd = (kind == "m") != (isinstance(c, int) and c == (0 if kind == "m" else LAST))
        return (q + 1) % 2 if odd else q % 2

    def units(kind, c, b):
        return [(kind, c, b, q) for q in range(Q)]

    def schedule(t):
        c = 2 * t
        first = units("m", c, 0)
        if not (isinstance(c, int) and c == 0):
            first += units("z", c - 1, 1)
        all_units = first + units("m", c + 1, 1) + units("z", c, 0)
        if isinstance(t, int) and t == TURNS - 1:
            all_units += units("z", LAST, 1)
        return all_units

    def turns_and_last(eng, body):
        body(0)
        with eng.Fori(1, TURNS - 1) as t:
            body(t)
        body(TURNS - 1)

    with Phase(nc, "emlp") as ph:
        idx_out = ph.sb("idx_out", [P, 2, CHUNK], i32)
        stack = ph.sb("stack", [P, 2, CHUNK, P], bf16)
        rows_t = ph.sb("rows_t", [P, 2, 512], bf16)
        same = ph.sb("same", [P, E], bf16)
        hid = ph.sb("hid", [P, 2, 2, 512])
        msgs = ph.sb("msgs", [P, 2, 2, E])
        mid = ph.sb("mid", [P, 2, 2, 512])
        res = ph.sb("res", [KF, 512])
        res_rows = ph.sb("res_rows", [P, 2, CHUNK * F])
        rows_ps, hid_ps, mid_ps = ph.ps("rows_ps", [P, 2, 1024], bf16), ph.ps("hid_ps", [P, 2, 512]), ph.ps("mid_ps", [P, 2, 512])
        res_ps, back_ps = ph.ps("res_ps", [P, 512]), ph.ps("back_ps", [P, 512])
        staged, tick, turned, rows_ok = ph.sem("staged"), ph.sem("tick"), ph.sem("turned"), ph.sem("rows_ok")
        hid_made, hid_ok, mid_made, mid_ok = (ph.sem(n) for n in ("hid_made", "hid_ok", "mid_made", "mid_ok"))
        scanned, added, res_ok, back, back_ok = (ph.sem(n) for n in ("scanned", "added", "res_ok", "back", "back_ok"))
        split = {n: ph.sem("split_" + n) for n in "mz"}
        own = {n: ph.sem("own_" + n) for n in "mz"}
        ring = s["ring"]
        same_in = ph.sem("same_in")
        block = ph.block()
        side = {"m": 0, "z": 1}

        @block.sync
        def _(sp):
            def load(t, first):
                for b in range(2):
                    c = 2 * t + b
                    wait(sp, scanned, PIECES * c)
                    sp.dma_start(same[:], same_flat[bass.ds(c * E, E)].partition_broadcast(P)).then_inc(same_in, 16)

            turns(sp, load)

        @block.gpsimd
        def _(pool):
            def put(c, b):
                pool.wait_ge(back_ok, c + 1)
                pool.sem_inc(tick, 1)
                for k in range(CHUNK):
                    pool.indirect_dma_start(
                        out=out, out_offset=bass.IndirectOffsetOnAxis(ap=idx_out[:, b, k:k + 1], axis=0),
                        in_=res_rows[:, b, k * F:(k + 1) * F], in_offset=None,
                        bounds_check=NODES - 1, oob_is_err=False).then_inc(ring.sems[4 + b], 16)

            def fetch(kind, c, b):
                e = side[kind]
                pool.wait_ge(staged, c + 1)
                pool.sem_inc(tick, 1)
                if not isinstance(c, int) or c >= 2:
                    pool.wait_ge(split[kind], c - 1)
                    pool.sem_inc(tick, 1)
                for k in range(CHUNK):
                    pool.indirect_dma_start(
                        out=rows[:, b, e, k * F:(k + 1) * F], out_offset=None, in_=table,
                        in_offset=bass.IndirectOffsetOnAxis(ap=idx[:, b, e, k:k + 1], axis=0)).then_inc(ring.sems[2 * b + e], 16)

            def steps(t):
                for b in range(2):
                    c = 2 * t + b
                    more = not (isinstance(c, int) and c == LAST)
                    if more:
                        fetch("m", c + 1, 1 - b)
                    if not isinstance(c, int) or c >= 2:
                        put(c - 2, b)
                    if more:
                        fetch("z", c + 1, 1 - b)

            turns_and_last(pool, steps)
            for b in range(2):
                put(NC - 2 + b, b)
            for b in range(2):
                ring.done(pool, 4 + b, ROUND * TURNS)

        @block.tensor
        def _(pe):
            def transpose(kind, c, b, q):
                u, at = order(kind, c, q), slot(kind, c, q)
                if q == 0:
                    pe.wait_ge(split[kind], c + 1)
                wait(pe, rows_ok, u - 1)
                for g in range(G):
                    last = nc.tensor.transpose(rows_ps[:, at, g * P:(g + 1) * P], stack[:, side[kind], g * Q + q, :],
                                               s["ident16"][:])
                last.then_inc(turned, 1)

            def hidden(kind, c, b, q):
                u, at = order(kind, c, q), slot(kind, c, q)
                pe.wait_ge(rows_ok, u + 1)
                wait(pe, hid_ok, u)
                for h in range(2):
                    last = nc.tensor.matmul(hid_ps[:, h, :], w["stack"][:, h * P:(h + 1) * P], rows_t[:, at, :],
                                            start=True, stop=True)
                last.then_inc(hid_made, 1)

            def middle(kind, c, b, q):
                u, at = order(kind, c, q), slot(kind, c, q)
                pe.wait_ge(hid_ok, u + 1)
                if kind == "z" and q == 0:
                    pe.wait_ge(scanned, PIECES * (c + 1))
                for h in range(2):
                    wait(pe, mid_ok, 2 * u - 1 + h)
                    for j in range(2):
                        last = nc.tensor.matmul(mid_ps[:, h, :], w["msg" if kind == "m" else "self"][:, j, h * P:(h + 1) * P],
                                                hid[:, at, j, :], start=(j == 0), stop=(kind == "m" and j == 1))
                    if kind == "z":
                        for j in range(2):
                            sums = msgs[:, b, j, :].rearrange("p (g q e) -> p g q e", q=Q, e=P)[:, :, q, :]
                            last = nc.tensor.matmul(mid_ps[:, h, :], w["agg"][:, j, h * P:(h + 1) * P], sums,
                                                    start=False, stop=(j == 1))
                    last.then_inc(mid_made, 1)

            def result(kind, c, b, q):
                pe.wait_ge(mid_ok, 2 * (order(kind, c, q) + 1))
                if q == 0:
                    wait(pe, res_ok, c)
                for j in range(2):
                    last = nc.tensor.matmul(res_ps[0:KF, :], w["post_w2"][:, j, q, 0:KF], mid[:, q % 2, j, :],
                                            start=(q == 0 and j == 0), stop=(q == Q - 1 and j == 1))
                last.then_inc(added, 1)

            def finish(c):
                pe.wait_ge(res_ok, c + 1)
                wait(pe, back_ok, c)
                for g in range(G):
                    last = nc.tensor.transpose(back_ps[:, g * KF:(g + 1) * KF], res[:, g * P:(g + 1) * P],
                                               s["ident"][0:KF, 0:KF])
                last.then_inc(back, 1)

            def steps(t):
                now = schedule(t)
                first, last = isinstance(t, int) and t == 0, isinstance(t, int) and t == TURNS - 1
                if first:
                    transpose(*now[0])
                    transpose(*now[1])
                    hidden(*now[0])
                ahead = now + ([] if last else units("m", 2 * t + 2, 0)[:2])
                behind = ([] if first else units("z", 2 * t - 2, 0)[-2:]) + now
                lag = len(behind) - len(now)
                for n, unit in enumerate(now):
                    if n + 2 < len(ahead):
                        transpose(*ahead[n + 2])
                    if n + 1 < len(ahead):
                        hidden(*ahead[n + 1])
                    middle(*unit)
                    for distance in (1, 2):
                        if n + lag - distance >= 0:
                            kind, c, b, q = behind[n + lag - distance]
                            if kind == "z" and distance == 1:
                                result(kind, c, b, q)
                            if kind == "z" and distance == 2 and q == Q - 1:
                                finish(c)
                if last:
                    result(*now[-1])
                    finish(LAST)

            turns_and_last(pe, steps)

        @block.scalar
        def _(act):
            def copy(kind, c, b, q):
                u, at = order(kind, c, q), slot(kind, c, q)
                act.wait_ge(turned, u + 1)
                wait(act, hid_made, u - 1)
                nc.scalar.copy(rows_t[:, at, :], rows_ps[:, at, 0:512]).then_inc(rows_ok, 1)

            def evacuate(kind, c, b, q):
                u, at = order(kind, c, q), slot(kind, c, q)
                act.wait_ge(hid_made, u + 1)
                wait(act, mid_made, 2 * (u - 1))
                for h in range(2):
                    last = nc.scalar.activation(hid[:, at, h, :], hid_ps[:, h, :], ACT.Relu, bias=w["pre_b1"][:, h:h + 1])
                last.then_inc(hid_ok, 1)

            def tanh(c):
                act.wait_ge(added, Q * (c + 1))
                wait(act, back, c)
                nc.scalar.activation(res[:], res_ps[0:KF, :], ACT.Tanh, bias=w["post_b2"][0:KF, 0:1]).then_inc(res_ok, 1)

            def steps(t):
                now = schedule(t)
                first, last = isinstance(t, int) and t == 0, isinstance(t, int) and t == TURNS - 1
                if first:
                    copy(*now[0])
                    copy(*now[1])
                    evacuate(*now[0])
                ahead = now + ([] if last else units("m", 2 * t + 2, 0)[:2])
                behind = ([] if first else units("z", 2 * t - 2, 0)[-1:]) + now
                lag = len(behind) - len(now)
                for n in range(len(now)):
                    if n + 2 < len(ahead):
                        copy(*ahead[n + 2])
                    if n + 1 < len(ahead):
                        evacuate(*ahead[n + 1])
                    if n + lag >= 1:
                        kind, c, b, q = behind[n + lag - 1]
                        if kind == "z" and q == Q - 1:
                            tanh(c)
                if last:
                    tanh(LAST)

            turns_and_last(act, steps)

        @block.vector
        def _(dve):
            splits = {n: Split(dve, own[n], split[n]) for n in "mz"}

            def stage(c, b, turns_before):
                for e in range(2):
                    if not isinstance(turns_before, int) or turns_before > 0:
                        ring.done(dve, 2 * b + e, ROUND * turns_before)
                for e in range(2):
                    last = nc.vector.tensor_copy(idx[:, b, e, :], tiles[e][:, bass.ds(c * CHUNK, CHUNK)])
                last.then_inc(staged, 1)

            def start_split(kind, c, b, t):
                ring.done(dve, 2 * b + side[kind], ROUND * (t + 1))
                if not isinstance(c, int) or c > 0:
                    dve.wait_ge(turned, order(kind, c - 1, Q - 1) + 1)
                splits[kind].start(split_steps(nc, rows[:, b, side[kind], :].rearrange("p (c f) -> p c f", f=F),
                                               stack[:, side[kind], :, :]), c)

            def message(c, b, q):
                u = order("m", c, q)
                if q == 0:
                    if not isinstance(c, int) or c >= 2:
                        dve.wait_ge(mid_made, 2 * (order("z", c - 2, Q - 1) + 1))
                for h in range(2):
                    dve.wait_ge(mid_made, 2 * u + h + 1)
                    place = msgs[:, b, h, :].rearrange("p (g q e) -> p g q e", q=Q, e=P)[:, :, q, :]
                    nc.vector.tensor_scalar(place, mid_ps[:, h, :].rearrange("p (g e) -> p g e", e=P),
                                            w["msg_b"][:, h:h + 1], 0.0, ALU.add, ALU.max).then_inc(mid_ok, 1)

            def scan(c, b, n):
                u = order("m", c, Q - 1)
                if n == 0:
                    dve.wait_ge(same_in, 16 * (c + 1))
                    dve.wait_ge(mid_ok, 2 * (u + 1))
                wait(dve, scanned, PIECES * c + n)
                a = 512 * n
                very_first = isinstance(c, int) and c == 0
                for h in range(2):
                    before = msgs[:, b, h, a - 1:a] if n else (0.0 if very_first else msgs[:, 1 - b, h, E - 1:E])
                    last = nc.vector.tensor_tensor_scan(msgs[:, b, h, a:a + 512], same[:, a:a + 512],
                                                        msgs[:, b, h, a:a + 512], before, ALU.mult, ALU.add)
                last.then_inc(scanned, 1)

            def middle(c, q):
                u = order("z", c, q)
                wait(dve, added, Q * c + max(q - 1, 0))
                for h in range(2):
                    dve.wait_ge(mid_made, 2 * u + h + 1)
                    nc.vector.tensor_scalar(mid[:, q % 2, h, :], mid_ps[:, h, :], w["self_b"][:, h:h + 1], 0.0,
                                            ALU.add, ALU.max).then_inc(mid_ok, 1)

            def give_back(c, b, turns_before):
                dve.wait_ge(back, c + 1)
                if not isinstance(turns_before, int) or turns_before > 0:
                    ring.done(dve, 4 + b, ROUND * turns_before)
                nc.vector.tensor_copy(idx_out[:, b, :], tiles[2][:, bass.ds(c * CHUNK, CHUNK)])
                nc.vector.tensor_copy(res_rows[:, b, :], back_ps[:, 0:CHUNK * F]).then_inc(back_ok, 1)

            def steps(t):
                for b in range(2):
                    c = 2 * t + b
                    early = isinstance(c, int)
                    next_turn = t + 1 if b == 1 else t
                    for q in range(Q):
                        message(c, b, q)
                        if not (early and c == 0):
                            if q == 0:
                                start_split("z", c - 1, 1 - b, t if b == 1 else t - 1)
                            if q < 5:
                                splits["z"].step()
                        elif q == 4:
                            start_split("m", 1, 1, 0)
                            splits["m"].finish()
                        if q == 2 and not (early and c < 2):
                            give_back(c - 2, b, t - 1)
                    stage(c + 2, b, t + 1)
                    for n in range(PIECES):
                        if not (early and c == 0):
                            middle(c - 1, n)
                            if not (early and c == LAST):
                                if n == 0:
                                    start_split("m", c + 1, 1 - b, next_turn)
                                if n < 5:
                                    splits["m"].step()
                            elif n == 4:
                                start_split("z", LAST, 1, TURNS - 1)
                                splits["z"].finish()
                        scan(c, b, n)

            dve.sem_inc(staged, 1)
            stage(1, 1, 0)
            start_split("m", 0, 0, 0)
            splits["m"].finish()
            turns_and_last(dve, steps)
            for q in range(Q):
                middle(LAST, q)
                if q == 2:
                    give_back(LAST - 1, 0, TURNS - 1)
            give_back(LAST, 1, TURNS - 1)
    s["ring"].end_phase(range(6), 16 * COLS // 2)


def count_beside(nc, s, o, kind, inverse, ph, block):
    R = RELS
    hot = ph.sb("hot", [P, COLS, R])
    seen = ph.sb("seen", [P, COLS, R])
    after = ph.sb("after", [P, COLS])
    in_last = ph.sb("in_last", [P, COLS])
    own_count = ph.sb("own_count", [P, COLS])
    into, mult, carry_t = ph.sb("into", [R, P]), ph.sb("mult", [R, P]), ph.sb("carry_t", [R, P])
    carry = ph.sb("carry", [P, R])
    edge_ps, carry_ps = ph.ps("edge_ps", [R, 512]), ph.ps("carry_ps", [P, 512])
    own, ready, turned, chained, back = (ph.sem("count_" + n) for n in ("own", "ready", "turned", "chained", "back"))

    @block.vector
    def _(dve):
        c = Chain(dve, own)
        c.do(nc.vector.tensor_tensor(hot[:], s["iota"][:, 0:R].unsqueeze(1).to_broadcast([P, COLS, R]),
                                     kind[:].unsqueeze(2).to_broadcast([P, COLS, R]), ALU.is_equal))
        c.do(nc.vector.tensor_copy(after[:, 0:COLS - 1], o["same"][:, 1:COLS]))
        c.do(nc.vector.memset(after[:, COLS - 1:COLS], 0.0))
        c.do(nc.vector.tensor_scalar(in_last[:], o["key"][:], o["key"][:, COLS - 1:COLS], None, ALU.is_equal))
        c.do(nc.vector.memset(into[:], 0.0))
        c.do(nc.vector.memset(mult[:], 0.0))
        c.sync()
        for r in range(R):
            c.do(nc.vector.tensor_tensor_scan(seen[:, :, r], o["same"][:], hot[:, :, r], 0.0, ALU.mult, ALU.add))
        c.do(nc.vector.tensor_tensor(mult[:, 1:P], o["cross"][0:R, 1:P], o["span"][0:R, 0:P - 1], ALU.mult))
        c.sync()
        dve.sem_inc(ready, 1)
        dve.wait_ge(turned, 1)
        c.do(nc.vector.tensor_tensor(into[:, 1:P], o["cross"][0:R, 1:P], edge_ps[:, 0:P - 1], ALU.mult))
        c.sync()
        c.do(nc.vector.tensor_tensor_scan(carry_t[:], mult[:], into[:], 0.0, ALU.mult, ALU.add))
        c.sync()
        dve.sem_inc(chained, 1)
        dve.wait_ge(back, 1)
        c.do(nc.vector.tensor_copy(carry[:], carry_ps[:, 0:R]))
        c.sync()
        for r in range(R):
            c.do(nc.vector.scalar_tensor_tensor(out=seen[:, :, r], in0=o["first"][:], scalar=carry[:, r:r + 1],
                                                in1=seen[:, :, r], op0=ALU.mult, op1=ALU.add))
        c.sync()
        for r in range(R):
            c.do(nc.vector.tensor_tensor_scan(seen[:, ::-1, r], after[:, ::-1], seen[:, ::-1, r], 0.0, ALU.mult, ALU.max))
        c.do(nc.vector.memset(into[:], 0.0))
        c.do(nc.vector.memset(mult[:], 0.0))
        c.sync()
        c.do(nc.vector.tensor_tensor(mult[:, 0:P - 1], o["cross"][0:R, 1:P], o["span"][0:R, 1:P], ALU.mult))
        dve.sem_inc(ready, 1)
        dve.wait_ge(turned, 2)
        c.do(nc.vector.tensor_tensor(into[:, 0:P - 1], o["cross"][0:R, 1:P], edge_ps[:, 1:P], ALU.mult))
        c.sync()
        c.do(nc.vector.tensor_tensor_scan(carry_t[:, ::-1], mult[:, ::-1], into[:, ::-1], 0.0, ALU.mult, ALU.max))
        c.sync()
        dve.sem_inc(chained, 1)
        dve.wait_ge(back, 2)
        c.do(nc.vector.tensor_copy(carry[:], carry_ps[:, 0:R]))
        c.sync()
        for r in range(R):
            c.do(nc.vector.scalar_tensor_tensor(out=seen[:, :, r], in0=in_last[:], scalar=carry[:, r:r + 1],
                                                in1=seen[:, :, r], op0=ALU.mult, op1=ALU.max))
        c.sync()
        c.do(nc.vector.tensor_tensor(seen[:], seen[:], hot[:], ALU.mult))
        c.sync()
        c.do(nc.vector.tensor_reduce(own_count[:], seen[:], AX, ALU.add))
        c.sync()
        c.do(nc.vector.reciprocal(inverse[:], own_count[:]))
        c.sync()

    @block.tensor
    def _(pe):
        for n in range(2):
            pe.wait_ge(ready, n + 1)
            col = COLS - 1 if n == 0 else 0
            nc.tensor.transpose(edge_ps[:, 0:P], seen[:, col, :], s["ident"][:]).then_inc(turned, 1)
            pe.wait_ge(chained, n + 1)
            nc.tensor.transpose(carry_ps[:, 0:R], carry_t[:], s["ident"][0:R, 0:R]).then_inc(back, 1)


def mean_weight_phase(nc, s, kind, inverse, weights):
    with Phase(nc, "mean") as ph:
        hot_built = ph.sem("hot_built")
        hot = ph.sb("hot", [P, COLS, RELS])
        block = ph.block()

        @block.vector
        def _(dve):
            nc.vector.tensor_tensor(hot[:], s["iota"][:, 0:RELS].unsqueeze(1).to_broadcast([P, COLS, RELS]),
                                    kind[:].unsqueeze(2).to_broadcast([P, COLS, RELS]), ALU.is_equal).then_inc(hot_built, 1)
            dve.wait_ge(hot_built, 1)
            nc.vector.tensor_tensor(weights[:], hot[:], inverse[:].unsqueeze(2).to_broadcast([P, COLS, RELS]), ALU.mult)


def node_relation_phase(nc, s, w, table, agg, mid_table):
    N, R5 = NODE_PARTS, 5
    W1, W2 = NCHUNK * F, NCHUNK * F2
    NT = NODE_COLS // NCHUNK // R5
    with Phase(nc, "nrel") as ph:
        rows = ph.sb("rows", [N, R5, W1])
        sums = ph.sb("sums", [N, R5, W2])
        rows_t = ph.sb("rows_t", [P, NG * N])
        mid = ph.sb("mid", [N, R5, W2])
        mid_t = ph.sb("mid_t", [P, 2 * NG * N])
        rows_ps = ph.ps("rows_ps", [P, 512])
        mid_ps = ph.ps("mid_ps", [P, 2, 512])
        mid_t_ps = ph.ps("mid_t_ps", [P, 2, 512])
        out_ps = ph.ps("out_ps", [P, 512])
        turned, rows_ok, mid_made, mid_sum, mid_ok = (ph.sem(n) for n in ("turned", "rows_ok", "mid_made", "mid_sum", "mid_ok"))
        mid_turned, mid_t_ok, out_made, out_ok, tick = (ph.sem(n) for n in ("mid_turned", "mid_t_ok", "out_made", "out_ok", "tick"))
        landed = [ph.sem(f"landed{k}") for k in range(R5)]
        ring = s["ring"]
        block = ph.block()
        src, agg_rows, dst = node_rows(table), node_rows(agg), node_rows(mid_table)

        def pipeline(eng, begin, step):
            def turn(t):
                last = isinstance(t, int) and t == NT - 1
                at = [(t, k) for k in range(R5)] + ([None, None] if last else [(t + 1, 0), (t + 1, 1)])
                for k in range(R5):
                    step(at[k], at[k + 1], at[k + 2])

            begin()
            turn(0)
            with eng.Fori(1, NT - 1) as t:
                turn(t)
            turn(NT - 1)

        @block.sync
        def _(sp):
            def load(t, first):
                for k in range(R5):
                    wait(sp, mid_sum, R5 * (t - 1) + k + 1)
                    node_dma(sp, rows[:, k, :], src[:, bass.ds((t * R5 + k) * W1, W1)], landed[k])
                    node_dma(sp, sums[:, k, :], agg_rows[:, bass.ds((t * R5 + k) * W2, W2)], landed[k])

            turns(sp, load, NT)

        @block.tensor
        def _(pe):
            def turn_rows(t, k):
                c = R5 * t + k
                pe.wait_ge(landed[k], 64 * (t + 1))
                wait(pe, rows_ok, c)
                for g in range(NG):
                    last = nc.tensor.transpose(rows_ps[:, g * N:(g + 1) * N], rows[:, k, g * P:(g + 1) * P],
                                               s["ident"][0:N, 0:N])
                last.then_inc(turned, 1)

            def make_mid(t, k):
                c = R5 * t + k
                pe.wait_ge(rows_ok, c + 1)
                wait(pe, mid_sum, c)
                for g in range(NG):
                    dst_ps = mid_ps[0:N, g // 2, (g % 2) * 256:(g % 2 + 1) * 256]
                    nc.tensor.matmul(dst_ps, rows_t[:, g * N:(g + 1) * N], w["root1"][:], start=True, stop=False)
                    last = nc.tensor.matmul(dst_ps, w["ones"][:, 0:N], w["bias"][:, 0:8 * F2], start=False, stop=True)
                last.then_inc(mid_made, 1)

            def turn_mid(t, k):
                c = R5 * t + k
                pe.wait_ge(mid_ok, c + 1)
                wait(pe, mid_t_ok, c)
                for g in range(2 * NG):
                    last = nc.tensor.transpose(mid_t_ps[:, g // 4, (g % 4) * N:(g % 4 + 1) * N], mid[:, k, g * P:(g + 1) * P],
                                               s["ident"][0:N, 0:N])
                last.then_inc(mid_turned, 1)

            def make_out(t, k):
                c = R5 * t + k
                pe.wait_ge(mid_t_ok, c + 1)
                wait(pe, out_ok, c)
                for g in range(2 * NG):
                    dst_ps = out_ps[0:N, g * 64:(g + 1) * 64]
                    nc.tensor.matmul(dst_ps, mid_t[:, g * N:(g + 1) * N], w["root2"][:], start=True, stop=False)
                    last = nc.tensor.matmul(dst_ps, w["ones"][:, 0:N], w["bias"][:, 8 * F2:], start=False, stop=True)
                last.then_inc(out_made, 1)

            def begin():
                turn_rows(0, 0)
                make_mid(0, 0)
                turn_rows(0, 1)

            def step(at, after, later):
                if after:
                    make_mid(*after)
                turn_mid(*at)
                if later:
                    turn_rows(*later)
                make_out(*at)

            pipeline(pe, begin, step)

        @block.scalar
        def _(act):
            def copy_rows(t, k):
                c = R5 * t + k
                act.wait_ge(turned, c + 1)
                wait(act, mid_made, c)
                nc.scalar.copy(rows_t[:], rows_ps[:, 0:NG * N]).then_inc(rows_ok, 1)

            def relu(t, k):
                act.wait_ge(mid_sum, R5 * t + k + 1)
                nc.scalar.activation(mid[:, k, :], mid[:, k, :], ACT.Relu).then_inc(mid_ok, 1)

            def copy_mid(t, k):
                c = R5 * t + k
                act.wait_ge(mid_turned, c + 1)
                wait(act, out_made, c)
                nc.scalar.copy(mid_t[:].rearrange("p (b m) -> p b m", b=2), mid_t_ps[:, :, 0:4 * N]).then_inc(mid_t_ok, 1)

            def begin():
                copy_rows(0, 0)
                copy_rows(0, 1)
                relu(0, 0)

            def step(at, after, later):
                copy_mid(*at)
                if later:
                    copy_rows(*later)
                if after:
                    relu(*after)

            pipeline(act, begin, step)

        @block.vector
        def _(dve):
            def add_sums(t, k):
                c = R5 * t + k
                dve.wait_ge(mid_made, c + 1)
                if not isinstance(t, int) or t > 0:
                    ring.done(dve, k, 16 * t)
                nc.vector.tensor_tensor(mid[:, k, :], mid_ps[0:N, :, :].rearrange("p b m -> p (b m)"), sums[:, k, :],
                                        ALU.add).then_inc(mid_sum, 1)

            def add_out(t, k):
                c = R5 * t + k
                dve.wait_ge(out_made, c + 1)
                x = s["x"][0:N, bass.ds(c * W1, W1)]
                nc.vector.tensor_tensor(x, x, out_ps[0:N, :], ALU.add).then_inc(out_ok, 1)

            def step(at, after, later):
                if after:
                    add_sums(*after)
                add_out(*at)

            pipeline(dve, lambda: add_sums(0, 0), step)

        @block.gpsimd
        def _(pool):
            def store(t, first):
                for k in range(R5):
                    pool.wait_ge(mid_ok, R5 * t + k + 1)
                    pool.sem_inc(tick, 1)
                    pool.dma_start(dst[:, bass.ds((t * R5 + k) * W2, W2)], mid[:, k, :]).then_inc(ring.sems[k], 16)

            turns(pool, store, NT)
            for k in range(R5):
                ring.done(pool, k, 16 * NT)
    s["ring"].end_phase(range(5), 16 * (NODE_COLS // NCHUNK // 5))


def propagate_phase(nc, s, name, table, gather, weight, o, msgs, next_gather=None):
    width = F if next_gather is None else F + 1
    with Phase(nc, name) as ph:
        idx = ph.sb("idx", [P, RING, GROUP], i32)
        rows = ph.sb("rows", [P, RING, GROUP * width])
        staged, used, tick, scaled, scanned = (ph.sem(n) for n in ("staged", "used", "tick", "scaled", "scanned"))
        ring = s["ring"]
        block = ph.block()

        @block.gpsimd
        def _(pool):
            def fetch(t, first):
                for g in range(RING):
                    pool.wait_ge(staged, RING * t + g + 1)
                    pool.sem_inc(tick, 1)
                    if not first:
                        pool.wait_ge(used, RING * (t - 1) + g + 1)
                        pool.sem_inc(tick, 1)
                    for k in range(GROUP):
                        pool.indirect_dma_start(
                            out=rows[:, g, k * width:(k + 1) * width], out_offset=None, in_=table,
                            in_offset=bass.IndirectOffsetOnAxis(ap=idx[:, g, k:k + 1], axis=0)).then_inc(ring.sems[g], 16)

            turns(pool, fetch)

        @block.scalar
        def _(act):
            for g in range(RING):
                nc.scalar.copy(idx[:, g, :], gather[:, g * GROUP:(g + 1) * GROUP]).then_inc(staged, 1)

            def stage(t, first):
                for g in range(RING):
                    ring.done(act, g, 16 * GROUP * (t + 1))
                    nc.scalar.copy(idx[:, g, :], gather[:, bass.ds((t + 1) * BODY + g * GROUP, GROUP)]).then_inc(staged, 1)

            turns(act, stage)

        @block.vector
        def _(dve):
            def scale(t, first):
                for g in range(RING):
                    ring.done(dve, g, 16 * GROUP * (t + 1))
                    col = bass.ds(t * BODY + g * GROUP, GROUP)
                    row = rows[:, g, :].rearrange("p (k f) -> p k f", f=width)
                    if next_gather is not None:
                        nc.vector.tensor_copy(next_gather[:, col], row[:, :, F])
                    nc.vector.tensor_tensor(msgs[:, col, 0:F], row[:, :, 0:F],
                                            weight[:, col].unsqueeze(2).to_broadcast([P, GROUP, F]), ALU.mult).then_inc(used, 1)
                dve.wait_ge(used, RING * (t + 1))
                scan_turn(nc, dve, scanned, o, msgs, F, t, first)

            turns(dve, scale)

    s["ring"].end_phase(range(RING), 16 * GROUP * TURNS)


def keep_phase(nc, name, msgs, table):
    with Phase(nc, name) as ph:
        stored = ph.sem("stored")
        block = ph.block()

        @block.sync
        def _(sp):
            sp.dma_start(table[1:1 + SLOTS, :].rearrange("(p j) f -> p j f", j=COLS), msgs[:, :, 0:F]).then_inc(stored, 16)
            sp.wait_ge(stored, 16)


def finish_phase(nc, s, table, out):
    PARTS, N = 5, NODE_PARTS
    W = NODE_COLS * F // PARTS
    with Phase(nc, "fin") as ph:
        add = ph.sb("add", [N, PARTS, W])
        summed, stored = ph.sem("summed"), ph.sem("stored")
        landed = [ph.sem(f"landed{i}") for i in range(PARTS)]
        block = ph.block()
        src, dst = node_rows(table), node_rows(out)

        @block.sync
        def _(sp):
            for i in range(PARTS):
                node_dma(sp, add[:, i, :], src[:, i * W:(i + 1) * W], landed[i])
            for i in range(PARTS):
                sp.wait_ge(summed, i + 1)
                node_dma(sp, dst[:, i * W:(i + 1) * W], add[:, i, :], stored)
            sp.wait_ge(stored, 32 * PARTS)

        @block.vector
        def _(dve):
            for i in range(PARTS):
                dve.wait_ge(landed[i], 32)
                nc.vector.tensor_tensor(add[:, i, :], s["x"][0:N, i * W:(i + 1) * W], add[:, i, :], ALU.add).then_inc(summed, 1)


def graph_kernel(nc, d, out):
    ctx = ExitStack()
    internal = lambda name, shape, dt=fp32: nc.dram_tensor(name, shape, dt, kind="Internal").ap()
    tables = {n: internal("t_" + n, (NODES, w)) for n, w in
              (("h0", F), ("agg0", F + 1), ("h1", F), ("mlp", F), ("h2", F), ("agg2", F2), ("mid", F2), ("agg3", F),
               ("y0", F + 1), ("y4", F))}
    steps = [internal(f"step{n}", (SLOTS + 1, F)) for n in range(STEPS - 1)]
    scratch = {"lo": internal("count_lo", (LO,)), "hi": internal("count_hi", (HI,))}
    sorted_once, sorted_src, sorted_dst = (internal(n, (SLOTS, REC)) for n in ("sorted_once", "sorted_src", "sorted_dst"))
    flats = [internal(f"flat{a}", (SLOTS,)) for a in range(3)]
    same_flat = internal("same_flat", (SLOTS,), bf16)

    with ctx:
        def sb(name, shape, dt=fp32, to=ctx):
            return to.enter_context(nc.sbuf_tensor(name, shape, dt))

        Phase.spent.clear()
        s = dict(ring=PoolRing(ctx, nc), ident=sb("ident", [P, P]), ident16=sb("ident16", [P, P], bf16), ones=sb("ones", [P, LO]), iota=sb("iota", [P, 32]), x=sb("x_nodes", [P, NODE_COLS * F]),
                 zero_tables=[tables[n] for n in ("agg0", "agg2", "agg3", "y4")], zero_rows=[t[0:1, :] for t in steps])
        s["place"] = sb("place", [P, NODE_COLS])
        orders = []
        for n in "ba":
            orders.append(dict(
                same=sb(n + "_same", [P, COLS]),
                first=sb(n + "_first", [P, COLS]), write=sb(n + "_write", [P, COLS]),
                gather=sb(n + "_gather", [P, COLS + BODY], i32), goes_on=sb(n + "_goes_on", [P, 1]),
                cross=sb(n + "_cross", [F2, P]), span=sb(n + "_span", [F2, P])))
        by_dst, by_src = orders
        weight = sb("weight", [P, COLS])
        kind, inverse = sb("kind", [P, COLS]), sb("inverse", [P, COLS])
        by_dst.update(key=sb("b_key", [P, COLS]), other=sb("b_other", [P, COLS]))
        early = ctx.enter_context(ExitStack())
        by_src.update(key=sb("a_key", [P, COLS], fp32, early), other=sb("a_other", [P, COLS], fp32, early))
        attr = sb("attr", [P, COLS, 2], fp32, early)

        with ExitStack() as part:
            t = lambda name, shape, dt=fp32: sb(name, shape, dt, part)
            s.update(zero=t("zero", [P, 3400]), iota16=t("iota16", [P, LO], fp16), earlier16=t("earlier16", [P, P], fp16), ones16=t("ones16", [P, P], fp16),
                     rec_a=t("rec_a", [P, COLS, REC]), rec_b=t("rec_b", [P, COLS, REC]), minus_lo=t("minus_lo", [P, COLS]),
                     minus_hi=t("minus_hi", [P, COLS]), row=t("row", [P, 1]),
                     base_lo=t("base_lo", [P, LO], fp16), base_hi=t("base_hi", [P, HI], fp16))
            setup_phase(nc, d, s)
            flag = t("flag", [1, 1], i32)
            descent_phase(nc, s, flag, sorted_dst)
            zeroed = part.enter_context(nc.semaphore("zeroed"))
            sort_records(nc, s, "a", s["rec_a"], scratch, sorted_once, sorted_src, lambda sp: zero_tables(sp, s, zeroed), tables["h0"])
            Phase.spent.append(zeroed.num)
            recycle(nc)
            unsorted = nc.values_load(flag[0:1, 0:1])
            with nc.If(unsorted != 0):
                enter_phase(nc)
                sort_records(nc, dict(s, ring=PoolRing(ctx, nc, "general")), "b", s["rec_b"], scratch, sorted_once, sorted_dst)
        order_phase(nc, s, "order_a", sorted_src, by_src, [(weight[:], 2), (attr[:], (3, 5))])
        order_phase(nc, s, "order_b", sorted_dst, by_dst, [(kind[:], 2)])

        with ExitStack() as part:
            t = lambda name, shape, dt=fp32: sb(name, shape, dt, part)
            msgs = t("msgs0", [P, COLS, F + 1])
            half = part.enter_context(ExitStack())
            basis, wpad = sb("basis", [P, COLS, BASIS * BASIS], fp32, half), sb("wpad0", [P, 8, 256], fp32, half)
            basis_phase(nc, s, attr, basis, msgs[:, :, F])
            flat_w = d["L0_gnn_weight"].rearrange("u v i o -> i (u v) o")
            pad_phase(nc, "pad0", [wpad[:]],
                      [(wpad[F * q:F * (q + 1), q, :].rearrange("p (k o) -> p k o", o=F), flat_w) for q in range(8)])
            message_phase(nc, s, "msg0", tables["h0"], F, by_src, wpad, basis, F, msgs)
            half.close()
            carry_phase(nc, s, "scan0", by_src, msgs, F)
            write_phase(nc, s, "write0", by_src, msgs, F + 1, tables["agg0"],
                        lambda ph, block: count_beside(nc, s, by_dst, kind, inverse, ph, block))
        early.close()

        with ExitStack() as part:
            t = lambda name, shape, dt=fp32: sb(name, shape, dt, part)
            w = dict(msg=t("w_msg", [P, 2, HID]), self=t("w_self", [P, 2, HID]), agg=t("w_agg", [P, 2, HID]),
                     msg_b=t("w_msg_b", [P, 2]), self_b=t("w_self_b", [P, 2]), pre_b1=t("w_pre_b1", [P, 2]),
                     stack=t("w_stack", [P, HID], bf16), post_w2=t("w_post_w2", [P, 2, 8, P]), post_b2=t("w_post_b2", [P, 1]))
            fold_phase(nc, s, d, w)
            places = []
            for q in range(8):
                rows = slice(F * q, F * (q + 1))
                for h in range(2):
                    places.append((w["post_w2"][:, h, q, rows], d["L1_gnn_post_w2"][h * P:(h + 1) * P, :]))
                places.append((w["post_b2"][rows, :], d["L1_gnn_post_b2"].rearrange("(p a) -> p a", a=1)))
            pad_phase(nc, "pad1", [w["post_w2"][:]], places)
            split_phase(nc, "wsplit", F, HID, [(slice(0, HID), d["L1_gnn_pre_w1"])], w["stack"], 8)
            tiles = [t(f"tile_{a}", [P, COLS + BODY], i32) for a in ("src", "dst", "write")]
            tile_order_phase(nc, s, "tiles", by_dst, flats, same_flat, tiles)
            idx, edge_rows = t("edge_idx", [P, 2, 2, CHUNK], i32), t("edge_rows", [P, 2, 2, CHUNK * F])
            node_mlp_phase(nc, s, w, tables["agg0"], tables["h1"], tables["mlp"], tiles, idx, edge_rows)
            edge_mlp_phase(nc, s, w, tables["h1"], tiles, same_flat, tables["mlp"], idx, edge_rows)
        norm_phase(nc, s, "norm2", tables["mlp"], tables["h2"])

        with ExitStack() as part:
            t = lambda name, shape, dt=fp32: sb(name, shape, dt, part)
            mean = t("mean_weight", [P, COLS, RELS])
            mean_weight_phase(nc, s, kind, inverse, mean)
            with ExitStack() as half:
                msgs, wpad = sb("msgs2", [P, COLS, F2], fp32, half), sb("wpad2", [P, 8, 256], fp32, half)
                pad_phase(nc, "pad2", [wpad[:]],
                          [(wpad[F * q:F * (q + 1), q, :].rearrange("p (r o) -> p r o", o=F2),
                            d["L2_gnn_W1"].rearrange("r i o -> i r o")) for q in range(8)])
                message_phase(nc, s, "msg2", tables["h2"], F, by_dst, wpad, mean, F2, msgs)
                carry_phase(nc, s, "scan2", by_dst, msgs, F2)
                write_phase(nc, s, "write2", by_dst, msgs, F2, tables["agg2"])
            with ExitStack() as half:
                h = lambda name, shape: sb(name, shape, fp32, half)
                w = dict(root1=h("w_root1", [P, 8 * F2]), root2=h("w_root2", [P, 4 * F]),
                         bias=sb("w_bias", [3, 8 * F2 + 4 * F], bf16, half), ones=sb("w_ones", [3, P], bf16, half))
                row = lambda v: v.rearrange("(a f) -> a f", a=1)
                pad_phase(nc, "pad3", [w["root1"][:], w["root2"][:]],
                          [(w["root1"][F * q:F * (q + 1), F2 * q:F2 * (q + 1)], d["L2_gnn_root1"]) for q in range(8)] +
                          [(w["root2"][F2 * q:F2 * (q + 1), F * q:F * (q + 1)], d["L2_gnn_root2"]) for q in range(4)])
                split_phase(nc, "bsplit", 1, 8 * F2 + 4 * F,
                            [(slice(F2 * q, F2 * (q + 1)), row(d["L2_gnn_b1"])) for q in range(8)] +
                            [(slice(8 * F2 + F * q, 8 * F2 + F * (q + 1)), row(d["L2_gnn_b2"])) for q in range(4)],
                            w["bias"], 3, w["ones"][:])
                node_relation_phase(nc, s, w, tables["h2"], tables["agg2"], tables["mid"])
            with ExitStack() as half:
                msgs, wpad = sb("msgs3", [P, COLS, F], fp32, half), sb("wpad3", [P, 4, 128], fp32, half)
                pad_phase(nc, "pad4", [wpad[:]],
                          [(wpad[F2 * q:F2 * (q + 1), q, :].rearrange("p (r o) -> p r o", o=F),
                            d["L2_gnn_W2"].rearrange("r i o -> i r o")) for q in range(4)])
                message_phase(nc, s, "msg3", tables["mid"], F2, by_dst, wpad, mean, F, msgs)
                carry_phase(nc, s, "scan3", by_dst, msgs, F)
                write_phase(nc, s, "write3", by_dst, msgs, F, tables["agg3"])
        norm_phase(nc, s, "norm3", tables["agg3"], tables["y0"])

        with ExitStack() as part:
            msgs = sb("msgs4", [P, COLS, F], fp32, part)
            places = sb("places", [P, COLS + BODY], i32, part)
            pad_phase(nc, "pad5", [places[:]], [])
            propagate_phase(nc, s, "prop0", tables["y0"], by_src["gather"], weight, by_src, msgs, places)
            carry_phase(nc, s, "carry40", by_src, msgs, F)
            for n in range(1, STEPS):
                keep_phase(nc, f"keep{n}", msgs, steps[n - 1])
                propagate_phase(nc, s, f"prop{n}", steps[n - 1], places, weight, by_src, msgs)
                carry_phase(nc, s, f"carry4{n}", by_src, msgs, F)
            write_phase(nc, s, "write4", by_src, msgs, F, tables["y4"])
        finish_phase(nc, s, tables["y4"], out)


_INS = ["x", "src", "dst", "edge_attr_2", "edge_type_8", "edge_weight", "L0_gnn_weight",
        "L1_gnn_pre_w1", "L1_gnn_pre_b1", "L1_gnn_pre_w2", "L1_gnn_pre_b2", "L1_gnn_conv_w", "L1_gnn_conv_b",
        "L1_gnn_post_w1", "L1_gnn_post_b1", "L1_gnn_post_w2", "L1_gnn_post_b2",
        "L2_gnn_W1", "L2_gnn_root1", "L2_gnn_b1", "L2_gnn_W2", "L2_gnn_root2", "L2_gnn_b2"]


def kernel(**inputs):
    import numpy as _np
    import concourse.bacc as _bacc
    from concourse.bass_utils import run_bass_kernel_spmd as _run

    nc = _bacc.Bacc("TRN2", target_bir_lowering=False, num_devices=1)
    arrays, d = {}, {}
    for name in _INS:
        a = _np.ascontiguousarray(inputs[name])
        arrays[f"in_{name}"] = a
        d[name] = nc.dram_tensor(f"in_{name}", a.shape, mybir.dt.from_np(a.dtype), kind="ExternalInput").ap()
    out = nc.dram_tensor("out_x", (NODES, F), fp32, kind="ExternalOutput").ap()
    graph_kernel(nc, d, out)
    r = _run(nc, [arrays], core_ids=[0])
    return r.results[0]["out_x"]
```
